# Optimizing a Trainium2 kernel written in Bass

```python
import numpy as np
import jax
import jax.numpy as jnp

def _softmax(x, axis=-1):
    return jax.nn.softmax(x, axis=axis)

def _gelu(x):
    return jax.nn.gelu(x, approximate=True)

def _silu(x):
    return jax.nn.silu(x)

def _sigmoid(x):
    return jax.nn.sigmoid(x)

def _layernorm(x, axis=-1, eps=1e-05):
    m = jnp.mean(x, axis=axis, keepdims=True)
    v = jnp.var(x, axis=axis, keepdims=True)
    return (x - m) / jnp.sqrt(v + eps)

def _scatter_add(tgt, idx, src, axis=0):
    return tgt.at[idx].add(src)

def _segment_sum(src, seg, n):
    return jax.ops.segment_sum(src, seg, n)
kernel_name = 'mk_early_fusion_d2_tok_img768_r4_22d014'

def setup_inputs(seed: int=0):
    np.random.seed(seed)
    _w = jnp.asarray

    def _rec_inputs():
        import jax
        import jax.numpy as jnp
        _rk = jax.random.key(seed)
        x = -0.00040386 + 0.999972 * jax.random.normal(jax.random.fold_in(_rk, 1), (16, 3, 128, 128), jnp.float32)
        txt = 0.198809 + 1.28268 * jax.random.normal(jax.random.fold_in(_rk, 2), (16, 77, 192), jnp.float32)
        return (x, txt)
    x, txt = _rec_inputs()

    def _L0_tok_setup():
        import jax, jax.numpy as jnp
        import numpy as np
        P = 16
        WIN = 64
        NH = 12

        def _layernorm(x, g, b, eps=1e-05):
            m = x.mean(-1, keepdims=True)
            v = ((x - m) ** 2).mean(-1, keepdims=True)
            return (x - m) * jax.lax.rsqrt(v + eps) * g + b

        def _sinusoidal_pe(n, d):
            pos = jnp.arange(n, dtype=jnp.float32)[:, None]
            i = jnp.arange(d // 2, dtype=jnp.float32)[None, :]
            ang = pos / jnp.power(10000.0, 2.0 * i / d)
            pe = jnp.zeros((n, d), jnp.float32)
            pe = pe.at[:, 0::2].set(jnp.sin(ang)).at[:, 1::2].set(jnp.cos(ang))
            return pe
        key = jax.random.key(seed)
        ks = jax.random.split(key, 8)
        B, C, H, W, D, F = (16, 3, 128, 128, 192, 768)
        s = lambda k, shape: jax.random.normal(k, shape, jnp.float32) * 0.02
        return {'input': jax.random.normal(ks[0], (B, C, H, W), jnp.float32), 'patch_w': s(ks[1], (D, C, P, P)), 'patch_b': jnp.zeros((D,), jnp.float32), 'ln_g': jnp.ones((D,), jnp.float32), 'ln_b': jnp.zeros((D,), jnp.float32), 'qkv_w': s(ks[2], (D, 3 * D)), 'qkv_b': jnp.zeros((3 * D,), jnp.float32), 'proj_w': s(ks[3], (D, D)), 'proj_b': jnp.zeros((D,), jnp.float32), 'ff1_w': s(ks[4], (D, F)), 'ff1_b': jnp.zeros((F,), jnp.float32), 'ff2_w': s(ks[5], (F, D)), 'ff2_b': jnp.zeros((D,), jnp.float32)}
    _L0_tok_all = _L0_tok_setup()
    _L0_tok_in = {k: v for k, v in _L0_tok_all.items() if k in ('patch_w', 'patch_b', 'ln_g', 'ln_b', 'qkv_w', 'qkv_b', 'proj_w', 'proj_b', 'ff1_w', 'ff1_b', 'ff2_w', 'ff2_b')}
    del _L0_tok_all

    def _L0_attn_setup():
        import jax, jax.numpy as jnp
        import numpy as np
        D_MODEL = 192
        N_LAYER = 4
        D_INNER = 2 * D_MODEL
        D_STATE = 16
        D_CONV = 4
        DT_RANK = (D_MODEL + 15) // 16
        EPS = 1e-05

        def _ln(x, w, b):
            mu = jnp.mean(x, axis=-1, keepdims=True)
            var = jnp.mean(jnp.square(x - mu), axis=-1, keepdims=True)
            return (x - mu) * jax.lax.rsqrt(var + EPS) * w + b

        def _mixer(u, p):
            B, L, _ = u.shape
            xz = jnp.einsum('bld,ed->ble', u, p['in_proj_w'])
            x, z = jnp.split(xz, 2, axis=-1)
            xp = jnp.pad(x, ((0, 0), (D_CONV - 1, 0), (0, 0)))
            x = sum((p['conv_w'][:, k] * xp[:, k:k + L, :] for k in range(D_CONV))) + p['conv_b']
            x = jax.nn.silu(x)
            x_dbl = jnp.einsum('bld,ed->ble', x, p['x_proj_w'])
            dt, Bm, Cm = jnp.split(x_dbl, [DT_RANK, DT_RANK + D_STATE], axis=-1)
            dt = jax.nn.softplus(jnp.einsum('blr,dr->bld', dt, p['dt_proj_w']) + p['dt_proj_b'])
            A = -jnp.exp(p['A_log'])

            def step(h, xs):
                dt_t, B_t, C_t, x_t = xs
                dA = jnp.exp(dt_t[:, :, None] * A)
                h = dA * h + (dt_t * x_t)[:, :, None] * B_t[:, None, :]
                y = jnp.einsum('bds,bs->bd', h, C_t)
                return (h, y)
            h0 = jnp.zeros((B, D_INNER, D_STATE), x.dtype)
            xs = (dt.transpose(1, 0, 2), Bm.transpose(1, 0, 2), Cm.transpose(1, 0, 2), x.transpose(1, 0, 2))
            _, ys = jax.lax.scan(step, h0, xs)
            y = ys.transpose(1, 0, 2) + x * p['D_skip']
            y = y * jax.nn.silu(z)
            return jnp.einsum('bld,ed->ble', y, p['out_proj_w'])
        key = jax.random.key(seed)
        ks = jax.random.split(key, 8)
        s = 0.02
        n, dm, di = (N_LAYER, D_MODEL, D_INNER)
        return {'embeddings': jax.random.normal(ks[0], (2, 256, dm), jnp.float32), 'norm_w': jnp.ones((n, dm), jnp.float32), 'norm_b': jnp.zeros((n, dm), jnp.float32), 'in_proj_w': jax.random.normal(ks[1], (n, 2 * di, dm), jnp.float32) * s, 'conv_w': jax.random.normal(ks[2], (n, di, D_CONV), jnp.float32) * s, 'conv_b': jnp.zeros((n, di), jnp.float32), 'x_proj_w': jax.random.normal(ks[3], (n, DT_RANK + 2 * D_STATE, di), jnp.float32) * s, 'dt_proj_w': jax.random.normal(ks[4], (n, di, DT_RANK), jnp.float32) * s, 'dt_proj_b': jnp.full((n, di), float(np.log(np.expm1(0.01))), jnp.float32), 'A_log': jnp.broadcast_to(jnp.log(jnp.arange(1, D_STATE + 1, dtype=jnp.float32)), (n, di, D_STATE)) + jnp.zeros((n, di, D_STATE), jnp.float32), 'D_skip': jnp.ones((n, di), jnp.float32), 'out_proj_w': jax.random.normal(ks[5], (n, dm, di), jnp.float32) * s, 'norm_f_w': jnp.ones((dm,), jnp.float32), 'norm_f_b': jnp.zeros((dm,), jnp.float32)}
    _L0_attn_all = _L0_attn_setup()
    _L0_attn_in = {k: v for k, v in _L0_attn_all.items() if k in ('norm_w', 'norm_b', 'in_proj_w', 'conv_w', 'conv_b', 'x_proj_w', 'dt_proj_w', 'dt_proj_b', 'A_log', 'D_skip', 'out_proj_w', 'norm_f_w', 'norm_f_b')}
    del _L0_attn_all

    def _L0_ffn_setup():
        import jax, jax.numpy as jnp
        import numpy as np
        B, S, D = (4, 256, 192)
        E = 8
        H = 192
        HS = 768
        TOPK_ROUTED = 2
        key = jax.random.key(seed)
        ks = jax.random.split(key, 10)
        w = lambda k, shape: jax.random.normal(k, shape, dtype=jnp.float32) * 0.02
        return {'x': jax.random.normal(ks[0], (B, S, D), dtype=jnp.float32), 'router_w': w(ks[1], (D, E)), 'w_gate': w(ks[2], (E, D, H)), 'w_up': w(ks[3], (E, D, H)), 'w_down': w(ks[4], (E, H, D)), 'ws_gate': w(ks[5], (D, HS)), 'ws_up': w(ks[6], (D, HS)), 'ws_down': w(ks[7], (HS, D)), 'sg_w': w(ks[8], (D, 1)), 'sg_b': jnp.zeros((1,), jnp.float32)}
    _L0_ffn_all = _L0_ffn_setup()
    _L0_ffn_in = {k: v for k, v in _L0_ffn_all.items() if k in ('router_w', 'w_gate', 'w_up', 'w_down', 'ws_gate', 'ws_up', 'ws_down', 'sg_w', 'sg_b')}
    del _L0_ffn_all

    def _L1_attn_setup():
        import jax, jax.numpy as jnp
        import numpy as np
        NUM_HEADS = 12

        def _attn(q, k, v, scale):
            s = jnp.einsum('bhqd,bhkd->bhqk', q, k) * scale
            p = jax.nn.softmax(s, axis=-1)
            return jnp.einsum('bhqk,bhkd->bhqd', p, v)
        key = jax.random.key(seed)
        k1, k2, k3 = jax.random.split(key, 3)
        B, N, C = (4, 128, 192)
        x = jax.random.normal(k1, (B, N, C), jnp.float32)
        qkv_w = jax.random.normal(k2, (3 * C, C), jnp.float32) * C ** (-0.5)
        proj_w = jax.random.normal(k3, (C, C), jnp.float32) * C ** (-0.5)
        proj_b = jnp.zeros((C,), jnp.float32)
        return {'x': x, 'qkv_w': qkv_w, 'proj_w': proj_w, 'proj_b': proj_b}
    _L1_attn_all = _L1_attn_setup()
    _L1_attn_in = {k: v for k, v in _L1_attn_all.items() if k in ('qkv_w', 'proj_w', 'proj_b')}
    del _L1_attn_all

    def _L1_ffn_setup():
        import jax, jax.numpy as jnp
        import numpy as np
        B, S, D, F, E = (8, 512, 192, 768, 16)
        CAP = 64
        EPS = 1e-06

        def _switch_moe_block(x, ln_w, w_router, wi, wo):
            var = jnp.mean(jnp.square(x.astype(jnp.float32)), axis=-1, keepdims=True)
            normed = (x * jax.lax.rsqrt(var + EPS)).astype(x.dtype) * ln_w
            logits = jnp.einsum('bsd,de->bse', normed.astype(jnp.float32), w_router.astype(jnp.float32))
            probs = jax.nn.softmax(logits, axis=-1)
            expert_idx = jnp.argmax(probs, axis=-1)
            onehot = jax.nn.one_hot(expert_idx, E, dtype=jnp.float32)
            priority = jnp.cumsum(onehot, axis=1)
            keep = onehot * (priority <= CAP)
            pos = (priority - 1.0).astype(jnp.int32)
            dispatch = keep[..., None] * jax.nn.one_hot(pos, CAP, dtype=jnp.float32)
            expert_in = jnp.einsum('bsec,bsd->becd', dispatch, normed)
            h = jax.nn.relu(jnp.einsum('becd,edf->becf', expert_in, wi))
            expert_out = jnp.einsum('becf,efd->becd', h, wo)
            combined = jnp.einsum('bsec,becd->bsd', dispatch, expert_out)
            routed = jnp.sum(dispatch, axis=(2, 3)) > 0
            next_states = jnp.where(routed[..., None], combined.astype(x.dtype), normed)
            router_prob = jnp.max(probs, axis=-1, keepdims=True).astype(x.dtype)
            return x + router_prob * next_states
        key = jax.random.key(seed)
        k_x, k_r, k_wi, k_wo = jax.random.split(key, 4)
        x = jax.random.normal(k_x, (B, S, D), dtype=jnp.float32)
        ln_w = jnp.ones((D,), dtype=jnp.float32)
        w_router = jax.random.normal(k_r, (D, E), dtype=jnp.float32) * 0.02
        wi = jax.random.normal(k_wi, (E, D, F), dtype=jnp.float32) * D ** (-0.5)
        wo = jax.random.normal(k_wo, (E, F, D), dtype=jnp.float32) * F ** (-0.5)
        return {'x': x, 'ln_w': ln_w, 'w_router': w_router, 'wi': wi, 'wo': wo}
    _L1_ffn_all = _L1_ffn_setup()
    _L1_ffn_in = {k: v for k, v in _L1_ffn_all.items() if k in ('ln_w', 'w_router', 'wi', 'wo')}
    del _L1_ffn_all
    return {'x': x, 'txt': txt, 'L0_tok_patch_w': _L0_tok_in['patch_w'], 'L0_tok_patch_b': _L0_tok_in['patch_b'], 'L0_tok_ln_g': _L0_tok_in['ln_g'], 'L0_tok_ln_b': _L0_tok_in['ln_b'], 'L0_tok_qkv_w': _L0_tok_in['qkv_w'], 'L0_tok_qkv_b': _L0_tok_in['qkv_b'], 'L0_tok_proj_w': _L0_tok_in['proj_w'], 'L0_tok_proj_b': _L0_tok_in['proj_b'], 'L0_tok_ff1_w': _L0_tok_in['ff1_w'], 'L0_tok_ff1_b': _L0_tok_in['ff1_b'], 'L0_tok_ff2_w': _L0_tok_in['ff2_w'], 'L0_tok_ff2_b': _L0_tok_in['ff2_b'], 'L0_attn_norm_w': _L0_attn_in['norm_w'], 'L0_attn_norm_b': _L0_attn_in['norm_b'], 'L0_attn_in_proj_w': _L0_attn_in['in_proj_w'], 'L0_attn_conv_w': _L0_attn_in['conv_w'], 'L0_attn_conv_b': _L0_attn_in['conv_b'], 'L0_attn_x_proj_w': _L0_attn_in['x_proj_w'], 'L0_attn_dt_proj_w': _L0_attn_in['dt_proj_w'], 'L0_attn_dt_proj_b': _L0_attn_in['dt_proj_b'], 'L0_attn_A_log': _L0_attn_in['A_log'], 'L0_attn_D_skip': _L0_attn_in['D_skip'], 'L0_attn_out_proj_w': _L0_attn_in['out_proj_w'], 'L0_attn_norm_f_w': _L0_attn_in['norm_f_w'], 'L0_attn_norm_f_b': _L0_attn_in['norm_f_b'], 'L0_ffn_router_w': _L0_ffn_in['router_w'], 'L0_ffn_w_gate': _L0_ffn_in['w_gate'], 'L0_ffn_w_up': _L0_ffn_in['w_up'], 'L0_ffn_w_down': _L0_ffn_in['w_down'], 'L0_ffn_ws_gate': _L0_ffn_in['ws_gate'], 'L0_ffn_ws_up': _L0_ffn_in['ws_up'], 'L0_ffn_ws_down': _L0_ffn_in['ws_down'], 'L0_ffn_sg_w': _L0_ffn_in['sg_w'], 'L0_ffn_sg_b': _L0_ffn_in['sg_b'], 'L1_attn_qkv_w': _L1_attn_in['qkv_w'], 'L1_attn_proj_w': _L1_attn_in['proj_w'], 'L1_attn_proj_b': _L1_attn_in['proj_b'], 'L1_ffn_ln_w': _L1_ffn_in['ln_w'], 'L1_ffn_w_router': _L1_ffn_in['w_router'], 'L1_ffn_wi': _L1_ffn_in['wi'], 'L1_ffn_wo': _L1_ffn_in['wo']}

def reference(x, txt, L0_tok_patch_w, L0_tok_patch_b, L0_tok_ln_g, L0_tok_ln_b, L0_tok_qkv_w, L0_tok_qkv_b, L0_tok_proj_w, L0_tok_proj_b, L0_tok_ff1_w, L0_tok_ff1_b, L0_tok_ff2_w, L0_tok_ff2_b, L0_attn_norm_w, L0_attn_norm_b, L0_attn_in_proj_w, L0_attn_conv_w, L0_attn_conv_b, L0_attn_x_proj_w, L0_attn_dt_proj_w, L0_attn_dt_proj_b, L0_attn_A_log, L0_attn_D_skip, L0_attn_out_proj_w, L0_attn_norm_f_w, L0_attn_norm_f_b, L0_ffn_router_w, L0_ffn_w_gate, L0_ffn_w_up, L0_ffn_w_down, L0_ffn_ws_gate, L0_ffn_ws_up, L0_ffn_ws_down, L0_ffn_sg_w, L0_ffn_sg_b, L1_attn_qkv_w, L1_attn_proj_w, L1_attn_proj_b, L1_ffn_ln_w, L1_ffn_w_router, L1_ffn_wi, L1_ffn_wo):
    import jax
    import jax.numpy as jnp

    def _L0_tok_ref(input, patch_w, patch_b, ln_g, ln_b, qkv_w, qkv_b, proj_w, proj_b, ff1_w, ff1_b, ff2_w, ff2_b):
        import jax, jax.numpy as jnp
        import numpy as np
        P = 16
        WIN = 64
        NH = 12

        def _layernorm(x, g, b, eps=1e-05):
            m = x.mean(-1, keepdims=True)
            v = ((x - m) ** 2).mean(-1, keepdims=True)
            return (x - m) * jax.lax.rsqrt(v + eps) * g + b

        def _sinusoidal_pe(n, d):
            pos = jnp.arange(n, dtype=jnp.float32)[:, None]
            i = jnp.arange(d // 2, dtype=jnp.float32)[None, :]
            ang = pos / jnp.power(10000.0, 2.0 * i / d)
            pe = jnp.zeros((n, d), jnp.float32)
            pe = pe.at[:, 0::2].set(jnp.sin(ang)).at[:, 1::2].set(jnp.cos(ang))
            return pe
        B, C, H, W = input.shape
        D = patch_w.shape[0]
        dh = D // NH
        xp = input.reshape(B, C, H // P, P, W // P, P)
        x = jnp.einsum('bchpwq,dcpq->bhwd', xp, patch_w) + patch_b
        x = x.reshape(B, -1, D)
        x = _layernorm(x, ln_g, ln_b)
        N = x.shape[1]
        x = x + _sinusoidal_pe(N, D)

        def ff(y):
            return jax.nn.gelu(y @ ff1_w + ff1_b) @ ff2_w + ff2_b

        def sparse_attn(y):
            nW = N // WIN
            qkv = (y @ qkv_w + qkv_b).reshape(B, nW, WIN, 3, NH, dh)
            q, k, v = (qkv[:, :, :, 0], qkv[:, :, :, 1], qkv[:, :, :, 2])
            scores = jnp.einsum('bwqhd,bwkhd->bwhqk', q, k) * dh ** (-0.5)
            a = jax.nn.softmax(scores, axis=-1)
            o = jnp.einsum('bwhqk,bwkhd->bwqhd', a, v).reshape(B, N, D)
            return o @ proj_w + proj_b
        identity = x
        x = ff(x)
        x = sparse_attn(x)
        x = x + identity
        identity = x
        x = ff(x)
        x = x + identity
        return x

    def _L0_attn_ref(embeddings, norm_w, norm_b, in_proj_w, conv_w, conv_b, x_proj_w, dt_proj_w, dt_proj_b, A_log, D_skip, out_proj_w, norm_f_w, norm_f_b):
        import jax, jax.numpy as jnp
        import numpy as np
        D_MODEL = 192
        N_LAYER = 4
        D_INNER = 2 * D_MODEL
        D_STATE = 16
        D_CONV = 4
        DT_RANK = (D_MODEL + 15) // 16
        EPS = 1e-05

        def _ln(x, w, b):
            mu = jnp.mean(x, axis=-1, keepdims=True)
            var = jnp.mean(jnp.square(x - mu), axis=-1, keepdims=True)
            return (x - mu) * jax.lax.rsqrt(var + EPS) * w + b

        def _mixer(u, p):
            B, L, _ = u.shape
            xz = jnp.einsum('bld,ed->ble', u, p['in_proj_w'])
            x, z = jnp.split(xz, 2, axis=-1)
            xp = jnp.pad(x, ((0, 0), (D_CONV - 1, 0), (0, 0)))
            x = sum((p['conv_w'][:, k] * xp[:, k:k + L, :] for k in range(D_CONV))) + p['conv_b']
            x = jax.nn.silu(x)
            x_dbl = jnp.einsum('bld,ed->ble', x, p['x_proj_w'])
            dt, Bm, Cm = jnp.split(x_dbl, [DT_RANK, DT_RANK + D_STATE], axis=-1)
            dt = jax.nn.softplus(jnp.einsum('blr,dr->bld', dt, p['dt_proj_w']) + p['dt_proj_b'])
            A = -jnp.exp(p['A_log'])

            def step(h, xs):
                dt_t, B_t, C_t, x_t = xs
                dA = jnp.exp(dt_t[:, :, None] * A)
                h = dA * h + (dt_t * x_t)[:, :, None] * B_t[:, None, :]
                y = jnp.einsum('bds,bs->bd', h, C_t)
                return (h, y)
            h0 = jnp.zeros((B, D_INNER, D_STATE), x.dtype)
            xs = (dt.transpose(1, 0, 2), Bm.transpose(1, 0, 2), Cm.transpose(1, 0, 2), x.transpose(1, 0, 2))
            _, ys = jax.lax.scan(step, h0, xs)
            y = ys.transpose(1, 0, 2) + x * p['D_skip']
            y = y * jax.nn.silu(z)
            return jnp.einsum('bld,ed->ble', y, p['out_proj_w'])
        params = dict(norm_w=norm_w, norm_b=norm_b, in_proj_w=in_proj_w, conv_w=conv_w, conv_b=conv_b, x_proj_w=x_proj_w, dt_proj_w=dt_proj_w, dt_proj_b=dt_proj_b, A_log=A_log, D_skip=D_skip, out_proj_w=out_proj_w)

        def layer_step(carry, p):
            hidden, residual = carry
            residual = hidden + residual
            h = _ln(residual, p['norm_w'], p['norm_b'])
            h = _mixer(h, p)
            return ((h, residual), None)
        carry = (embeddings, jnp.zeros_like(embeddings))
        (hidden, residual), _ = jax.lax.scan(layer_step, carry, params)
        residual = hidden + residual
        return _ln(residual, norm_f_w, norm_f_b)

    def _L0_ffn_ref(x, router_w, w_gate, w_up, w_down, ws_gate, ws_up, ws_down, sg_w, sg_b):
        import jax, jax.numpy as jnp
        import numpy as np
        B, S, D = (4, 256, 192)
        E = 8
        H = 192
        HS = 768
        TOPK_ROUTED = 2
        probs = jax.nn.softmax(x @ router_w, axis=-1)
        gates, idx = jax.lax.top_k(probs, TOPK_ROUTED)
        gates = gates / jnp.sum(gates, axis=-1, keepdims=True)
        n_exp = router_w.shape[1]
        dense_g = jnp.sum(jax.nn.one_hot(idx, n_exp, dtype=x.dtype) * gates[..., None], axis=-2)
        g = jax.nn.silu(jnp.einsum('bsd,edh->bseh', x, w_gate))
        u = jnp.einsum('bsd,edh->bseh', x, w_up)
        expert_out = jnp.einsum('bseh,ehd->bsed', g * u, w_down)
        routed = jnp.einsum('bse,bsed->bsd', dense_g, expert_out)
        shared = jax.nn.silu(x @ ws_gate) * (x @ ws_up) @ ws_down
        alpha = jax.nn.sigmoid(x @ sg_w + sg_b)
        return alpha * shared + (1.0 - alpha) * routed

    def _L1_attn_ref(x, qkv_w, proj_w, proj_b):
        import jax, jax.numpy as jnp
        import numpy as np
        NUM_HEADS = 12

        def _attn(q, k, v, scale):
            s = jnp.einsum('bhqd,bhkd->bhqk', q, k) * scale
            p = jax.nn.softmax(s, axis=-1)
            return jnp.einsum('bhqk,bhkd->bhqd', p, v)
        B, N, C = x.shape
        H = NUM_HEADS
        hd = C // H
        scale = hd ** (-0.5)
        t = 0.5 * scale
        qkv = (x @ qkv_w.T).reshape(B, N, 3, H, hd).transpose(2, 0, 3, 1, 4)
        q, k, v = (qkv[0], qkv[1], qkv[2])
        qd = jax.lax.stop_gradient(q)
        kd = jax.lax.stop_gradient(k)
        vd = jax.lax.stop_gradient(v)

        def body(carry, ei):
            qp = qd.at[..., ei].add(t)
            qm = qd.at[..., ei].add(-t)
            Hp = _attn(qp, kd, vd, scale)
            Hm = _attn(qm, kd, vd, scale)
            Wi = jnp.sum(jnp.abs(Hp - Hm), axis=(-1, -2)) / (2.0 * t * N)
            return (carry, Wi)
        _, Ws = jax.lax.scan(body, None, jnp.arange(hd))
        W = jnp.transpose(Ws, (1, 2, 0))
        out = _attn(q * W[:, :, None, :], k, v, scale)
        out = out.transpose(0, 2, 1, 3).reshape(B, N, C)
        return out @ proj_w.T + proj_b

    def _L1_ffn_ref(x, ln_w, w_router, wi, wo):
        import jax, jax.numpy as jnp
        import numpy as np
        B, S, D, F, E = (8, 512, 192, 768, 16)
        CAP = 64
        EPS = 1e-06

        def _switch_moe_block(x, ln_w, w_router, wi, wo):
            var = jnp.mean(jnp.square(x.astype(jnp.float32)), axis=-1, keepdims=True)
            normed = (x * jax.lax.rsqrt(var + EPS)).astype(x.dtype) * ln_w
            logits = jnp.einsum('bsd,de->bse', normed.astype(jnp.float32), w_router.astype(jnp.float32))
            probs = jax.nn.softmax(logits, axis=-1)
            expert_idx = jnp.argmax(probs, axis=-1)
            onehot = jax.nn.one_hot(expert_idx, E, dtype=jnp.float32)
            priority = jnp.cumsum(onehot, axis=1)
            keep = onehot * (priority <= CAP)
            pos = (priority - 1.0).astype(jnp.int32)
            dispatch = keep[..., None] * jax.nn.one_hot(pos, CAP, dtype=jnp.float32)
            expert_in = jnp.einsum('bsec,bsd->becd', dispatch, normed)
            h = jax.nn.relu(jnp.einsum('becd,edf->becf', expert_in, wi))
            expert_out = jnp.einsum('becf,efd->becd', h, wo)
            combined = jnp.einsum('bsec,becd->bsd', dispatch, expert_out)
            routed = jnp.sum(dispatch, axis=(2, 3)) > 0
            next_states = jnp.where(routed[..., None], combined.astype(x.dtype), normed)
            router_prob = jnp.max(probs, axis=-1, keepdims=True).astype(x.dtype)
            return x + router_prob * next_states
        return _switch_moe_block(x, ln_w, w_router, wi, wo)
    h = _L0_tok_ref(x, L0_tok_patch_w, L0_tok_patch_b, L0_tok_ln_g, L0_tok_ln_b, L0_tok_qkv_w, L0_tok_qkv_b, L0_tok_proj_w, L0_tok_proj_b, L0_tok_ff1_w, L0_tok_ff1_b, L0_tok_ff2_w, L0_tok_ff2_b)
    h = jnp.concatenate([h, txt], axis=1)
    h = h + _L0_attn_ref(_layernorm(h, axis=-1), L0_attn_norm_w, L0_attn_norm_b, L0_attn_in_proj_w, L0_attn_conv_w, L0_attn_conv_b, L0_attn_x_proj_w, L0_attn_dt_proj_w, L0_attn_dt_proj_b, L0_attn_A_log, L0_attn_D_skip, L0_attn_out_proj_w, L0_attn_norm_f_w, L0_attn_norm_f_b)
    h = h + _L0_ffn_ref(_layernorm(h, axis=-1), L0_ffn_router_w, L0_ffn_w_gate, L0_ffn_w_up, L0_ffn_w_down, L0_ffn_ws_gate, L0_ffn_ws_up, L0_ffn_ws_down, L0_ffn_sg_w, L0_ffn_sg_b)
    h = h + _L1_attn_ref(_layernorm(h, axis=-1), L1_attn_qkv_w, L1_attn_proj_w, L1_attn_proj_b)
    h = h + _L1_ffn_ref(_layernorm(h, axis=-1), L1_ffn_ln_w, L1_ffn_w_router, L1_ffn_wi, L1_ffn_wo)
    return h

_drawn_inputs = setup_inputs


def setup_inputs(seed=0):
    import zlib

    import numpy as np

    out = dict(_drawn_inputs(seed))
    spreads = {'L0_tok_patch_b': (0.0, 0.1),
     'L0_tok_ln_g': (1.0, 0.2),
     'L0_tok_ln_b': (0.0, 0.1),
     'L0_tok_qkv_b': (0.0, 0.539),
     'L0_tok_proj_b': (0.0, 0.1),
     'L0_tok_ff1_b': (0.0, 0.459),
     'L0_tok_ff2_b': (0.0, 0.1),
     'L0_attn_norm_w': (1.0, 0.6),
     'L0_attn_norm_b': (0.0, 0.8),
     'L0_attn_conv_b': (0.0, 0.8),
     'L0_attn_dt_proj_b': (-4.600165843963623, 0.6),
     'L0_attn_D_skip': (1.0, 0.6),
     'L0_attn_norm_f_w': (1.0, 0.2),
     'L0_attn_norm_f_b': (0.0, 0.1),
     'L1_attn_proj_b': (0.0, 0.495),
     'L1_ffn_ln_w': (1.0, 0.6)}
    factors = {'L0_tok_qkv_w': 8.0,
     'L0_tok_proj_w': 3.593,
     'L0_attn_in_proj_w': 8.0,
     'L0_attn_conv_w': 8.0,
     'L0_attn_x_proj_w': 8.0,
     'L0_attn_dt_proj_w': 8.0,
     'L0_attn_A_log': 8.0,
     'L0_attn_out_proj_w': 8.0,
     'L0_ffn_router_w': 8.0,
     'L0_ffn_w_gate': 8.0,
     'L0_ffn_w_up': 8.0,
     'L0_ffn_w_down': 8.0,
     'L0_ffn_ws_gate': 8.0,
     'L0_ffn_ws_up': 8.0,
     'L0_ffn_ws_down': 8.0,
     'L0_ffn_sg_w': 8.0,
     'L1_ffn_wi': 3.06}
    for name, (base, spread) in spreads.items():
        noise = np.random.default_rng([zlib.crc32(name.encode()), seed]).standard_normal(out[name].shape)
        drawn = base * np.exp(spread * noise) if base else spread * noise
        out[name] = jnp.asarray(drawn.astype(out[name].dtype))
    for name, factor in factors.items():
        out[name] = (out[name] * factor).astype(out[name].dtype)
    return out
```

```python
from contextlib import ExitStack

import numpy as np

import concourse.bass as bass
from concourse import mybir

F32 = mybir.dt.float32
BF16 = mybir.dt.bfloat16
ALU = mybir.AluOpType
ACT = mybir.ActivationFunctionType
AX = mybir.AxisListType

B = 16
NIMG, NTXT = 64, 77
T = NIMG + NTXT
N = B * T
D = 192
P = 96
KD = D // P
NH, DH = 12, 16
HP = 32
QC = NH * HP // 128
FF = 768
FC = FF // 128
PAIR = 2 * T
NPAIR = B // 2
ds = bass.ds


def bcast(ap, axis, shape):
    return ap.unsqueeze(axis).broadcast_to(shape)


class Scope:

    def __init__(self, nc, ctx, tag):
        self.nc, self.ctx, self.tag = nc, ctx, tag
        self.all_sems = []
        ctx.callback(self.clear)

    def clear(self):
        if self.all_sems:
            self.nc.all_engine_barrier()
            self.nc.clear_and_free_semaphores(self.all_sems)
            self.nc.all_engine_barrier()

    def sb(self, name, shape, dt=F32):
        return self.ctx.enter_context(self.nc.sbuf_tensor(f"{self.tag}_{name}", shape, dt))

    def sem(self, name):
        self.all_sems.append(self.nc.alloc_semaphore(f"{self.tag}_{name}"))
        return self.all_sems[-1]

    def sems(self, *names):
        return [self.sem(n) for n in names]


class Norm:

    def __init__(self, s, tag, q, w, mean_ps, var_ps, ones, eps, center=True, xc=None, sq=None):
        self.q, self.w, self.mean_ps, self.var_ps, self.ones, self.eps = q, w, mean_ps, var_ps, ones, eps
        self.center = center
        self.xc = s.sb(f"{tag}_xc", [P, KD, q * w]) if center and xc is None else xc
        self.sq = s.sb(f"{tag}_sq", [P, KD, q * w]) if sq is None else sq
        self.rstd = s.sb(f"{tag}_rstd", [P, q * w])
        self.x_ready, self.mean_ready, self.centered, self.squared, self.var_ready, self.logvar, \
            self.rstd_ready, self.normed = s.sems(*(f"{tag}_{x}" for x in (
                "x_ready", "mean_ready", "centered", "squared", "var_ready", "logvar", "rstd_ready", "normed")))

    def total(self, nc, ps, x):
        for q in range(self.q):
            for k in range(KD):
                mm = nc.tensor.matmul(ps[:, q, :], self.ones[:, :], x[:, k, q * self.w:(q + 1) * self.w],
                                      start=k == 0, stop=k == KD - 1)
        return mm

    def split(self, ap):
        return ap.rearrange("p k (q t) -> p k q t", t=self.w)

    def pe(self, nc, pe, v, cols=None):
        if self.center:
            pe.wait_ge(self.x_ready, v)
            for q in range(self.q):
                for k in range(KD):
                    mm = nc.tensor.matmul(self.mean_ps[:, q, :], self.ones[:, :], cols(k, q * self.w, self.w),
                                          start=k == 0, stop=k == KD - 1)
            mm.then_inc(self.mean_ready, 1)
        pe.wait_ge(self.squared, v)
        self.total(nc, self.var_ps, self.sq).then_inc(self.var_ready, 1)

    def act(self, nc, act, v, x=None):
        if self.center:
            act.wait_ge(self.centered, v)
            nc.scalar.activation(self.sq[:, :, :], self.xc[:, :, :], ACT.Square).then_inc(self.squared, 1)
        else:
            act.wait_ge(self.x_ready, v)
            nc.scalar.activation(self.sq[:, :, :], x, ACT.Square).then_inc(self.squared, 1)
        act.wait_ge(self.var_ready, v)
        nc.scalar.activation(self.rstd[:, :].rearrange("p (q t) -> p q t", t=self.w), self.var_ps, ACT.Ln,
                             bias=self.eps[:, 0:1]).then_inc(self.logvar, 1)
        act.wait_ge(self.logvar, v)
        nc.scalar.activation(self.rstd[:, :], self.rstd[:, :], ACT.Exp, scale=-0.5).then_inc(self.rstd_ready, 1)

    def dve(self, nc, dve, v, x, out):
        if self.center:
            dve.wait_ge(self.mean_ready, v)
            nc.vector.tensor_tensor(self.split(self.xc[:, :, :]), self.split(x),
                                    bcast(self.mean_ps, 1, [P, KD, self.q, self.w]),
                                    ALU.subtract).then_inc(self.centered, 1)
        dve.wait_ge(self.rstd_ready, v)
        src = self.xc[:, :, :] if self.center else x
        nc.vector.tensor_tensor(out, src, bcast(self.rstd[:, :], 1, [P, KD, self.q * self.w]), ALU.mult)\
            .then_inc(self.normed, 1)


class FeedForward:

    def __init__(self, s, n, PS, bank, w1, b1, w2):
        self.n, self.PS, self.bank, self.w1, self.b1, self.w2 = n, PS, bank, w1, b1, w2
        self.hid = s.sb("ff_hid", [128, FC, n])
        self.in_ready, self.hid_summed, self.hid_ready, self.out_summed = s.sems(
            "ff_in_ready", "ff_hid_summed", "ff_hid_ready", "ff_out_summed")

    def pe(self, nc, pe, v, x):
        pe.wait_ge(self.in_ready, v + 1)
        for j in range(FC):
            if j >= 2:
                pe.wait_ge(self.hid_ready, v * FC + (j - 1))
            for k in range(KD):
                mm = nc.tensor.matmul(self.PS[:, self.bank + j % 2, 0:self.n], self.w1[:, k, j * 128:(j + 1) * 128],
                                      x[:, k, :], start=k == 0, stop=k == KD - 1)
            mm.then_inc(self.hid_summed, 1)
        for j in range(FC):
            pe.wait_ge(self.hid_ready, v * FC + (j + 1))
            for m in range(KD):
                mm = nc.tensor.matmul(self.PS[0:P, self.bank + 2 + m, 0:self.n], self.w2[:, j, m * P:(m + 1) * P],
                                      self.hid[:, j, :], start=j == 0, stop=j == FC - 1)
        mm.then_inc(self.out_summed, 1)

    def act(self, nc, act, v):
        for j in range(FC):
            act.wait_ge(self.hid_summed, v * FC + (j + 1))
            nc.scalar.activation(self.hid[:, j, :], self.PS[:, self.bank + j % 2, 0:self.n], ACT.Gelu_apprx_tanh,
                                 bias=self.b1[:, j:j + 1]).then_inc(self.hid_ready, 1)


def tokenizer(nc, dr, PS, C, h):
    NI = B * NIMG
    NB = 512
    NL = NI // NB
    WT = 2 * NIMG
    NW = NI // WT
    KP = 6
    with ExitStack() as ctx:
        s = Scope(nc, ctx, "tok")
        pix = s.sb("pix", [128, KP, NI])
        wp = s.sb("wp", [128, KP, D])
        ff1 = s.sb("ff1", [P, KD, FF])
        ff2 = s.sb("ff2", [128, FC, D])
        wqk = s.sb("wqk", [P, KD, 2, QC * 128])
        wv = s.sb("wv", [P, KD, QC * 128])
        wo = s.sb("wo", [128, QC, D])
        vec = s.sb("vec", [P, 5, KD])
        b1 = s.sb("b1", [128, FC])
        bqk = s.sb("bqk", [128, 2, QC])
        bv = s.sb("bv", [NIMG, QC * 128])
        pos = s.sb("pos", [P, KD, NIMG])
        emb = s.sb("emb", [P, KD, NB])
        xg = s.sb("xg", [P, KD, NB])
        ident = s.sb("ident", [P, KD, NI])
        y1 = s.sb("y1", [P, KD, NI])
        x2 = s.sb("x2", [P, KD, NI])
        yb = s.sb("yb", [P, KD, WT])
        qk = s.sb("qk", [128, 2, QC, WT])
        v = s.sb("v", [NIMG, 2, QC * 128])
        mx = s.sb("mx", [NIMG, 4, 6])
        sx = s.sb("sx", [NIMG, 4, 6, NIMG])
        ex = s.sb("ex", [NIMG, 4, 6, NIMG])
        pT = s.sb("pT", [NIMG, 24, NIMG])
        oT = s.sb("oT", [128, QC, WT])
        ln = Norm(s, "ln", 1, NB, PS[0:P, 6:7, :], PS[0:P, 7:8, :], C.ones, C.eps5)
        ff = FeedForward(s, NB, PS, 2, ff1, b1, ff2)
        loaded, patch_summed, ident_ready, y1_ready, gained, scaled = s.sems(
            "loaded", "patch_summed", "ident_ready", "y1_ready", "gained", "scaled")
        yb_ready, qk_summed, qk_ready, v_summed, v_ready, scored, maxed, shifted, exped, summed, inverted, probs, \
            turned, pT_ready, mixed, oT_ready, projected, x2_ready, h_ready = s.sems(
                "yb_ready", "qk_summed", "qk_ready", "v_summed", "v_ready", "scored", "maxed", "shifted", "exped",
                "summed", "inverted", "probs", "turned", "pT_ready", "mixed", "oT_ready", "projected", "x2_ready",
                "h_ready")
        h4 = h[:, :, :].rearrange("p k (b t) -> p k b t", t=T)
        loads = [(pix[:, :, :], dr["pix"]), (wp[:, :, :], dr["wp"]), (vec[:, :, :], dr["tok_vec"]),
                 (pos[:, :, :], dr["pos"]), (ff1[:, :, :], dr["ff1"]), (b1[:, :], dr["ff1_b"]),
                 (ff2[:, :, :], dr["ff2"]), (wqk[:, :, :, :], dr["tok_wqk"]), (bqk[:, :, :], dr["tok_bqk"]),
                 (wv[:, :, :], dr["tok_wv"]), (bv[:, :], dr["tok_bv"].partition_broadcast(NIMG)),
                 (wo[:, :, :], dr["tok_wo"]), (C.ones[:, :], dr["ones"]), (C.ident[:, :], dr["ident"])]
        loads += [(h4[:, k, :, NIMG:T], dr["txt"][:, k, :, :]) for k in range(KD)]
        ALL = 16 * len(loads)
        block = ctx.enter_context(nc.Block())

        @block.sync
        def _(sp):
            for dst, src in loads:
                sp.dma_start(dst, src).then_inc(loaded, 16)
            sp.wait_ge(loaded, ALL)

        @block.tensor
        def _(pe):
            pe.wait_ge(loaded, ALL)
            with pe.Fori(0, NL) as i:
                for m in range(KD):
                    for k in range(KP):
                        mm = nc.tensor.matmul(PS[0:P, m, :], wp[:, k, m * P:(m + 1) * P], pix[:, k, ds(i * NB, NB)],
                                              start=k == 0, stop=k == KP - 1)
                mm.then_inc(patch_summed, 1)
                ln.pe(nc, pe, i + 1, lambda k, at, w: emb[:, k, at:at + w])
                ff.pe(nc, pe, i, ident[:, :, ds(i * NB, NB)])
            with pe.Fori(0, NW) as i:
                pe.wait_ge(yb_ready, i + 1)
                for a in range(2):
                    for c in range(QC):
                        for k in range(KD):
                            mm = nc.tensor.matmul(PS[:, a, c * WT:(c + 1) * WT], wqk[:, k, a, c * 128:(c + 1) * 128],
                                                  yb[:, k, :], start=k == 0, stop=k == KD - 1)
                    mm.then_inc(qk_summed, 1)
                for w in range(2):
                    for k in range(KD):
                        mm = nc.tensor.matmul(PS[0:NIMG, 2 + w, 0:QC * 128], yb[:, k, w * NIMG:(w + 1) * NIMG],
                                              wv[:, k, :], start=k == 0, stop=k == KD - 1)
                mm.then_inc(v_summed, 1)
                pe.wait_ge(qk_ready, 2 * i + 2)
                for j in range(4):
                    for w in range(2):
                        for c in range(QC):
                            rows, cols, slot = slice(HP * j, HP * j + DH), slice(w * NIMG, (w + 1) * NIMG), w * QC + c
                            mm = nc.tensor.matmul(PS[0:NIMG, 4 + j, slot * NIMG:(slot + 1) * NIMG],
                                                  qk[rows, 0, c, cols], qk[rows, 1, c, cols], start=True, stop=True)
                mm.then_inc(scored, 1)
                pe.wait_ge(loaded, ALL)
                pe.wait_ge(probs, i + 1)
                pe.wait_ge(v_ready, i + 1)
                for n in range(24):
                    mm = nc.tensor.transpose(PS[0:NIMG, n // 8, (n % 8) * NIMG:(n % 8 + 1) * NIMG],
                                             ex[:, n // 6, n % 6, :], C.ident[0:NIMG, 0:NIMG])
                mm.then_inc(turned, 1)
                pe.wait_ge(loaded, ALL)
                pe.wait_ge(pT_ready, i + 1)
                for j in range(4):
                    for w in range(2):
                        for c in range(QC):
                            mm = nc.tensor.matmul(PS[HP * j:HP * (j + 1), 3, c * WT + w * NIMG:c * WT + (w + 1) * NIMG],
                                                  v[:, w, (4 * c + j) * HP:(4 * c + j + 1) * HP],
                                                  pT[:, j * 6 + w * QC + c, :], start=True, stop=True)
                mm.then_inc(mixed, 1)
                pe.wait_ge(oT_ready, i + 1)
                for m in range(KD):
                    for c in range(QC):
                        mm = nc.tensor.matmul(PS[0:P, 4, m * WT:(m + 1) * WT], wo[:, c, m * P:(m + 1) * P],
                                              oT[:, c, :], start=c == 0, stop=c == QC - 1)
                mm.then_inc(projected, 1)
            with pe.Fori(0, NL) as i:
                ff.pe(nc, pe, i + NL, x2[:, :, ds(i * NB, NB)])

        @block.scalar
        def _(act):
            act.wait_ge(loaded, ALL)
            with act.Fori(0, NL) as i:
                act.wait_ge(patch_summed, i + 1)
                for m in range(KD):
                    op = nc.scalar.activation(emb[:, m, :], PS[0:P, m, :], ACT.Identity, bias=vec[:, 0, m:m + 1])
                op.then_inc(ln.x_ready, 1)
                ln.act(nc, act, i + 1)
                ff.act(nc, act, i)
                act.wait_ge(ff.out_summed, i + 1)
                for m in range(KD):
                    op = nc.scalar.activation(y1[:, m, ds(i * NB, NB)], PS[0:P, 4 + m, :], ACT.Identity,
                                              bias=vec[:, 3, m:m + 1])
                op.then_inc(y1_ready, 1)
            with act.Fori(0, NW) as i:
                act.wait_ge(shifted, i + 1)
                nc.scalar.activation(ex[:, :, :, :], sx[:, :, :, :], ACT.Exp, scale=DH ** -0.5).then_inc(exped, 1)
                act.wait_ge(turned, i + 1)
                nc.scalar.activation(pT[:, :, :], PS[0:NIMG, 0:3, :].rearrange("p a (b t) -> p (a b) t", t=NIMG),
                                     ACT.Copy).then_inc(pT_ready, 1)
                act.wait_ge(mixed, i + 1)
                nc.scalar.activation(oT[:, :, :], PS[:, 3, 0:QC * WT].rearrange("p (c t) -> p c t", t=WT),
                                     ACT.Copy).then_inc(oT_ready, 1)
            with act.Fori(0, NL) as i:
                ff.act(nc, act, i + NL)

        @block.vector
        def _(dve):
            dve.wait_ge(loaded, ALL)
            with dve.Fori(0, NL) as i:
                ln.dve(nc, dve, i + 1, emb[:, :, :], emb[:, :, :])
                dve.wait_ge(ln.normed, i + 1)
                for m in range(KD):
                    op = nc.vector.tensor_scalar(xg[:, m, :], emb[:, m, :], vec[:, 1, m:m + 1], vec[:, 2, m:m + 1],
                                                 ALU.mult, ALU.add)
                op.then_inc(gained, 1)
                dve.wait_ge(gained, i + 1)
                for m in range(KD):
                    op = nc.vector.tensor_tensor(
                        ident[:, m, ds(i * NB, NB)].rearrange("p (b t) -> p b t", t=NIMG),
                        xg[:, m, :].rearrange("p (b t) -> p b t", t=NIMG),
                        bcast(pos[:, m, :], 1, [P, NB // NIMG, NIMG]), ALU.add)
                op.then_inc(ff.in_ready, 1)
            with dve.Fori(0, NW) as i:
                dve.wait_ge(y1_ready, NL)
                nc.vector.tensor_copy(yb[:, :, :], y1[:, :, ds(i * WT, WT)]).then_inc(yb_ready, 1)
                for a in range(2):
                    dve.wait_ge(qk_summed, 2 * i + (a + 1))
                    nc.vector.tensor_tensor(qk[:, a, :, :], PS[:, a, 0:QC * WT].rearrange("p (c t) -> p c t", t=WT),
                                            bcast(bqk[:, a, :], 2, [128, QC, WT]), ALU.add).then_inc(qk_ready, 1)
                dve.wait_ge(v_summed, i + 1)
                nc.vector.tensor_tensor(v[:, :, :], PS[0:NIMG, 2:4, 0:QC * 128],
                                        bcast(bv[:, :], 1, [NIMG, 2, QC * 128]), ALU.add).then_inc(v_ready, 1)
                sc = PS[0:NIMG, 4:8, 0:6 * NIMG].rearrange("p j (n t) -> p j n t", t=NIMG)
                dve.wait_ge(scored, i + 1)
                nc.vector.reduce_max(mx[:, :, :], sc, AX.X).then_inc(maxed, 1)
                dve.wait_ge(maxed, i + 1)
                for j in range(4):
                    op = nc.vector.tensor_tensor(sx[:, j, :, :], sc[:, j, :, :], bcast(mx[:, j, :], 2, [NIMG, 6, NIMG]),
                                                 ALU.subtract)
                op.then_inc(shifted, 1)
                dve.wait_ge(exped, i + 1)
                nc.vector.reduce_sum(mx[:, :, :], ex[:, :, :, :], AX.X).then_inc(summed, 1)
                dve.wait_ge(summed, i + 1)
                nc.vector.reciprocal(mx[:, :, :], mx[:, :, :]).then_inc(inverted, 1)
                dve.wait_ge(inverted, i + 1)
                for j in range(4):
                    op = nc.vector.tensor_tensor(ex[:, j, :, :], ex[:, j, :, :], bcast(mx[:, j, :], 2, [NIMG, 6, NIMG]),
                                                 ALU.mult)
                op.then_inc(probs, 1)
                dve.wait_ge(projected, i + 1)
                for m in range(KD):
                    op = nc.vector.scalar_tensor_tensor(
                        out=x2[:, m, ds(i * WT, WT)], in0=PS[0:P, 4, m * WT:(m + 1) * WT], scalar=vec[:, 4, m:m + 1],
                        in1=ident[:, m, ds(i * WT, WT)], op0=ALU.add, op1=ALU.add)
                op.then_inc(x2_ready, 1)
            dve.wait_ge(x2_ready, NW)
            with dve.Fori(0, NL) as i:
                nc.vector.sem_inc(ff.in_ready, 1)
                dve.wait_ge(ff.out_summed, i + NL + 1)
                for m in range(KD):
                    op = nc.vector.scalar_tensor_tensor(
                        out=h4[:, m, ds(i * 8, 8), 0:NIMG],
                        in0=PS[0:P, 4 + m, :].rearrange("p (b t) -> p b t", t=NIMG), scalar=vec[:, 3, m:m + 1],
                        in1=x2[:, m, ds(i * NB, NB)].rearrange("p (b t) -> p b t", t=NIMG), op0=ALU.add, op1=ALU.add)
                op.then_inc(h_ready, 1)
                dve.wait_ge(h_ready, i + 1)


def mamba(nc, dr, PS, C, h):
    L, DI, DS, DC, DR = 4, 384, 16, 4, 12
    CT = DI // 128
    QW = 4 * T
    NQ = N // QW
    HW = QW // 2
    SP2 = DS // 2
    UW = 2 * QW
    RESTART = 1e20
    with ExitStack() as ctx:
        s = Scope(nc, ctx, "ssm")
        res = s.sb("res", [P, KD, N])
        winx = s.sb("winx", [P, KD, DI])
        winz = s.sb("winz", [P, KD, DI])
        nvec = s.sb("nvec", [P, 2, KD])
        fvec = s.sb("fvec", [P, 2, KD])
        cvec = s.sb("cvec", [128, CT, DC + 3])
        a_log = s.sb("a_log", [128, CT, DS])
        amat = s.sb("amat", [128, CT, DS])
        wbc = s.sb("wbc", [128, CT, P])
        wdt = s.sb("wdt", [128, CT, DR])
        wdt2 = s.sb("wdt2", [DR, DI])
        wout = s.sb("wout", [128, CT, D])
        sel = s.sb("sel", [P, 2 * DS * 128], BF16)
        hn = s.sb("hn", [P, KD, QW])
        xs = s.sb("xs", [128, CT, QW])
        sz = s.sb("sz", [128, CT, QW])
        dt = s.sb("dt", [128, CT, QW])
        sp = s.sb("sp", [128, CT, QW])
        us = s.sb("us", [128, CT, QW])
        low = s.sb("low", [DR, QW])
        bcf = s.sb("bcf", [P, QW])
        bcr = s.sb("bcr", [P, QW])
        mid = s.sb("mid", [P, QW], BF16)
        bcp = s.sb("bcp", [P, QW], BF16)
        bb = s.sb("bb", [128, DS, QW])
        cb = s.sb("cb", [128, DS, QW])
        da = s.sb("da", [128, 2, UW])
        hs = s.sb("hs", [128, 2, UW])
        hc = s.sb("hc", [128, 2, UW])
        flat = PS[:, :, :].rearrange("p a b -> p (a b)")
        u_ps = flat[:, 0:QW]
        dbx = [flat[:, QW + n * UW:QW + (n + 1) * UW] for n in range(2)]
        assert QW + 2 * UW <= 6 * 512
        ln = Norm(s, "ln", 2, HW, PS[0:P, 0:2, 0:HW], PS[0:P, 2:4, 0:HW], C.ones, C.eps5,
                  xc=us[0:P, 0:KD, :], sq=sp[0:P, 0:KD, :])
        loaded, wloaded, layer_done, gained, xin_summed, tap, conv_done, z_summed, sz_ready, xs_ready, low_summed, \
            low_ready, dt_summed, dt_pre, dt_abs, dt_exp, dt_log, dt_ready, split1, split2, split3, bcp_ready, \
            b_summed, c_summed, b_ready, c_ready, a_exp, a_ready, us_ready, restart, u_ready, \
            da_ready, dbx_ready, scanned, weighted, reduced, y_taken, gated, out_summed, res_ready, h_ready = s.sems(
                "loaded", "wloaded", "layer_done", "gained", "xin_summed", "tap", "conv_done", "z_summed", "sz_ready",
                "xs_ready", "low_summed", "low_ready", "dt_summed", "dt_pre", "dt_abs", "dt_exp", "dt_log", "dt_ready",
                "split1", "split2", "split3", "bcp_ready", "b_summed", "c_summed", "b_ready", "c_ready", "a_exp",
                "a_ready", "us_ready", "restart", "u_ready", "da_ready", "dbx_ready", "scanned", "weighted", "reduced",
                "y_taken", "gated", "out_summed", "res_ready", "h_ready")
        entered = s.sems("pe_loop_entered", "dve_loop_entered", "pool_loop_entered")
        wloads = [(winx[:, :, :], "ssm_winx"), (winz[:, :, :], "ssm_winz"), (nvec[:, :, :], "ssm_nvec"),
                  (cvec[:, :, :], "ssm_cvec"), (a_log[:, :, :], "ssm_alog"), (wbc[:, :, :], "ssm_wbc"),
                  (wdt[:, :, :], "ssm_wdt"), (wdt2[:, :], "ssm_wdt2"), (wout[:, :, :], "ssm_wout")]
        NWL = 16 * len(wloads)
        two = lambda ap: ap.rearrange("p (q t) -> p q t", t=HW)
        block = ctx.enter_context(nc.Block())

        @block.sync
        def _(sync):
            sync.dma_start(sel[:, :], dr["ssm_sel"]).then_inc(loaded, 16)
            sync.dma_start(fvec[:, :, :], dr["ssm_fvec"]).then_inc(loaded, 16)
            with sync.Fori(0, L) as l:
                sync.wait_ge(layer_done, l + 1)
                for dst, name in wloads:
                    src = dr[name][ds(l, 1)]
                    src = src.rearrange("a p b -> (a p) b") if len(src.shape) == 3 else \
                        src.rearrange("a p b c -> (a p) b c")
                    sync.dma_start(dst, src).then_inc(wloaded, 16)
            sync.wait_ge(wloaded, NWL * L)
            sync.wait_ge(loaded, 32)

        @block.tensor
        def _(pe):
            with pe.Fori(0, NQ) as q:
                ln.pe(nc, pe, q + 1, lambda k, at, w: h[:, k, ds(q * QW + at, w)])
            pe.wait_ge(loaded, 32)
            with pe.Fori(0, L) as l:
                pe.wait_ge(wloaded, l * NWL + NWL)
                nc.tensor.sem_inc(entered[0], 1)
                with pe.Fori(0, NQ) as q:
                    v = l * NQ + q
                    ln.pe(nc, pe, v + (NQ + 1), lambda k, at, w: res[:, k, ds(q * QW + at, w)])
                    pe.wait_ge(gained, v + 1)
                    for c in range(CT):
                        for b in range(2):
                            for k in range(KD):
                                mm = nc.tensor.matmul(PS[:, 2 * c + b, 0:HW], winx[:, k, c * 128:(c + 1) * 128],
                                                      hn[:, k, b * HW:(b + 1) * HW], start=k == 0, stop=k == KD - 1)
                    mm.then_inc(xin_summed, 1)
                    pe.wait_ge(conv_done, v + 1)
                    for c in range(CT):
                        for b in range(2):
                            for k in range(KD):
                                mm = nc.tensor.matmul(PS[:, 2 * c + b, 0:HW], winz[:, k, c * 128:(c + 1) * 128],
                                                      hn[:, k, b * HW:(b + 1) * HW], start=k == 0, stop=k == KD - 1)
                    mm.then_inc(z_summed, 1)
                    pe.wait_ge(xs_ready, v + 1)
                    for b in range(2):
                        for c in range(CT):
                            nc.tensor.matmul(PS[0:P, 6 + b, 0:HW], wbc[:, c, :], xs[:, c, b * HW:(b + 1) * HW],
                                             start=c == 0, stop=c == CT - 1)
                    pe.wait_ge(sz_ready, v + 1)
                    for b in range(2):
                        for c in range(CT):
                            mm = nc.tensor.matmul(PS[0:DR, b, 0:HW], wdt[:, c, :], xs[:, c, b * HW:(b + 1) * HW],
                                                  start=c == 0, stop=c == CT - 1)
                    mm.then_inc(low_summed, 1)
                    pe.wait_ge(low_ready, v + 1)
                    for c in range(CT):
                        for b in range(2):
                            mm = nc.tensor.matmul(PS[:, 2 + 2 * c + b, 0:HW], wdt2[:, c * 128:(c + 1) * 128],
                                                  low[:, b * HW:(b + 1) * HW], start=True, stop=True)
                    mm.then_inc(dt_summed, 1)
                    pe.wait_ge(dt_pre, v + 1)
                    pe.wait_ge(bcp_ready, v + 1)
                    nc.tensor.sem_inc(entered[0], 1)
                    with pe.Fori(0, DS // 2) as j:
                        for e in range(2):
                            n = v * DS + j * 2 + e
                            for x, (taken, summed) in enumerate(((b_ready, b_summed), (c_ready, c_summed))):
                                pe.wait_ge(taken, n + 1)
                                for b in range(2):
                                    mm = nc.tensor.matmul(PS[:, 4 * x + 2 * e + b, 0:HW],
                                                          sel[:, ds(j * 256 + (x * DS + e) * 128, 128)],
                                                          bcp[:, b * HW:(b + 1) * HW], start=True, stop=True)
                                mm.then_inc(summed, 1)
                    with pe.Fori(0, CT) as c:
                        pe.wait_ge(y_taken, v * CT + c + 1)
                        for n in range(SP2):
                            pe.wait_ge(weighted, v * CT * SP2 + c * SP2 + (n + 3))
                            for e in range(2):
                                for b in range(2):
                                    at = e * QW + b * HW
                                    mm = nc.tensor.matmul(PS[:, 6 + b, 0:HW], C.ident[:, :], hc[:, n % 2, at:at + HW],
                                                          start=n == 0 and e == 0, stop=n == SP2 - 1 and e == 1)
                            mm.then_inc(reduced, 1)
                    pe.wait_ge(gated, v + 1)
                    for m in range(KD):
                        for b in range(2):
                            for c in range(CT):
                                mm = nc.tensor.matmul(PS[0:P, 2 * m + b, 0:HW], wout[:, c, m * P:(m + 1) * P],
                                                      xs[:, c, b * HW:(b + 1) * HW], start=c == 0, stop=c == CT - 1)
                    mm.then_inc(out_summed, 1)
            with pe.Fori(0, NQ) as q:
                ln.pe(nc, pe, q + (NQ + L * NQ + 1), lambda k, at, w: res[:, k, ds(q * QW + at, w)])

        @block.scalar
        def _(act):
            with act.Fori(0, NQ) as q:
                ln.act(nc, act, q + 1)
            with act.Fori(0, L) as l:
                act.wait_ge(wloaded, l * NWL + NWL)
                with act.Fori(0, NQ) as q:
                    v = l * NQ + q
                    ln.act(nc, act, v + (NQ + 1))
                    nc.scalar.activation(amat[:, :, :], a_log[:, :, :], ACT.Exp).then_inc(a_exp, 1)
                    act.wait_ge(conv_done, v + 1)
                    nc.scalar.activation(xs[:, :, :], xs[:, :, :], ACT.Silu).then_inc(xs_ready, 1)
                    act.wait_ge(z_summed, v + 1)
                    nc.scalar.activation(sz[:, :, :].rearrange("p c (b t) -> p (c b) t", t=HW), PS[:, 0:6, 0:HW],
                                         ACT.Silu).then_inc(sz_ready, 1)
                    act.wait_ge(low_summed, v + 1)
                    nc.scalar.activation(two(bcf[:, :]), PS[0:P, 6:8, 0:HW], ACT.Copy)
                    nc.scalar.activation(two(low[:, :]), PS[0:DR, 0:2, 0:HW], ACT.Copy).then_inc(low_ready, 1)
                    act.wait_ge(dt_summed, v + 1)
                    for c in range(CT):
                        op = nc.scalar.activation(two(dt[:, c, :]), PS[:, 2 + 2 * c:4 + 2 * c, 0:HW], ACT.Identity,
                                                  bias=cvec[:, c, DC + 1:DC + 2])
                    op.then_inc(dt_pre, 1)
                    act.wait_ge(dt_pre, v + 1)
                    nc.scalar.activation(sp[:, :, :], dt[:, :, :], ACT.Abs).then_inc(dt_abs, 1)
                    act.wait_ge(dt_abs, v + 1)
                    nc.scalar.activation(sp[:, :, :], sp[:, :, :], ACT.Exp, scale=-1.0).then_inc(dt_exp, 1)
                    act.wait_ge(dt_exp, v + 1)
                    nc.scalar.activation(sp[:, :, :], sp[:, :, :], ACT.Ln, bias=1.0).then_inc(dt_log, 1)
                    with act.Fori(0, DS // 2) as j:
                        for e in range(2):
                            n = v * DS + j * 2 + e
                            act.wait_ge(b_summed, n + 1)
                            nc.scalar.activation(two(bb[:, ds(j * 2 + e, 1), :].rearrange("p a t -> p (a t)")),
                                                 PS[:, 2 * e:2 * e + 2, 0:HW], ACT.Copy).then_inc(b_ready, 1)
                    act.wait_ge(restart, v + 1)
                    act.wait_ge(a_ready, v + 1)
                    with act.Fori(0, CT) as c:
                        for n in range(SP2):
                            act.wait_ge(scanned, v * CT * SP2 + c * SP2 + (n + 1))
                            for e in range(2):
                                op = nc.scalar.activation(
                                    da[:, n % 2, e * QW:(e + 1) * QW],
                                    dt[:, ds(c, 1), :].rearrange("p a t -> p (a t)"), ACT.Exp,
                                    scale=amat[:, ds(c, 1), 2 * n + e:2 * n + e + 1].rearrange("p a t -> p (a t)"))
                            op.then_inc(da_ready, 1)
            with act.Fori(0, NQ) as q:
                ln.act(nc, act, q + (NQ + L * NQ + 1))

        @block.gpsimd
        def _(pool):
            pool.sem_inc(weighted, 2)
            with pool.Fori(0, L * NQ) as v:
                pool.wait_ge(c_ready, v * DS + (DS + 2))
                nc.gpsimd.sem_inc(entered[2], 1)
                with pool.Fori(0, CT) as c:
                    for n in range(SP2):
                        u = v * CT * SP2 + c * SP2 + n
                        pool.wait_ge(scanned, u + 3)
                        pool.wait_ge(reduced, u + 1)
                        nc.gpsimd.tensor_tensor(hc[:, n % 2, :], hs[:, n % 2, :],
                                                cb[:, 2 * n:2 * n + 2, :].rearrange("p a t -> p (a t)"),
                                                ALU.mult).then_inc(weighted, 1)

        @block.vector
        def _(dve):
            nc.vector.sem_inc(layer_done, 1)
            nc.vector.sem_inc(scanned, 2)
            nc.vector.sem_inc(reduced, 2)
            nc.vector.sem_inc(b_ready, 2)
            nc.vector.sem_inc(c_ready, 2)
            nc.vector.sem_inc(y_taken, 1)
            with dve.Fori(0, NQ) as q:
                nc.vector.sem_inc(ln.x_ready, 1)
                ln.dve(nc, dve, q + 1, h[:, :, ds(q * QW, QW)], res[:, :, ds(q * QW, QW)])
                dve.wait_ge(ln.normed, q + 1)
            with dve.Fori(0, L) as l:
                dve.wait_ge(wloaded, l * NWL + NWL)
                nc.vector.sem_inc(entered[1], 1)
                with dve.Fori(0, NQ) as q:
                    v = l * NQ + q
                    nc.vector.sem_inc(ln.x_ready, 1)
                    ln.dve(nc, dve, v + (NQ + 1), res[:, :, ds(q * QW, QW)], hn[:, :, :])
                    dve.wait_ge(ln.normed, v + (NQ + 1))
                    for m in range(KD):
                        op = nc.vector.tensor_scalar(hn[:, m, :], hn[:, m, :], nvec[:, 0, m:m + 1],
                                                     nvec[:, 1, m:m + 1], ALU.mult, ALU.add)
                    op.then_inc(gained, 1)
                    dve.wait_ge(a_exp, v + 1)
                    nc.vector.tensor_scalar(amat[:, :, :], amat[:, :, :], -1.0, -2e-18, ALU.mult, ALU.min)\
                        .then_inc(a_ready, 1)
                    dve.wait_ge(xin_summed, v + 1)
                    for back in range(DC):
                        if back:
                            dve.wait_ge(tap, v * (DC - 1) + back)
                        for c in range(CT):
                            for b in range(2):
                                src = PS[:, 2 * c + b, 0:HW].rearrange("p (b t) -> p b t", t=T)
                                dst = xs[:, c, b * HW:(b + 1) * HW].rearrange("p (b t) -> p b t", t=T)
                                w = cvec[:, c, DC - 1 - back:DC - back]
                                if back == 0:
                                    op = nc.vector.tensor_scalar(dst, src, w, cvec[:, c, DC:DC + 1],
                                                                 ALU.mult, ALU.add)
                                else:
                                    op = nc.vector.scalar_tensor_tensor(
                                        out=dst[:, :, back:T], in0=src[:, :, 0:T - back], scalar=w,
                                        in1=dst[:, :, back:T], op0=ALU.mult, op1=ALU.add)
                        op.then_inc(tap if back < DC - 1 else conv_done, 1)
                    dve.wait_ge(low_ready, v + 1)
                    nc.vector.tensor_copy(bcp[:, :], bcf[:, :]).then_inc(split1, 1)
                    dve.wait_ge(split1, v + 1)
                    nc.vector.tensor_tensor(bcr[:, :], bcf[:, :], bcp[:, :], ALU.subtract).then_inc(split2, 1)
                    dve.wait_ge(split2, v + 1)
                    nc.vector.tensor_copy(mid[:, :], bcr[:, :]).then_inc(split3, 1)
                    dve.wait_ge(split3, v + 1)
                    nc.vector.tensor_copy(bcp[32:64, :], mid[32:64, :])
                    nc.vector.tensor_tensor(bcp[64:96, :], bcr[64:96, :], mid[64:96, :], ALU.subtract)\
                        .then_inc(bcp_ready, 1)
                    dve.wait_ge(dt_log, v + 1)
                    nc.vector.scalar_tensor_tensor(
                        out=dt[:, :, :].rearrange("p c t -> p (c t)"), in0=dt[:, :, :].rearrange("p c t -> p (c t)"),
                        scalar=0.0, in1=sp[:, :, :].rearrange("p c t -> p (c t)"), op0=ALU.max, op1=ALU.add)\
                        .then_inc(dt_ready, 1)
                    dve.wait_ge(dt_ready, v + 1)
                    nc.vector.tensor_tensor(us[:, :, :], dt[:, :, :], xs[:, :, :], ALU.mult).then_inc(us_ready, 1)
                    dve.wait_ge(us_ready, v + 1)
                    nc.vector.memset(dt[:, :, :].rearrange("p c (b t) -> p (c b) t", t=T)[:, :, 0:1], RESTART)\
                        .then_inc(restart, 1)
                    with dve.Fori(0, DS // 2) as j:
                        for e in range(2):
                            n = v * DS + j * 2 + e
                            dve.wait_ge(c_summed, n + 1)
                            nc.vector.tensor_copy(two(cb[:, ds(j * 2 + e, 1), :].rearrange("p a t -> p (a t)")),
                                                  PS[:, 4 + 2 * e:6 + 2 * e, 0:HW]).then_inc(c_ready, 1)
                    dve.wait_ge(b_ready, v * DS + (DS + 2))
                    dve.wait_ge(us_ready, v + 1)
                    nc.vector.sem_inc(entered[1], 1)
                    def finish(c):
                        dve.wait_ge(reduced, (v * CT + c) * SP2 + (SP2 + 2))
                        nc.vector.scalar_tensor_tensor(
                            out=two(xs[:, c, :]), in0=two(xs[:, c, :]), scalar=cvec[:, c, DC + 2:DC + 3],
                            in1=PS[:, 6:8, 0:HW], op0=ALU.mult, op1=ALU.add).then_inc(y_taken, 1)

                    for c in range(CT):
                        vc = v * CT + c
                        u0 = vc * SP2
                        if c:
                            dve.wait_ge(dbx_ready, u0)
                        nc.vector.tensor_copy(u_ps, us[:, c, :]).then_inc(u_ready, 1)
                        dve.wait_ge(u_ready, vc + 1)

                        def inject(n):
                            dve.wait_ge(scanned, u0 + (n + 1))
                            nc.vector.tensor_tensor(dbx[n % 2].rearrange("p (a t) -> p a t", t=QW),
                                                    bcast(u_ps, 1, [128, 2, QW]), bb[:, 2 * n:2 * n + 2, :],
                                                    ALU.mult).then_inc(dbx_ready, 1)

                        inject(0)
                        for n in range(SP2):
                            if n + 1 < SP2:
                                inject(n + 1)
                            dve.wait_ge(da_ready, u0 + (n + 1))
                            dve.wait_ge(dbx_ready, u0 + (n + 1))
                            dve.wait_ge(weighted, u0 + (n + 1))
                            nc.vector.tensor_tensor_scan(out=hs[:, n % 2, :], data0=da[:, n % 2, :], data1=dbx[n % 2],
                                                         initial=0.0, op0=ALU.mult, op1=ALU.add).then_inc(scanned, 1)
                            if c and n == 1:
                                finish(c - 1)
                    finish(CT - 1)
                    dve.wait_ge(y_taken, v * CT + (CT + 1))
                    nc.vector.tensor_tensor(xs[:, :, :], xs[:, :, :], sz[:, :, :], ALU.mult).then_inc(gated, 1)
                    dve.wait_ge(out_summed, v + 1)
                    nc.vector.tensor_tensor(
                        ln.split(res[:, :, ds(q * QW, QW)]), ln.split(res[:, :, ds(q * QW, QW)]),
                        PS[0:P, 0:4, 0:HW].rearrange("p (k b) t -> p k b t", b=2), ALU.add).then_inc(res_ready, 1)
                    dve.wait_ge(res_ready, v + 1)
                nc.vector.sem_inc(layer_done, 1)
            dve.wait_ge(loaded, 32)
            with dve.Fori(0, NQ) as q:
                v = q + (NQ + L * NQ + 1)
                nc.vector.sem_inc(ln.x_ready, 1)
                ln.dve(nc, dve, v, res[:, :, ds(q * QW, QW)], hn[:, :, :])
                dve.wait_ge(ln.normed, v)
                for m in range(KD):
                    op = nc.vector.tensor_scalar(hn[:, m, :], hn[:, m, :], fvec[:, 0, m:m + 1], fvec[:, 1, m:m + 1],
                                                 ALU.mult, ALU.add)
                op.then_inc(gained, 1)
                dve.wait_ge(gained, q + (L * NQ + 1))
                nc.vector.tensor_tensor(h[:, :, ds(q * QW, QW)], h[:, :, ds(q * QW, QW)], hn[:, :, :], ALU.add)\
                    .then_inc(h_ready, 1)
                dve.wait_ge(h_ready, q + 1)


def experts(nc, dr, PS, C, h):
    E, EH = 8, 192
    G = E + 1
    TW = 94
    NT = N // TW
    SC = FF // 128
    NU = E * KD + SC
    with ExitStack() as ctx:
        s = Scope(nc, ctx, "moe")
        x = s.sb("x", [P, KD, N])
        xb = s.sb("xb", [P, KD, PAIR])
        wr = s.sb("wr", [P, KD, G])
        wg = s.sb("wg", [P, KD, E * EH])
        wu = s.sb("wu", [P, KD, E * EH])
        wd = s.sb("wd", [P, E * KD, D])
        wsg = s.sb("wsg", [P, KD, FF])
        wsu = s.sb("wsu", [P, KD, FF])
        wsd = s.sb("wsd", [128, SC, D])
        sgb = s.sb("sgb", [TW, 1])
        rank = s.sb("rank", [TW, E])
        pick = s.sb("pick", [G, G * 128])
        lg = s.sb("lg", [TW, NT, G])
        pr = s.sb("pr", [TW, NT, E])
        pr2 = s.sb("pr2", [TW, NT, E])
        c1 = s.sb("c1", [TW, NT, E])
        c2 = s.sb("c2", [TW, NT, E])
        m1 = s.sb("m1", [TW, NT])
        m2 = s.sb("m2", [TW, NT])
        mm_ = s.sb("mm_", [TW, NT])
        al = s.sb("al", [TW, NT])
        gates = s.sb("gates", [TW, NT, G])
        gT = s.sb("gT", [G, N])
        sg = s.sb("sg", [128, 2, PAIR])
        gu = s.sb("gu", [128, 2, PAIR])
        hid = s.sb("hid", [128, 2, PAIR])
        ln = Norm(s, "ln", 1, PAIR, PS[0:P, 0:1, 0:PAIR], PS[0:P, 1:2, 0:PAIR], C.ones, C.eps5)
        small, loaded, routed, logits, kept, shifted, exped, step, al_in, al_exp, gates_ready, turned, gT_ready, \
            gb_ready, gu_summed, silu_ready, gu_ready, hid_ready, down_done, out_summed, h_ready = s.sems(
                "small", "loaded", "routed", "logits", "kept", "shifted", "exped", "step", "al_in", "al_exp",
                "gates_ready", "turned", "gT_ready", "gb_ready", "gu_summed", "silu_ready", "gu_ready", "hid_ready",
                "down_done", "out_summed", "h_ready")
        gate_asked = s.sem("gate_asked")
        smalls = [(wr[:, :, :], "moe_wr"), (rank[:, :], "moe_rank"), (pick[:, :], "moe_pick")]
        bigs = [(wg[:, :, :], "moe_wg"), (wu[:, :, :], "moe_wu"), (wd[:, :, :], "moe_wd"), (wsg[:, :, :], "moe_wsg"),
                (wsu[:, :, :], "moe_wsu"), (wsd[:, :, :], "moe_wsd")]
        NS, NBIG = 16 * (len(smalls) + 1), 16 * len(bigs)
        gcols = [slice(t % 5 * TW, (t % 5 + 1) * TW) for t in range(NT)]
        block = ctx.enter_context(nc.Block())

        @block.sync
        def _(sp):
            sp.dma_start(sgb[:, :], dr["moe_sgb"].partition_broadcast(TW)).then_inc(small, 16)
            for dst, name in smalls:
                sp.dma_start(dst, dr[name]).then_inc(small, 16)
            for dst, name in bigs:
                sp.dma_start(dst, dr[name]).then_inc(loaded, 16)
            sp.wait_ge(loaded, NBIG)

        @block.tensor
        def _(pe):
            pe.wait_ge(small, NS)
            with pe.Fori(0, NPAIR) as i:
                ln.pe(nc, pe, i + 1, lambda k, at, w: h[:, k, ds(i * PAIR + at, w)])
                pe.wait_ge(ln.normed, i + 1)
                for t in range(3):
                    for k in range(KD):
                        mm = nc.tensor.matmul(PS[0:TW, 4, t * G:(t + 1) * G], xb[:, k, t * TW:(t + 1) * TW],
                                              wr[:, k, :], start=k == 0, stop=k == KD - 1)
                mm.then_inc(routed, 1)
            pe.wait_ge(gates_ready, 1)
            for t in range(NT):
                mm = nc.tensor.transpose(PS[0:G, t // 5, gcols[t]], gates[:, t, :], C.ident[0:TW, 0:TW])
            mm.then_inc(turned, 1)
            pe.wait_ge(gT_ready, 1)
            pe.wait_ge(loaded, NBIG)
            pe.wait_ge(kept, NPAIR + 1)
            with pe.Fori(0, NPAIR) as i:
                cols = ds(i * PAIR, PAIR)

                def down(u):
                    if u == 0:
                        pe.wait_ge(h_ready, i + 1)
                    pe.wait_ge(hid_ready, i * NU + (u + 2))
                    for m in range(KD):
                        if u < E * KD:
                            w, hd = wd[:, u, m * P:(m + 1) * P], hid[0:P, u % 2, :]
                        else:
                            w, hd = wsd[:, u - E * KD, m * P:(m + 1) * P], hid[:, u % 2, :]
                        mm = nc.tensor.matmul(PS[0:P, 6 + m, 0:PAIR], w, hd, start=u == 0, stop=u == NU - 1)
                    mm.then_inc(down_done, 1)
                    return mm

                for u in range(NU):
                    g = min(u // KD, E)
                    if u == g * KD:
                        pe.wait_ge(hid_ready, i * NU + (max(0, 2 * g - 2) + 1))
                        nc.tensor.sem_inc(gate_asked, 1)
                        nc.tensor.matmul(PS[:, 4 + g % 2, 0:PAIR], pick[:, g * 128:(g + 1) * 128], gT[:, cols],
                                         start=True, stop=True).then_inc(gb_ready, 1)
                    pe.wait_ge(gu_ready, i * NU + (u + 1))
                    for b, w in enumerate((wg, wu) if u < E * KD else (wsg, wsu)):
                        M = P if u < E * KD else 128
                        at = u * P if u < E * KD else (u - E * KD) * 128
                        for k in range(KD):
                            mm = nc.tensor.matmul(PS[0:M, u % 2 * 2 + b, 0:PAIR], w[:, k, at:at + M], x[:, k, cols],
                                                  start=k == 0, stop=k == KD - 1)
                    mm.then_inc(gu_summed, 1)
                    if u >= 2:
                        down(u - 2)
                down(NU - 2)
                down(NU - 1)

        @block.scalar
        def _(act):
            with act.Fori(0, NPAIR) as i:
                ln.act(nc, act, i + 1)
                act.wait_ge(routed, i + 1)
                nc.scalar.activation(lg[:, ds(i * 3, 3), :], PS[0:TW, 4, 0:3 * G].rearrange("p (t g) -> p t g", g=G),
                                     ACT.Copy).then_inc(logits, 1)
            act.wait_ge(shifted, 1)
            nc.scalar.activation(pr[:, :, :], pr[:, :, :], ACT.Exp).then_inc(exped, 1)
            act.wait_ge(al_in, 1)
            nc.scalar.activation(al[:, :], al[:, :], ACT.Exp, scale=-1.0).then_inc(al_exp, 1)
            act.wait_ge(turned, 1)
            full = NT // 5
            nc.scalar.activation(gT[:, 0:full * 5 * TW].rearrange("p (a t) -> p a t", a=full),
                                 PS[0:G, 0:full, 0:5 * TW], ACT.Copy)
            nc.scalar.activation(gT[:, full * 5 * TW:N], PS[0:G, full, 0:(NT - full * 5) * TW], ACT.Copy)\
                .then_inc(gT_ready, 1)
            with act.Fori(0, NPAIR) as i:
                for u in range(NU):
                    M = P if u < E * KD else 128
                    act.wait_ge(gu_summed, i * NU + (u + 1))
                    act.wait_ge(gu_ready, i * NU + (u + 1))
                    nc.scalar.activation(sg[0:M, u % 2, :], PS[0:M, u % 2 * 2, 0:PAIR], ACT.Silu)\
                        .then_inc(silu_ready, 1)

        @block.gpsimd
        def _(pool):
            with pool.Fori(0, NPAIR) as i:
                pool.wait_ge(ln.normed, i + 1)
                nc.gpsimd.tensor_copy(x[:, :, ds(i * PAIR, PAIR)], xb[:, :, :]).then_inc(kept, 1)

        @block.vector
        def _(dve):
            nc.vector.sem_inc(gu_ready, 2)
            nc.vector.sem_inc(hid_ready, 1)
            nc.vector.sem_inc(down_done, 2)
            nc.vector.sem_inc(h_ready, 1)
            nc.vector.sem_inc(kept, 1)
            with dve.Fori(0, NPAIR) as i:
                nc.vector.sem_inc(ln.x_ready, 1)
                dve.wait_ge(kept, i + 1)
                ln.dve(nc, dve, i + 1, h[:, :, ds(i * PAIR, PAIR)], xb[:, :, :])
            dve.wait_ge(small, NS)
            dve.wait_ge(logits, NPAIR)
            steps = [0]

            def link(op):
                steps[0] += 1
                op.then_inc(step, 1)
                dve.wait_ge(step, steps[0])

            V = nc.vector
            sh = [TW, NT, E]
            rk = bcast(rank[:, :], 1, sh)
            link(V.reduce_max(m1[:, :], lg[:, :, 0:E], AX.X))
            V.tensor_tensor(pr[:, :, :], lg[:, :, 0:E], bcast(m1[:, :], 2, sh), ALU.subtract).then_inc(shifted, 1)
            V.tensor_scalar(al[:, :], lg[:, :, E], sgb[:, 0:1], None, ALU.add).then_inc(al_in, 1)
            dve.wait_ge(exped, 1)
            link(V.reduce_sum(m1[:, :], pr[:, :, :], AX.X))
            link(V.reciprocal(m1[:, :], m1[:, :]))
            link(V.tensor_tensor(pr[:, :, :], pr[:, :, :], bcast(m1[:, :], 2, sh), ALU.mult))
            link(V.reduce_max(m1[:, :], pr[:, :, :], AX.X))
            link(V.tensor_tensor(c1[:, :, :], pr[:, :, :], bcast(m1[:, :], 2, sh), ALU.is_equal))
            link(V.tensor_tensor(c1[:, :, :], c1[:, :, :], rk, ALU.mult))
            link(V.reduce_max(mm_[:, :], c1[:, :, :], AX.X))
            link(V.tensor_tensor(c1[:, :, :], c1[:, :, :], bcast(mm_[:, :], 2, sh), ALU.is_equal))
            link(V.scalar_tensor_tensor(out=pr2[:, :, :], in0=c1[:, :, :], scalar=-2.0, in1=pr[:, :, :],
                                        op0=ALU.mult, op1=ALU.add))
            link(V.reduce_max(m2[:, :], pr2[:, :, :], AX.X))
            link(V.tensor_tensor(c2[:, :, :], pr2[:, :, :], bcast(m2[:, :], 2, sh), ALU.is_equal))
            link(V.tensor_tensor(c2[:, :, :], c2[:, :, :], rk, ALU.mult))
            link(V.reduce_max(mm_[:, :], c2[:, :, :], AX.X))
            link(V.tensor_tensor(c2[:, :, :], c2[:, :, :], bcast(mm_[:, :], 2, sh), ALU.is_equal))
            link(V.tensor_tensor(mm_[:, :], m1[:, :], m2[:, :], ALU.add))
            link(V.reciprocal(mm_[:, :], mm_[:, :]))
            dve.wait_ge(al_exp, 1)
            link(V.tensor_scalar(al[:, :], al[:, :], 1.0, None, ALU.add))
            link(V.reciprocal(gates[:, :, E], al[:, :]))
            link(V.tensor_scalar(al[:, :], gates[:, :, E], -1.0, 1.0, ALU.mult, ALU.add))
            link(V.tensor_tensor(m1[:, :], m1[:, :], mm_[:, :], ALU.mult))
            link(V.tensor_tensor(m2[:, :], m2[:, :], mm_[:, :], ALU.mult))
            link(V.tensor_tensor(c1[:, :, :], c1[:, :, :], bcast(m1[:, :], 2, sh), ALU.mult))
            link(V.tensor_tensor(c2[:, :, :], c2[:, :, :], bcast(m2[:, :], 2, sh), ALU.mult))
            link(V.tensor_tensor(c1[:, :, :], c1[:, :, :], c2[:, :, :], ALU.add))
            V.tensor_tensor(gates[:, :, 0:E], c1[:, :, :], bcast(al[:, :], 2, sh), ALU.mult).then_inc(gates_ready, 1)
            with dve.Fori(0, NPAIR) as i:
                for u in range(NU):
                    M = P if u < E * KD else 128
                    g = min(u // KD, E)
                    U = i * NU + u
                    dve.wait_ge(silu_ready, U + 1)
                    V.tensor_tensor(gu[0:M, u % 2, :], sg[0:M, u % 2, :], PS[0:M, u % 2 * 2 + 1, 0:PAIR], ALU.mult)\
                        .then_inc(gu_ready, 1)
                    dve.wait_ge(gu_ready, U + 3)
                    dve.wait_ge(gb_ready, i * G + (g + 1))
                    dve.wait_ge(down_done, U + 1)
                    V.tensor_tensor(hid[0:M, u % 2, :], gu[0:M, u % 2, :], PS[0:M, 4 + g % 2, 0:PAIR], ALU.mult)\
                        .then_inc(hid_ready, 1)
                dve.wait_ge(down_done, i * NU + (NU + 2))
                V.tensor_tensor(h[:, :, ds(i * PAIR, PAIR)], h[:, :, ds(i * PAIR, PAIR)], PS[0:P, 6:8, 0:PAIR],
                                ALU.add).then_inc(h_ready, 1)
            dve.wait_ge(h_ready, NPAIR + 1)


def attention(nc, dr, PS, C, h):
    TT = 71
    PT = 2 * TT
    STEP = 0.5 * DH ** -0.5
    TILT = STEP * DH ** -0.5
    EG = 8
    SH = 2 * NH
    with ExitStack() as ctx:
        s = Scope(nc, ctx, "att")
        wqk = s.sb("wqk", [P, KD, 2, QC * 128])
        wk = s.sb("wk", [P, KD, D])
        wv = s.sb("wv", [P, KD, QC * 128])
        wo = s.sb("wo", [128, QC, D])
        bo = s.sb("bo", [P, KD])
        mean_sel = s.sb("mean_sel", [128, 2, HP])
        xn = s.sb("xn", [P, KD, PT])
        qk = s.sb("qk", [128, 2, QC, PT])
        qs = s.sb("qs", [128, QC, PT])
        keys = s.sb("keys", [TT, 2, D])
        tilt = s.sb("tilt", [128, 2, NH, 2, DH])
        spread_sel = s.sb("spread_sel", [2 * DH, 4, 128])
        v = s.sb("v", [128, 2, QC * 128])
        wvt = s.sb("wvt", [128, 2, 2, 2, DH, DH])
        ex = s.sb("ex", [TT, 3, 2, PT])
        mx = s.sb("mx", [TT, 3, 2])
        eT = s.sb("eT", [128, 3, 2, PT])
        inv = s.sb("inv", [2 * DH, 2, T])
        rb = s.sb("rb", [128, 2, 2, T])
        rat = s.sb("rat", [128, 2, 2, T])
        dif = s.sb("dif", [128, 2, T])
        absd = s.sb("absd", [128, 2, T])
        acc = s.sb("acc", [128, NH, 2])
        oT = s.sb("oT", [128, QC, PT])
        ln = Norm(s, "ln", 1, T, PS[0:P, 2:3, 0:T], PS[0:P, 3:4, 0:T], C.ones, C.eps5)
        loaded, padded, qk_summed, qk_ready, kv_summed, keys_ready, tilt_ready, v_ready, scored, maxed, shifted, exped, e_ready, \
            turned, eT_ready, wvt_ready, weights_summed, sums_ready, inverted, spread, rb_ready, ratio, differed, \
            acc_ready, w_summed, qs_ready, rowinv, mixed, oT_ready, projected, h_ready = s.sems(
                "loaded", "padded", "qk_summed", "qk_ready", "kv_summed", "keys_ready", "tilt_ready", "v_ready", "scored", "maxed",
                "shifted", "exped", "e_ready", "turned", "eT_ready", "wvt_ready", "weights_summed", "sums_ready",
                "inverted", "spread", "rb_ready", "ratio", "differed", "acc_ready", "w_summed", "qs_ready", "rowinv", "mixed", "oT_ready",
                "projected", "h_ready")
        loads = [(wqk[:, :, :, :], "att_wqk"), (wk[:, :, :], "att_wk"), (wv[:, :, :], "att_wv"), (wo[:, :, :], "att_wo"),
                 (bo[:, :], "att_bo"), (mean_sel[:, :, :], "att_sel"), (spread_sel[:, :, :], "att_spread")]
        NLD, PADS = 16 * len(loads), 6
        acc_j = acc[:, :, :].rearrange("p (c j) g -> p j c g", j=4)
        block = ctx.enter_context(nc.Block())

        @block.sync
        def _(sp):
            for dst, name in loads:
                sp.dma_start(dst, dr[name]).then_inc(loaded, 16)
            sp.wait_ge(loaded, NLD)

        @block.tensor
        def _(pe):
            pe.wait_ge(loaded, NLD)
            pe.wait_ge(padded, PADS)
            with pe.Fori(0, B) as i:
                ln.pe(nc, pe, i + 1, lambda k, at, w: h[:, k, ds(i * T + at, w)])
                pe.wait_ge(ln.normed, i + 1)
                for a in range(2):
                    for c in range(QC):
                        for k in range(KD):
                            mm = nc.tensor.matmul(PS[:, a, c * PT:(c + 1) * PT], wqk[:, k, a, c * 128:(c + 1) * 128],
                                                  xn[:, k, :], start=k == 0, stop=k == KD - 1)
                mm.then_inc(qk_summed, 1)
                for bank, w, n in ((4, wk, D), (6, wv, QC * 128)):
                    for t in range(2):
                        for k in range(KD):
                            mm = nc.tensor.matmul(PS[0:TT, bank + t, 0:n], xn[:, k, t * TT:(t + 1) * TT], w[:, k, :],
                                                  start=k == 0, stop=k == KD - 1)
                mm.then_inc(kv_summed, 1)
                pe.wait_ge(qk_ready, i + 1)

                def score(p, n):
                    H = i * SH + (p * NH + n)
                    c, r = n // 4, slice(HP * (n % 4), HP * (n % 4 + 1))
                    pe.wait_ge(shifted, H + 1)
                    for t in range(2):
                        q = qk[r, 0, c, t * TT:(t + 1) * TT] if p == 0 else qs[r, c, t * TT:(t + 1) * TT]
                        mm = nc.tensor.matmul(PS[0:TT, n % 2, t * PT:t * PT + T], q, qk[r, 1, c, 0:T],
                                              start=True, stop=True)
                    mm.then_inc(scored, 1)

                def turn(p, n):
                    H = i * SH + (p * NH + n)
                    pe.wait_ge(e_ready, H + 1)
                    pe.wait_ge(eT_ready, H + 1)
                    if p == 0 and n >= 2:
                        pe.wait_ge(inverted, i * NH + (n - 1))
                    for t in range(2):
                        for kt in range(2):
                            at = kt * PT + t * TT
                            mm = nc.tensor.transpose(PS[0:TT, 2 + n % 2, at:at + TT],
                                                     ex[:, n % 3, t, kt * TT:(kt + 1) * TT], C.ident[0:TT, 0:TT])
                    mm.then_inc(turned, 1)

                def spread_of(m):
                    pe.wait_ge(inverted, i * NH + (m + 1))
                    if m == 0:
                        pe.wait_ge(v_ready, i + 1)
                    for g in range(2):
                        pe.wait_ge(rb_ready, (i * NH + m) * 2 + (g + 1))
                        for sign in range(2):
                            mm = nc.tensor.matmul(PS[:, 6 + g, sign * PT:sign * PT + T],
                                                  spread_sel[:, 2 * g + sign, :], inv[:, m % 2, :],
                                                  start=True, stop=True)
                        mm.then_inc(spread, 1)

                def weights_of(m):
                    pe.wait_ge(eT_ready, i * SH + (m + 3))
                    pe.wait_ge(tilt_ready, i + 1)
                    for kt in range(2):
                        mm = nc.tensor.matmul(PS[0:2 * DH, 2 + m % 2, 2 * PT:2 * PT + T],
                                              tilt[:, kt, m, :, :].rearrange("p s e -> p (s e)"),
                                              eT[:, m % 3, kt, 0:T], start=kt == 0, stop=kt == 1)
                    mm.then_inc(weights_summed, 1)

                def values_of(m):
                    pe.wait_ge(wvt_ready, i * NH + (m + 1))
                    for g in range(2):
                        pe.wait_ge(ratio, (i * NH + m) * 2 + (g + 1))
                        for sign in range(2):
                            for kt in range(2):
                                mm = nc.tensor.matmul(
                                    PS[:, 4 + g, sign * PT:sign * PT + T],
                                    wvt[:, m % 2, kt, sign, g * EG:(g + 1) * EG, :].rearrange("p e d -> p (e d)"),
                                    eT[:, m % 3, kt, 0:T], start=kt == 0, stop=kt == 1)
                        mm.then_inc(sums_ready, 1)

                for n in range(NH + 3):
                    if n < NH:
                        score(0, n)
                    if 1 <= n <= NH:
                        turn(0, n - 1)
                    if n >= 3:
                        spread_of(n - 3)
                    if 2 <= n <= NH + 1:
                        weights_of(n - 2)
                    if n >= 3:
                        values_of(n - 3)
                pe.wait_ge(acc_ready, (i + 1) * 2 * NH)
                for j in range(4):
                    for g in range(2):
                        mm = nc.tensor.matmul(PS[HP * j:HP * (j + 1), 4, 0:QC], mean_sel[:, g, :], acc_j[:, j, :, g],
                                              start=g == 0, stop=g == 1)
                mm.then_inc(w_summed, 1)
                pe.wait_ge(qs_ready, i + 1)
                for n in range(NH + 3):
                    if n < NH:
                        score(1, n)
                    if 2 <= n <= NH + 1:
                        turn(1, n - 2)
                    if n >= 3:
                        m = n - 3
                        pe.wait_ge(eT_ready, i * SH + (NH + m + 3))
                        for kt in range(2):
                            mm = nc.tensor.matmul(PS[HP * (m % 4):HP * (m % 4 + 1), 5, m // 4 * PT:(m // 4 + 1) * PT],
                                                  v[:, kt, m * HP:(m + 1) * HP], eT[:, m % 3, kt, :],
                                                  start=kt == 0, stop=kt == 1)
                        mm.then_inc(mixed, 1)
                pe.wait_ge(oT_ready, i + 1)
                for m in range(KD):
                    for c in range(QC):
                        mm = nc.tensor.matmul(PS[0:P, 6, m * PT:m * PT + T], wo[:, c, m * P:(m + 1) * P],
                                              oT[:, c, 0:T], start=c == 0, stop=c == QC - 1)
                mm.then_inc(projected, 1)

        @block.scalar
        def _(act):
            with act.Fori(0, B) as i:
                ln.act(nc, act, i + 1)
                act.wait_ge(qk_summed, i + 1)
                nc.scalar.activation(qk[:, :, :, :].rearrange("p a c t -> p a (c t)"), PS[:, 0:2, 0:QC * PT], ACT.Copy)\
                    .then_inc(qk_ready, 1)
                act.wait_ge(kv_summed, i + 1)
                nc.scalar.activation(keys[:, :, :], PS[0:TT, 4:6, 0:D], ACT.Copy).then_inc(keys_ready, 1)
                act.wait_ge(keys_ready, i + 1)

                for sign in range(2):
                    op = nc.scalar.activation(tilt[0:TT, :, :, sign, :],
                                              keys[:, :, :].rearrange("p a (n e) -> p a n e", e=DH), ACT.Exp,
                                              scale=TILT * (1 - 2 * sign))
                op.then_inc(tilt_ready, 1)

                def exp_of(p, n):
                    H = i * SH + (p * NH + n)
                    act.wait_ge(shifted, H + 3)
                    if p == 0:
                        nc.scalar.activation(ex[:, n % 3, :, 0:T], ex[:, n % 3, :, 0:T], ACT.Exp, scale=DH ** -0.5)\
                            .then_inc(e_ready, 1)
                    else:
                        for t in range(2):
                            op = nc.scalar.activation(ex[:, n % 3, t, 0:T], ex[:, n % 3, t, 0:T], ACT.Exp,
                                                      scale=DH ** -0.5, accum_out=mx[:, n % 3, t:t + 1])
                        op.then_inc(exped, 1)

                def keep_turned(p, n):
                    H = i * SH + (p * NH + n)
                    act.wait_ge(turned, H + 1)
                    if p == 0:
                        act.wait_ge(sums_ready, (i * NH + n) * 2 + 2)
                    elif n < 3:
                        act.wait_ge(sums_ready, (i + 1) * 2 * NH + 6)
                    else:
                        act.wait_ge(mixed, i * NH + (n - 2))
                    nc.scalar.activation(eT[0:TT, n % 3, :, :].rearrange("p a t -> p (a t)"),
                                         PS[0:TT, 2 + n % 2, 0:2 * PT], ACT.Copy).then_inc(eT_ready, 1)

                for n in range(NH + 4):
                    if 1 <= n <= NH:
                        keep_turned(0, n - 1)
                    if 3 <= n <= NH + 2:
                        for g in range(2):
                            M = (i * NH + (n - 3)) * 2 + g
                            act.wait_ge(spread, M + 1)
                            act.wait_ge(ratio, M + 1)
                            nc.scalar.activation(rb[:, g, :, :], PS[:, 6 + g, 0:2 * PT].rearrange(
                                "p (a t) -> p a t", t=PT)[:, :, 0:T], ACT.Copy).then_inc(rb_ready, 1)
                    if n < NH:
                        exp_of(0, n)
                    if n >= 4:
                        m = n - 4
                        for g in range(2):
                            act.wait_ge(differed, (i * NH + m) * 2 + (g + 1))
                            nc.scalar.activation(absd[:, g, :], dif[:, g, :], ACT.Abs, accum_out=acc[:, m, g:g + 1])\
                                .then_inc(acc_ready, 1)
                for n in range(NH + 2):
                    if n < NH:
                        exp_of(1, n)
                    if n >= 2:
                        keep_turned(1, n - 2)
                act.wait_ge(mixed, (i + 1) * NH)
                nc.scalar.activation(oT[:, :, :].rearrange("p c t -> p (c t)"), PS[:, 5, 0:QC * PT], ACT.Copy)\
                    .then_inc(oT_ready, 1)

        @block.gpsimd
        def _(pool):
            pool.memset(xn[:, :, T:PT], 0.0).then_inc(padded, 1)
            pool.memset(ex[:, :, :, T:PT], 0.0).then_inc(padded, 1)
            pool.memset(tilt[:, :, :, :, :], 0.0).then_inc(padded, 1)
            pool.memset(wvt[:, :, :, :, :, :], 0.0).then_inc(padded, 1)
            pool.memset(v[:, :, :], 0.0).then_inc(padded, 1)
            pool.memset(eT[:, :, :, :], 0.0).then_inc(padded, 1)
            pool.wait_ge(padded, PADS)
            with pool.Fori(0, B) as i:
                pool.wait_ge(v_ready, i + 1)
                pool.wait_ge(tilt_ready, i + 1)
                for n in range(NH):
                    pool.wait_ge(sums_ready, (i * NH + n) * 2 + 4)
                    for kt in range(2):
                        op = nc.gpsimd.tensor_tensor(
                            wvt[0:TT, n % 2, kt, :, :, :].rearrange("p s e d -> p (s e) d"),
                            bcast(tilt[0:TT, kt, n, :, :].rearrange("p s e -> p (s e)"), 2, [TT, 2 * DH, DH]),
                            bcast(v[0:TT, kt, n * HP:n * HP + DH], 1, [TT, 2 * DH, DH]), ALU.mult)
                    op.then_inc(wvt_ready, 1)

        @block.vector
        def _(dve):
            V = nc.vector
            V.sem_inc(shifted, 2)
            V.sem_inc(eT_ready, 2)
            V.sem_inc(ratio, 2)
            V.sem_inc(rb_ready, 2)
            V.sem_inc(sums_ready, 6)
            with dve.Fori(0, B) as i:
                V.sem_inc(ln.x_ready, 1)
                ln.dve(nc, dve, i + 1, h[:, :, ds(i * T, T)], xn[:, :, 0:T])
                dve.wait_ge(kv_summed, i + 1)
                V.tensor_copy(v[0:TT, :, :], PS[0:TT, 6:8, 0:QC * 128]).then_inc(v_ready, 1)

                def shift(p, n):
                    H = i * SH + (p * NH + n)
                    dve.wait_ge(scored, H + 1)
                    sc = PS[0:TT, n % 2, 0:2 * PT].rearrange("p (a t) -> p a t", t=PT)[:, :, 0:T]
                    V.reduce_max(mx[:, n % 3, :], sc, AX.X).then_inc(maxed, 1)
                    dve.wait_ge(maxed, H + 1)
                    if p == 1 or n >= 3:
                        dve.wait_ge(turned, H - 2)
                    V.tensor_tensor(ex[:, n % 3, :, 0:T], sc, bcast(mx[:, n % 3, :], 2, [TT, 2, T]), ALU.subtract)\
                        .then_inc(shifted, 1)

                for n in range(NH + 3):
                    if n < NH:
                        shift(0, n)
                    if 2 <= n <= NH + 1:
                        m = n - 2
                        dve.wait_ge(weights_summed, i * NH + (m + 1))
                        V.reciprocal(inv[:, m % 2, :], PS[0:2 * DH, 2 + m % 2, 2 * PT:2 * PT + T]).then_inc(inverted, 1)
                    if n >= 3:
                        m = n - 3
                        M = (i * NH + m) * 2
                        for g in range(2):
                            dve.wait_ge(sums_ready, M + (g + 7))
                            dve.wait_ge(rb_ready, M + (g + 3))
                            if m >= 1:
                                dve.wait_ge(differed, M + (g - 1))
                            V.tensor_tensor(rat[:, g, :, :], rb[:, g, :, :], PS[:, 4 + g, 0:2 * PT].rearrange(
                                "p (a t) -> p a t", t=PT)[:, :, 0:T], ALU.mult).then_inc(ratio, 1)
                        for g in range(2):
                            dve.wait_ge(ratio, M + (g + 3))
                            if m >= 1:
                                dve.wait_ge(acc_ready, M + (g - 1))
                            V.tensor_tensor(dif[:, g, :], rat[:, g, 0, :], rat[:, g, 1, :], ALU.subtract)\
                                .then_inc(differed, 1)
                dve.wait_ge(w_summed, i + 1)
                V.tensor_tensor(qs[:, :, :], qk[:, 0, :, :], bcast(PS[:, 4, 0:QC], 2, [128, QC, PT]), ALU.mult)\
                    .then_inc(qs_ready, 1)
                for n in range(NH + 1):
                    if n < NH:
                        shift(1, n)
                    if n >= 1:
                        m = n - 1
                        dve.wait_ge(exped, i * NH + (m + 1))
                        V.reciprocal(mx[:, m % 3, :], mx[:, m % 3, :]).then_inc(rowinv, 1)
                        dve.wait_ge(rowinv, i * NH + (m + 1))
                        V.tensor_tensor(ex[:, m % 3, :, 0:T], ex[:, m % 3, :, 0:T],
                                        bcast(mx[:, m % 3, :], 2, [TT, 2, T]), ALU.mult).then_inc(e_ready, 1)
                dve.wait_ge(projected, i + 1)
                for m in range(KD):
                    op = V.scalar_tensor_tensor(out=h[:, m, ds(i * T, T)], in0=PS[0:P, 6, m * PT:m * PT + T],
                                                scalar=bo[:, m:m + 1], in1=h[:, m, ds(i * T, T)],
                                                op0=ALU.add, op1=ALU.add)
                op.then_inc(h_ready, 1)
                dve.wait_ge(h_ready, i + 1)


def switch(nc, dr, PS, C, h):
    E, CAP = 16, 64
    G = E + 2
    TW = 94
    NT = N // TW
    BLOCKS = [(0, 0), (0, 1), (1, 1), (1, 2), (2, 2)]
    with ExitStack() as ctx:
        s = Scope(nc, ctx, "sw")
        nrm = s.sb("nrm", [P, KD, N])
        acc = s.sb("acc", [P, KD, N])
        xb = s.sb("xb", [P, KD, PAIR])
        nb = s.sb("nb", [P, KD, PAIR])
        lnw = s.sb("lnw", [P, KD])
        wr = s.sb("wr", [P, KD, E])
        wi = s.sb("wi", [P, 2, KD, FF])
        wo = s.sb("wo", [128, 2, FC, D])
        rank = s.sb("rank", [TW, E])
        upto = s.sb("upto", [TW, len(BLOCKS), TW])
        pick = s.sb("pick", [G, G * 128])
        picked = s.sb("picked", [G, 2, 128])
        lg = s.sb("lg", [TW, NT, E])
        oh = s.sb("oh", [TW, NT, E])
        m1 = s.sb("m1", [TW, NT])
        m2 = s.sb("m2", [TW, NT])
        gates = s.sb("gates", [TW, NT, G])
        gT = s.sb("gT", [G, N])
        xk = s.sb("xk", [P, 2, KD, PAIR])
        hid = s.sb("hid", [128, 2, FC, PAIR])
        eps6 = s.sb("eps6", [P, 1])
        ln = Norm(s, "ln", 1, PAIR, PS[0:P, 0:1, 0:PAIR], PS[0:P, 1:2, 0:PAIR], C.ones, C.eps5)
        rms = Norm(s, "rms", 1, PAIR, None, PS[0:P, 2:3, 0:PAIR], C.ones, eps6, center=False)
        small, eps_ready, summed, scaled, weighted, routed, logits, kept, shifted, exped, step, oh_ready, counted, \
            gates_ready, turned, gT_ready, picked_ready, kb_ready, xk_ready, hid_summed, hid_ready, out_summed, \
            acc_ready, e_done, p_ready, next_ready, h_ready, entered = s.sems(
                "small", "eps_ready", "summed", "scaled", "weighted", "routed", "logits", "kept", "shifted", "exped",
                "step", "oh_ready", "counted", "gates_ready", "turned", "gT_ready", "picked_ready", "kb_ready",
                "xk_ready", "hid_summed", "hid_ready", "out_summed", "acc_ready", "e_done", "p_ready", "next_ready",
                "h_ready", "entered")
        wloaded = s.sems("wloaded0", "wloaded1")
        smalls = [(lnw[:, :], "sw_lnw"), (wr[:, :, :], "sw_wr"), (rank[:, :], "sw_rank"), (upto[:, :, :], "sw_upto"),
                  (pick[:, :], "sw_pick")]
        NS = 16 * len(smalls)
        gcols = [slice(t % 5 * TW, (t % 5 + 1) * TW) for t in range(NT)]
        full = NT // 5
        block = ctx.enter_context(nc.Block())

        @block.sync
        def _(sp):
            for dst, name in smalls:
                sp.dma_start(dst, dr[name]).then_inc(small, 16)
            with sp.Fori(0, E // 2) as ee:
                for b in range(2):
                    sp.wait_ge(e_done, ee * 2 + (b + 1))
                    sp.dma_start(wi[:, b, :, :], dr["sw_wi"][ds(ee * 2 + b, 1)].rearrange("a p k f -> (a p) k f"))\
                        .then_inc(wloaded[b], 16)
                    sp.dma_start(wo[:, b, :, :], dr["sw_wo"][ds(ee * 2 + b, 1)].rearrange("a p k f -> (a p) k f"))\
                        .then_inc(wloaded[b], 16)
            for b in range(2):
                sp.wait_ge(wloaded[b], E * 16)

        @block.tensor
        def _(pe):
            pe.wait_ge(small, NS)
            with pe.Fori(0, NPAIR) as i:
                ln.pe(nc, pe, i + 1, lambda k, at, w: h[:, k, ds(i * PAIR + at, w)])
                rms.pe(nc, pe, i + 1)
                pe.wait_ge(weighted, i + 1)
                for t in range(3):
                    for k in range(KD):
                        mm = nc.tensor.matmul(PS[0:TW, 4, t * E:(t + 1) * E], nb[:, k, t * TW:(t + 1) * TW],
                                              wr[:, k, :], start=k == 0, stop=k == KD - 1)
                mm.then_inc(routed, 1)
            pe.wait_ge(oh_ready, 1)
            ohp = oh[:, :, :].rearrange("p (i t) e -> p t i e", t=3)
            for t in range(3):
                srcs = [(n, a) for n, (a, b) in enumerate(BLOCKS) if b == t]
                for n, a in srcs:
                    mm = nc.tensor.matmul(PS[0:TW, 5 + t, 0:NPAIR * E], upto[:, n, :], ohp[:, a, :, :],
                                          start=n == srcs[0][0], stop=n == srcs[-1][0])
            mm.then_inc(counted, 1)
            pe.wait_ge(gates_ready, 1)
            for t in range(NT):
                mm = nc.tensor.transpose(PS[0:G, t // 5, gcols[t]], gates[:, t, :], C.ident[0:TW, 0:TW])
            mm.then_inc(turned, 1)
            pe.wait_ge(gT_ready, 1)
            pe.wait_ge(kept, NPAIR + 1)
            with pe.Fori(0, E // 2) as ee:
                for b in range(2):
                    pe.wait_ge(wloaded[b], ee * 32 + 32)
                    pe.wait_ge(picked_ready, ee * 2 + (b + 1))
                    nc.tensor.sem_inc(entered, 1)
                    with pe.Fori(0, NPAIR // 2) as ii:
                        for o in range(2):
                            n = (ee * 2 + b) * NPAIR + ii * 2 + o
                            pe.wait_ge(xk_ready, n + 1)
                            nc.tensor.sem_inc(entered, 1)
                            nc.tensor.matmul(PS[:, o, 0:PAIR], picked[:, b, :], gT[:, ds(ii * 2 * PAIR + o * PAIR, PAIR)],
                                             start=True, stop=True).then_inc(kb_ready, 1)
                            pe.wait_ge(xk_ready, n + 3)
                            for j in range(FC):
                                pe.wait_ge(hid_ready, n * FC + (j + 1))
                                for k in range(KD):
                                    mm = nc.tensor.matmul(PS[:, 2 + j % 2, 0:PAIR], wi[:, b, k, j * 128:(j + 1) * 128],
                                                          xk[:, o, k, :], start=k == 0, stop=k == KD - 1)
                                mm.then_inc(hid_summed, 1)
                            pe.wait_ge(acc_ready, n + 1)
                            pe.wait_ge(hid_ready, n * FC + (FC + 2))
                            for m in range(KD):
                                for j in range(FC):
                                    mm = nc.tensor.matmul(PS[0:P, 4 + 2 * o + m, 0:PAIR], wo[:, b, j, m * P:(m + 1) * P],
                                                          hid[:, o, j, :], start=j == 0, stop=j == FC - 1)
                            mm.then_inc(out_summed, 1)
                    nc.tensor.sem_inc(entered, 1)
            pe.wait_ge(acc_ready, E * NPAIR + 2)
            with pe.Fori(0, NPAIR) as i:
                pe.wait_ge(h_ready, i + 1)
                nc.tensor.sem_inc(entered, 1)
                for g in range(2):
                    mm = nc.tensor.matmul(PS[:, g, 0:PAIR], pick[:, (E + g) * 128:(E + g + 1) * 128],
                                          gT[:, ds(i * PAIR, PAIR)], start=True, stop=True)
                mm.then_inc(p_ready, 1)

        @block.scalar
        def _(act):
            act.wait_ge(eps_ready, 1)
            with act.Fori(0, NPAIR) as i:
                ln.act(nc, act, i + 1)
                rms.act(nc, act, i + 1, xb[:, :, :])
                act.wait_ge(routed, i + 1)
                nc.scalar.activation(lg[:, ds(i * 3, 3), :], PS[0:TW, 4, 0:3 * E].rearrange("p (t g) -> p t g", g=E),
                                     ACT.Copy).then_inc(logits, 1)
            act.wait_ge(shifted, 1)
            nc.scalar.activation(lg[:, :, :], lg[:, :, :], ACT.Exp).then_inc(exped, 1)
            act.wait_ge(turned, 1)
            nc.scalar.activation(gT[:, 0:full * 5 * TW].rearrange("p (a t) -> p a t", a=full),
                                 PS[0:G, 0:full, 0:5 * TW], ACT.Copy)
            nc.scalar.activation(gT[:, full * 5 * TW:N], PS[0:G, full, 0:(NT - full * 5) * TW], ACT.Copy)\
                .then_inc(gT_ready, 1)
            with act.Fori(0, E * NPAIR // 2) as ii:
                for o in range(2):
                    n = ii * 2 + o
                    act.wait_ge(out_summed, n + 1)
                    for j in range(FC):
                        act.wait_ge(hid_summed, n * FC + (j + 1))
                        nc.scalar.activation(hid[:, o, j, :], PS[:, 2 + j % 2, 0:PAIR], ACT.Relu).then_inc(hid_ready, 1)

        @block.gpsimd
        def _(pool):
            with pool.Fori(0, NPAIR) as i:
                pool.wait_ge(weighted, i + 1)
                nc.gpsimd.tensor_copy(nrm[:, :, ds(i * PAIR, PAIR)], nb[:, :, :]).then_inc(kept, 1)

        @block.vector
        def _(dve):
            V = nc.vector
            V.memset(eps6[:, :], 1e-6).then_inc(eps_ready, 1)
            V.memset(acc[:, :, :], 0.0).then_inc(eps_ready, 1)
            V.sem_inc(kept, 1)
            V.sem_inc(e_done, 2)
            V.sem_inc(xk_ready, 2)
            V.sem_inc(hid_ready, 2)
            V.sem_inc(acc_ready, 2)
            V.sem_inc(out_summed, 2)
            V.sem_inc(h_ready, 1)
            dve.wait_ge(small, NS)
            with dve.Fori(0, NPAIR) as i:
                V.sem_inc(ln.x_ready, 1)
                cols = ds(i * PAIR, PAIR)
                ln.dve(nc, dve, i + 1, h[:, :, cols], xb[:, :, :])
                dve.wait_ge(ln.normed, i + 1)
                V.sem_inc(rms.x_ready, 1)
                V.tensor_tensor(h[:, :, cols], h[:, :, cols], xb[:, :, :], ALU.add).then_inc(summed, 1)
                dve.wait_ge(kept, i + 1)
                rms.dve(nc, dve, i + 1, xb[:, :, :], nb[:, :, :])
                dve.wait_ge(rms.normed, i + 1)
                for m in range(KD):
                    op = V.tensor_scalar(nb[:, m, :], nb[:, m, :], lnw[:, m:m + 1], None, ALU.mult)
                op.then_inc(weighted, 1)
            dve.wait_ge(logits, NPAIR)
            dve.wait_ge(summed, NPAIR)
            steps = [0]

            def link(op):
                steps[0] += 1
                op.then_inc(step, 1)
                dve.wait_ge(step, steps[0])

            sh = [TW, NT, E]
            link(V.reduce_max(m1[:, :], lg[:, :, :], AX.X))
            V.tensor_tensor(lg[:, :, :], lg[:, :, :], bcast(m1[:, :], 2, sh), ALU.subtract).then_inc(shifted, 1)
            dve.wait_ge(exped, 1)
            link(V.reduce_sum(m1[:, :], lg[:, :, :], AX.X))
            link(V.reciprocal(m1[:, :], m1[:, :]))
            link(V.tensor_tensor(lg[:, :, :], lg[:, :, :], bcast(m1[:, :], 2, sh), ALU.mult))
            link(V.reduce_max(m1[:, :], lg[:, :, :], AX.X))
            link(V.tensor_tensor(oh[:, :, :], lg[:, :, :], bcast(m1[:, :], 2, sh), ALU.is_equal))
            link(V.tensor_tensor(oh[:, :, :], oh[:, :, :], bcast(rank[:, :], 1, sh), ALU.mult))
            link(V.reduce_max(m2[:, :], oh[:, :, :], AX.X))
            V.tensor_tensor(oh[:, :, :], oh[:, :, :], bcast(m2[:, :], 2, sh), ALU.is_equal).then_inc(oh_ready, 1)
            dve.wait_ge(counted, 1)
            ohp = oh[:, :, :].rearrange("p (i t) e -> p t i e", t=3)
            gp = gates[:, :, :].rearrange("p (i t) e -> p t i e", t=3)
            for t in range(3):
                link(V.scalar_tensor_tensor(out=gp[:, t, :, 0:E],
                                            in0=PS[0:TW, 5 + t, 0:NPAIR * E].rearrange("p (i e) -> p i e", e=E),
                                            scalar=float(CAP), in1=ohp[:, t, :, :], op0=ALU.is_le, op1=ALU.mult))
            link(V.reduce_sum(m2[:, :], gates[:, :, 0:E], AX.X))
            link(V.tensor_scalar(m2[:, :], m2[:, :], -1.0, 1.0, ALU.mult, ALU.add))
            V.tensor_copy(gates[:, :, E], m1[:, :])
            V.tensor_tensor(gates[:, :, E + 1], m1[:, :], m2[:, :], ALU.mult).then_inc(gates_ready, 1)
            dve.wait_ge(gT_ready, 1)
            dve.wait_ge(eps_ready, 2)
            with dve.Fori(0, E // 2) as ee:
                for b in range(2):
                    e = ee * 2 + b
                    dve.wait_ge(e_done, e + 1)
                    V.tensor_copy(picked[:, b, :], pick[:, ds(ee * 256 + b * 128, 128)]).then_inc(picked_ready, 1)
                    with dve.Fori(0, NPAIR // 2) as ii:
                        for o in range(2):
                            n = e * NPAIR + ii * 2 + o
                            cols = ds(ii * 2 * PAIR + o * PAIR, PAIR)
                            dve.wait_ge(kb_ready, n + 1)
                            V.tensor_tensor(xk[:, o, :, :], nrm[:, :, cols], bcast(PS[0:P, o, 0:PAIR], 1, [P, KD, PAIR]),
                                            ALU.mult).then_inc(xk_ready, 1)
                            dve.wait_ge(out_summed, n + 3)
                            V.tensor_tensor(acc[:, :, cols], acc[:, :, cols], PS[0:P, 4 + 2 * o:6 + 2 * o, 0:PAIR],
                                            ALU.add).then_inc(acc_ready, 1)
                            dve.wait_ge(acc_ready, n + 3)
                    V.sem_inc(e_done, 1)
            with dve.Fori(0, NPAIR) as i:
                cols = ds(i * PAIR, PAIR)
                dve.wait_ge(p_ready, i + 1)
                V.tensor_tensor(acc[:, :, cols], acc[:, :, cols], bcast(PS[0:P, 0, 0:PAIR], 1, [P, KD, PAIR]), ALU.mult)
                V.tensor_tensor(nrm[:, :, cols], nrm[:, :, cols], bcast(PS[0:P, 1, 0:PAIR], 1, [P, KD, PAIR]), ALU.mult)\
                    .then_inc(next_ready, 1)
                dve.wait_ge(next_ready, i * 2 + 1)
                V.tensor_tensor(acc[:, :, cols], acc[:, :, cols], nrm[:, :, cols], ALU.add).then_inc(next_ready, 1)
                dve.wait_ge(next_ready, i * 2 + 2)
                V.tensor_tensor(h[:, :, cols], h[:, :, cols], acc[:, :, cols], ALU.add).then_inc(h_ready, 1)
            dve.wait_ge(h_ready, NPAIR + 1)


class Consts:
    pass


def store(nc, h, out):
    with nc.semaphore("out_stored") as stored, nc.Block() as block:

        @block.sync
        def _(sp):
            for k in range(KD):
                sp.dma_start(out[:, k, :], h[:, k, :]).then_inc(stored, 16)
            sp.wait_ge(stored, 16 * KD)


STAGES = 5


def build(nc, dr, out):
    with ExitStack() as ctx:
        s = Scope(nc, ctx, "all")
        h = s.sb("h", [P, KD, N])
        PS = ctx.enter_context(nc.psum_tensor("PS", [128, 8, 512], F32))
        C = Consts()
        C.ones = s.sb("ones", [P, P])
        C.ident = s.sb("identity", [128, 128])
        C.eps5 = s.sb("eps5", [P, 1])
        with nc.Block() as block:

            @block.vector
            def _(dve):
                nc.vector.memset(C.eps5[:, :], 1e-5)

        tokenizer(nc, dr, PS, C, h)
        if STAGES >= 2:
            mamba(nc, dr, PS, C, h)
        if STAGES >= 3:
            experts(nc, dr, PS, C, h)
        if STAGES >= 4:
            attention(nc, dr, PS, C, h)
        if STAGES >= 5:
            switch(nc, dr, PS, C, h)
        store(nc, h, out)



def layouts(i):
    a = {k: np.asarray(v) for k, v in i.items()}

    def rows(w, p):
        return w.reshape(w.shape[0] // p, p, *w.shape[1:]).transpose(1, 0, *range(2, w.ndim + 1))

    def headpad(w):
        z = np.zeros((*w.shape[:-1], NH, HP), w.dtype)
        z[..., :DH] = w.reshape(*w.shape[:-1], NH, DH)
        return z.reshape(*w.shape[:-1], NH * HP)

    o = {}
    o["pix"] = rows(a["x"].reshape(B, 3, 8, 16, 8, 16).transpose(1, 3, 5, 0, 2, 4).reshape(768, B * NIMG), 128)
    o["txt"] = rows(a["txt"].transpose(2, 0, 1), P)
    o["wp"] = rows(a["L0_tok_patch_w"].reshape(D, 768).T, 128)
    o["tok_vec"] = np.stack([rows(a["L0_tok_" + n], P) for n in ("patch_b", "ln_g", "ln_b", "ff2_b", "proj_b")], 1)
    o["ff1"] = rows(a["L0_tok_ff1_w"], P)
    o["ff1_b"] = rows(a["L0_tok_ff1_b"], 128)
    o["ff2"] = rows(a["L0_tok_ff2_w"], 128)
    qkv, qkvb = a["L0_tok_qkv_w"].reshape(D, 3, D), a["L0_tok_qkv_b"].reshape(3, D)
    o["tok_wqk"] = rows(headpad(qkv[:, 0:2]), P)
    o["tok_bqk"] = headpad(qkvb[0:2]).reshape(2, QC, 128).transpose(2, 0, 1)
    o["tok_wv"] = rows(headpad(qkv[:, 2]), P)
    o["tok_bv"] = headpad(qkvb[2])
    o["tok_wo"] = rows(headpad(a["L0_tok_proj_w"].T).T, 128)
    inw = a["L0_attn_in_proj_w"].transpose(0, 2, 1)
    lrows = lambda w, p: np.stack([rows(x, p) for x in w])
    o["ssm_winx"], o["ssm_winz"] = lrows(inw[:, :, :384], P), lrows(inw[:, :, 384:], P)
    o["ssm_nvec"] = np.stack([lrows(a["L0_attn_norm_w"], P), lrows(a["L0_attn_norm_b"], P)], 2)
    o["ssm_fvec"] = np.stack([rows(a["L0_attn_norm_f_w"], P), rows(a["L0_attn_norm_f_b"], P)], 1)
    o["ssm_cvec"] = lrows(np.concatenate([a["L0_attn_conv_w"], *(a["L0_attn_" + n][..., None] for n in
                                                                 ("conv_b", "dt_proj_b", "D_skip"))], -1), 128)
    o["ssm_alog"] = lrows(a["L0_attn_A_log"], 128)
    xw = a["L0_attn_x_proj_w"].transpose(0, 2, 1)
    o["ssm_wbc"] = lrows(np.concatenate([xw[:, :, 12:]] * 3, -1), 128)
    o["ssm_wdt"] = lrows(xw[:, :, :12], 128)
    o["ssm_wdt2"] = a["L0_attn_dt_proj_w"].transpose(0, 2, 1)
    o["ssm_wout"] = lrows(a["L0_attn_out_proj_w"].transpose(0, 2, 1), 128)
    pick = np.zeros((3, 32, 32, 128), mybir.dt.np(BF16))
    for n in range(32):
        pick[:, n, n] = 1
    o["ssm_sel"] = pick.reshape(P, 32 * 128)
    m = {k[7:]: v for k, v in a.items() if k.startswith("L0_ffn_")}
    o["moe_wr"] = rows(np.concatenate([m["router_w"], m["sg_w"]], 1), P)
    o["moe_wg"], o["moe_wu"] = (rows(m[k].transpose(1, 0, 2).reshape(D, 8 * 192), P) for k in ("w_gate", "w_up"))
    o["moe_wd"] = rows(m["w_down"].reshape(8 * 192, D), P)
    o["moe_wsg"], o["moe_wsu"], o["moe_wsd"] = rows(m["ws_gate"], P), rows(m["ws_up"], P), rows(m["ws_down"], 128)
    o["moe_sgb"] = m["sg_b"]
    o["moe_rank"] = np.tile(np.arange(8, 0, -1, dtype=np.float32), (94, 1))
    o["moe_pick"] = np.repeat(np.eye(9, dtype=np.float32), 128, 1)
    qkv = a["L1_attn_qkv_w"].T.reshape(D, 3, D)
    o["att_wqk"], o["att_wk"], o["att_wv"] = rows(headpad(qkv[:, 0:2]), P), rows(qkv[:, 1], P), \
        rows(headpad(qkv[:, 2]), P)
    o["att_wo"] = rows(headpad(a["L1_attn_proj_w"]).T, 128)
    o["att_bo"] = rows(a["L1_attn_proj_b"], P)
    pick = np.zeros((8, DH, 2, HP), np.float32)
    for g in range(2):
        for r in range(8):
            pick[r, :, g, g * 8 + r] = 1 / (2 * (0.5 * DH ** -0.5) * T)
    o["att_sel"] = pick.reshape(128, 2, HP)
    pick = np.zeros((2, 2, 8, 2, 2, 8, DH), np.float32)
    for g in range(2):
        for sign in range(2):
            for r in range(8):
                pick[sign, g, r, g, sign, r] = 1
    o["att_spread"] = pick.reshape(2 * DH, 4, 128)
    o["sw_lnw"], o["sw_wr"] = rows(a["L1_ffn_ln_w"], P), rows(a["L1_ffn_w_router"], P)
    o["sw_wi"], o["sw_wo"] = lrows(a["L1_ffn_wi"], P), lrows(a["L1_ffn_wo"], 128)
    o["sw_rank"] = np.tile(np.arange(16, 0, -1, dtype=np.float32), (94, 1))
    o["sw_pick"] = np.repeat(np.eye(18, dtype=np.float32), 128, 1)
    at = np.arange(PAIR)
    before = ((at[:, None] <= at[None]) & (at[:, None] // T == at[None] // T)).astype(np.float32)
    o["sw_upto"] = np.stack([before[x * 94:(x + 1) * 94, y * 94:(y + 1) * 94] for x, y in
                             ((0, 0), (0, 1), (1, 1), (1, 2), (2, 2))], 1)
    at, fr = np.arange(NIMG, dtype=np.float32)[:, None], np.arange(D // 2, dtype=np.float32)[None, :]
    ang = at / np.power(np.float32(10000.0), np.float32(2.0) * fr / np.float32(D))
    pe = np.zeros((NIMG, D), np.float32)
    pe[:, 0::2], pe[:, 1::2] = np.sin(ang), np.cos(ang)
    o["pos"] = rows(pe.T, P)
    o["ones"] = np.full((P, P), 1.0 / D, np.float32)
    o["ident"] = np.eye(128, dtype=np.float32)
    return {k: np.ascontiguousarray(v) for k, v in o.items()}


def kernel(**inputs):
    import concourse.bacc as _bacc
    from concourse.bass_utils import run_bass_kernel_spmd as _run

    nc = _bacc.Bacc("TRN2", target_bir_lowering=False, num_devices=1)
    arrays = layouts(inputs)
    dr = {k: nc.dram_tensor("in_" + k, v.shape, mybir.dt.from_np(v.dtype), kind="ExternalInput").ap() for k, v in arrays.items()}
    out = nc.dram_tensor("out", (P, KD, N), F32, kind="ExternalOutput").ap()
    build(nc, dr, out)
    r = _run(nc, [{"in_" + k: v for k, v in arrays.items()}], core_ids=[0]).results[0]["out"]
    return np.ascontiguousarray(r.transpose(1, 0, 2).reshape(D, B, T).transpose(1, 2, 0))
```

```python
from contextlib import ExitStack

import numpy as np

import concourse.bass as bass
from concourse import mybir

F32 = mybir.dt.float32
BF16 = mybir.dt.bfloat16
I32 = mybir.dt.int32
ALU = mybir.AluOpType
ACT = mybir.ActivationFunctionType
AX = mybir.AxisListType

B = 16
NIMG, NTXT = 64, 77
T = NIMG + NTXT
N = B * T
D = 192
P = 96
KD = D // P
NH, DH = 12, 16
HP = 32
QC = NH * HP // 128
FF = 768
FC = FF // 128
PAIR = 2 * T
NPAIR = B // 2
ds = bass.ds


def bcast(ap, axis, shape):
    return ap.unsqueeze(axis).broadcast_to(shape)


class Scope:

    def __init__(self, nc, ctx, tag):
        self.nc, self.ctx, self.tag = nc, ctx, tag
        self.all_sems = []
        ctx.callback(self.clear)

    def clear(self):
        if self.all_sems:
            self.nc.all_engine_barrier()
            self.nc.clear_and_free_semaphores(self.all_sems)
            self.nc.all_engine_barrier()

    def sb(self, name, shape, dt=F32):
        return self.ctx.enter_context(self.nc.sbuf_tensor(f"{self.tag}_{name}", shape, dt))

    def sem(self, name):
        self.all_sems.append(self.nc.alloc_semaphore(f"{self.tag}_{name}"))
        return self.all_sems[-1]

    def sems(self, *names):
        return [self.sem(n) for n in names]


class Norm:

    def __init__(self, s, tag, q, w, mean_ps, var_ps, ones, eps, center=True, xc=None, sq=None):
        self.q, self.w, self.mean_ps, self.var_ps, self.ones, self.eps = q, w, mean_ps, var_ps, ones, eps
        self.center = center
        self.xc = s.sb(f"{tag}_xc", [P, KD, q * w]) if center and xc is None else xc
        self.sq = s.sb(f"{tag}_sq", [P, KD, q * w]) if sq is None else sq
        self.rstd = s.sb(f"{tag}_rstd", [P, q * w])
        self.x_ready, self.mean_ready, self.centered, self.squared, self.var_ready, self.logvar, \
            self.rstd_ready, self.normed = s.sems(*(f"{tag}_{x}" for x in (
                "x_ready", "mean_ready", "centered", "squared", "var_ready", "logvar", "rstd_ready", "normed")))

    def total(self, nc, ps, x):
        for q in range(self.q):
            for k in range(KD):
                mm = nc.tensor.matmul(ps[:, q, :], self.ones[:, :], x[:, k, q * self.w:(q + 1) * self.w],
                                      start=k == 0, stop=k == KD - 1)
        return mm

    def split(self, ap):
        return ap.rearrange("p k (q t) -> p k q t", t=self.w)

    def pe(self, nc, pe, v, cols=None):
        if self.center:
            pe.wait_ge(self.x_ready, v)
            for q in range(self.q):
                for k in range(KD):
                    mm = nc.tensor.matmul(self.mean_ps[:, q, :], self.ones[:, :], cols(k, q * self.w, self.w),
                                          start=k == 0, stop=k == KD - 1)
            mm.then_inc(self.mean_ready, 1)
        pe.wait_ge(self.squared, v)
        self.total(nc, self.var_ps, self.sq).then_inc(self.var_ready, 1)

    def act(self, nc, act, v, x=None):
        if self.center:
            act.wait_ge(self.centered, v)
            nc.scalar.activation(self.sq[:, :, :], self.xc[:, :, :], ACT.Square).then_inc(self.squared, 1)
        else:
            act.wait_ge(self.x_ready, v)
            nc.scalar.activation(self.sq[:, :, :], x, ACT.Square).then_inc(self.squared, 1)
        act.wait_ge(self.var_ready, v)
        nc.scalar.activation(self.rstd[:, :].rearrange("p (q t) -> p q t", t=self.w), self.var_ps, ACT.Ln,
                             bias=self.eps[:, 0:1]).then_inc(self.logvar, 1)
        act.wait_ge(self.logvar, v)
        nc.scalar.activation(self.rstd[:, :], self.rstd[:, :], ACT.Exp, scale=-0.5).then_inc(self.rstd_ready, 1)

    def dve(self, nc, dve, v, x, out):
        if self.center:
            dve.wait_ge(self.mean_ready, v)
            nc.vector.tensor_tensor(self.split(self.xc[:, :, :]), self.split(x),
                                    bcast(self.mean_ps, 1, [P, KD, self.q, self.w]),
                                    ALU.subtract).then_inc(self.centered, 1)
        dve.wait_ge(self.rstd_ready, v)
        src = self.xc[:, :, :] if self.center else x
        nc.vector.tensor_tensor(out, src, bcast(self.rstd[:, :], 1, [P, KD, self.q * self.w]), ALU.mult)\
            .then_inc(self.normed, 1)


class FeedForward:

    def __init__(self, s, n, PS, bank, w1, b1, w2):
        self.n, self.PS, self.bank, self.w1, self.b1, self.w2 = n, PS, bank, w1, b1, w2
        self.hid = s.sb("ff_hid", [128, FC, n])
        self.in_ready, self.hid_summed, self.hid_ready, self.out_summed = s.sems(
            "ff_in_ready", "ff_hid_summed", "ff_hid_ready", "ff_out_summed")

    def pe(self, nc, pe, v, x):
        pe.wait_ge(self.in_ready, v + 1)
        for j in range(FC):
            if j >= 2:
                pe.wait_ge(self.hid_ready, v * FC + (j - 1))
            for k in range(KD):
                mm = nc.tensor.matmul(self.PS[:, self.bank + j % 2, 0:self.n], self.w1[:, k, j * 128:(j + 1) * 128],
                                      x[:, k, :], start=k == 0, stop=k == KD - 1)
            mm.then_inc(self.hid_summed, 1)
        for j in range(FC):
            pe.wait_ge(self.hid_ready, v * FC + (j + 1))
            for m in range(KD):
                mm = nc.tensor.matmul(self.PS[0:P, self.bank + 2 + m, 0:self.n], self.w2[:, j, m * P:(m + 1) * P],
                                      self.hid[:, j, :], start=j == 0, stop=j == FC - 1)
        mm.then_inc(self.out_summed, 1)

    def act(self, nc, act, v):
        for j in range(FC):
            act.wait_ge(self.hid_summed, v * FC + (j + 1))
            nc.scalar.activation(self.hid[:, j, :], self.PS[:, self.bank + j % 2, 0:self.n], ACT.Gelu_apprx_tanh,
                                 bias=self.b1[:, j:j + 1]).then_inc(self.hid_ready, 1)


def tokenizer(nc, dr, PS, C, h):
    NI = B * NIMG
    NB = 512
    NL = NI // NB
    WT = 2 * NIMG
    NW = NI // WT
    KP = 6
    with ExitStack() as ctx:
        s = Scope(nc, ctx, "tok")
        pix = s.sb("pix", [128, KP, NI])
        wp = s.sb("wp", [128, KP, D])
        ff1 = s.sb("ff1", [P, KD, FF])
        ff2 = s.sb("ff2", [128, FC, D])
        wqk = s.sb("wqk", [P, KD, 2, QC * 128])
        wv = s.sb("wv", [P, KD, QC * 128])
        wo = s.sb("wo", [128, QC, D])
        vec = s.sb("vec", [P, 5, KD])
        b1 = s.sb("b1", [128, FC])
        bqk = s.sb("bqk", [128, 2, QC])
        bv = s.sb("bv", [NIMG, QC * 128])
        pos = s.sb("pos", [P, KD, NIMG])
        emb = s.sb("emb", [P, KD, NB])
        xg = s.sb("xg", [P, KD, NB])
        ident = s.sb("ident", [P, KD, NI])
        y1 = s.sb("y1", [P, KD, NI])
        x2 = s.sb("x2", [P, KD, NI])
        yb = s.sb("yb", [P, KD, WT])
        qk = s.sb("qk", [128, 2, QC, WT])
        v = s.sb("v", [NIMG, 2, QC * 128])
        mx = s.sb("mx", [NIMG, 4, 6])
        sx = s.sb("sx", [NIMG, 4, 6, NIMG])
        ex = s.sb("ex", [NIMG, 4, 6, NIMG])
        pT = s.sb("pT", [NIMG, 24, NIMG])
        oT = s.sb("oT", [128, QC, WT])
        ln = Norm(s, "ln", 1, NB, PS[0:P, 6:7, :], PS[0:P, 7:8, :], C.ones, C.eps5)
        ff = FeedForward(s, NB, PS, 2, ff1, b1, ff2)
        loaded, patch_summed, ident_ready, y1_ready, gained, scaled = s.sems(
            "loaded", "patch_summed", "ident_ready", "y1_ready", "gained", "scaled")
        yb_ready, qk_summed, qk_ready, v_summed, v_ready, scored, maxed, shifted, exped, summed, inverted, probs, \
            turned, pT_ready, mixed, oT_ready, projected, x2_ready, h_ready = s.sems(
                "yb_ready", "qk_summed", "qk_ready", "v_summed", "v_ready", "scored", "maxed", "shifted", "exped",
                "summed", "inverted", "probs", "turned", "pT_ready", "mixed", "oT_ready", "projected", "x2_ready",
                "h_ready")
        h4 = h[:, :, :].rearrange("p k (b t) -> p k b t", t=T)
        loads = [(pix[:, :, :], dr["pix"]), (wp[:, :, :], dr["wp"]), (vec[:, :, :], dr["tok_vec"]),
                 (pos[:, :, :], dr["pos"]), (ff1[:, :, :], dr["ff1"]), (b1[:, :], dr["ff1_b"]),
                 (ff2[:, :, :], dr["ff2"]), (wqk[:, :, :, :], dr["tok_wqk"]), (bqk[:, :, :], dr["tok_bqk"]),
                 (wv[:, :, :], dr["tok_wv"]), (bv[:, :], dr["tok_bv"].partition_broadcast(NIMG)),
                 (wo[:, :, :], dr["tok_wo"]), (C.ones[:, :], dr["ones"]), (C.ident[:, :], dr["ident"])]
        loads += [(h4[:, k, :, NIMG:T], dr["txt"][:, k, :, :]) for k in range(KD)]
        ALL = 16 * len(loads)
        block = ctx.enter_context(nc.Block())

        @block.sync
        def _(sp):
            for dst, src in loads:
                sp.dma_start(dst, src).then_inc(loaded, 16)
            sp.wait_ge(loaded, ALL)

        @block.tensor
        def _(pe):
            pe.wait_ge(loaded, ALL)
            with pe.Fori(0, NL) as i:
                for m in range(KD):
                    for k in range(KP):
                        mm = nc.tensor.matmul(PS[0:P, m, :], wp[:, k, m * P:(m + 1) * P], pix[:, k, ds(i * NB, NB)],
                                              start=k == 0, stop=k == KP - 1)
                mm.then_inc(patch_summed, 1)
                ln.pe(nc, pe, i + 1, lambda k, at, w: emb[:, k, at:at + w])
                ff.pe(nc, pe, i, ident[:, :, ds(i * NB, NB)])
            with pe.Fori(0, NW) as i:
                pe.wait_ge(yb_ready, i + 1)
                for a in range(2):
                    for c in range(QC):
                        for k in range(KD):
                            mm = nc.tensor.matmul(PS[:, a, c * WT:(c + 1) * WT], wqk[:, k, a, c * 128:(c + 1) * 128],
                                                  yb[:, k, :], start=k == 0, stop=k == KD - 1)
                    mm.then_inc(qk_summed, 1)
                for w in range(2):
                    for k in range(KD):
                        mm = nc.tensor.matmul(PS[0:NIMG, 2 + w, 0:QC * 128], yb[:, k, w * NIMG:(w + 1) * NIMG],
                                              wv[:, k, :], start=k == 0, stop=k == KD - 1)
                mm.then_inc(v_summed, 1)
                pe.wait_ge(qk_ready, 2 * i + 2)
                for j in range(4):
                    for w in range(2):
                        for c in range(QC):
                            rows, cols, slot = slice(HP * j, HP * j + DH), slice(w * NIMG, (w + 1) * NIMG), w * QC + c
                            mm = nc.tensor.matmul(PS[0:NIMG, 4 + j, slot * NIMG:(slot + 1) * NIMG],
                                                  qk[rows, 0, c, cols], qk[rows, 1, c, cols], start=True, stop=True)
                mm.then_inc(scored, 1)
                pe.wait_ge(loaded, ALL)
                pe.wait_ge(probs, i + 1)
                pe.wait_ge(v_ready, i + 1)
                for n in range(24):
                    mm = nc.tensor.transpose(PS[0:NIMG, n // 8, (n % 8) * NIMG:(n % 8 + 1) * NIMG],
                                             ex[:, n // 6, n % 6, :], C.ident[0:NIMG, 0:NIMG])
                mm.then_inc(turned, 1)
                pe.wait_ge(loaded, ALL)
                pe.wait_ge(pT_ready, i + 1)
                for j in range(4):
                    for w in range(2):
                        for c in range(QC):
                            mm = nc.tensor.matmul(PS[HP * j:HP * (j + 1), 3, c * WT + w * NIMG:c * WT + (w + 1) * NIMG],
                                                  v[:, w, (4 * c + j) * HP:(4 * c + j + 1) * HP],
                                                  pT[:, j * 6 + w * QC + c, :], start=True, stop=True)
                mm.then_inc(mixed, 1)
                pe.wait_ge(oT_ready, i + 1)
                for m in range(KD):
                    for c in range(QC):
                        mm = nc.tensor.matmul(PS[0:P, 4, m * WT:(m + 1) * WT], wo[:, c, m * P:(m + 1) * P],
                                              oT[:, c, :], start=c == 0, stop=c == QC - 1)
                mm.then_inc(projected, 1)
            with pe.Fori(0, NL) as i:
                ff.pe(nc, pe, i + NL, x2[:, :, ds(i * NB, NB)])

        @block.scalar
        def _(act):
            act.wait_ge(loaded, ALL)
            with act.Fori(0, NL) as i:
                act.wait_ge(patch_summed, i + 1)
                for m in range(KD):
                    op = nc.scalar.activation(emb[:, m, :], PS[0:P, m, :], ACT.Identity, bias=vec[:, 0, m:m + 1])
                op.then_inc(ln.x_ready, 1)
                ln.act(nc, act, i + 1)
                ff.act(nc, act, i)
                act.wait_ge(ff.out_summed, i + 1)
                for m in range(KD):
                    op = nc.scalar.activation(y1[:, m, ds(i * NB, NB)], PS[0:P, 4 + m, :], ACT.Identity,
                                              bias=vec[:, 3, m:m + 1])
                op.then_inc(y1_ready, 1)
            with act.Fori(0, NW) as i:
                act.wait_ge(shifted, i + 1)
                nc.scalar.activation(ex[:, :, :, :], sx[:, :, :, :], ACT.Exp, scale=DH ** -0.5).then_inc(exped, 1)
                act.wait_ge(turned, i + 1)
                nc.scalar.activation(pT[:, :, :], PS[0:NIMG, 0:3, :].rearrange("p a (b t) -> p (a b) t", t=NIMG),
                                     ACT.Copy).then_inc(pT_ready, 1)
                act.wait_ge(mixed, i + 1)
                nc.scalar.activation(oT[:, :, :], PS[:, 3, 0:QC * WT].rearrange("p (c t) -> p c t", t=WT),
                                     ACT.Copy).then_inc(oT_ready, 1)
            with act.Fori(0, NL) as i:
                ff.act(nc, act, i + NL)

        @block.vector
        def _(dve):
            dve.wait_ge(loaded, ALL)
            with dve.Fori(0, NL) as i:
                ln.dve(nc, dve, i + 1, emb[:, :, :], emb[:, :, :])
                dve.wait_ge(ln.normed, i + 1)
                for m in range(KD):
                    op = nc.vector.tensor_scalar(xg[:, m, :], emb[:, m, :], vec[:, 1, m:m + 1], vec[:, 2, m:m + 1],
                                                 ALU.mult, ALU.add)
                op.then_inc(gained, 1)
                dve.wait_ge(gained, i + 1)
                for m in range(KD):
                    op = nc.vector.tensor_tensor(
                        ident[:, m, ds(i * NB, NB)].rearrange("p (b t) -> p b t", t=NIMG),
                        xg[:, m, :].rearrange("p (b t) -> p b t", t=NIMG),
                        bcast(pos[:, m, :], 1, [P, NB // NIMG, NIMG]), ALU.add)
                op.then_inc(ff.in_ready, 1)
            with dve.Fori(0, NW) as i:
                dve.wait_ge(y1_ready, NL)
                nc.vector.tensor_copy(yb[:, :, :], y1[:, :, ds(i * WT, WT)]).then_inc(yb_ready, 1)
                for a in range(2):
                    dve.wait_ge(qk_summed, 2 * i + (a + 1))
                    nc.vector.tensor_tensor(qk[:, a, :, :], PS[:, a, 0:QC * WT].rearrange("p (c t) -> p c t", t=WT),
                                            bcast(bqk[:, a, :], 2, [128, QC, WT]), ALU.add).then_inc(qk_ready, 1)
                dve.wait_ge(v_summed, i + 1)
                nc.vector.tensor_tensor(v[:, :, :], PS[0:NIMG, 2:4, 0:QC * 128],
                                        bcast(bv[:, :], 1, [NIMG, 2, QC * 128]), ALU.add).then_inc(v_ready, 1)
                sc = PS[0:NIMG, 4:8, 0:6 * NIMG].rearrange("p j (n t) -> p j n t", t=NIMG)
                dve.wait_ge(scored, i + 1)
                nc.vector.reduce_max(mx[:, :, :], sc, AX.X).then_inc(maxed, 1)
                dve.wait_ge(maxed, i + 1)
                for j in range(4):
                    op = nc.vector.tensor_tensor(sx[:, j, :, :], sc[:, j, :, :], bcast(mx[:, j, :], 2, [NIMG, 6, NIMG]),
                                                 ALU.subtract)
                op.then_inc(shifted, 1)
                dve.wait_ge(exped, i + 1)
                nc.vector.reduce_sum(mx[:, :, :], ex[:, :, :, :], AX.X).then_inc(summed, 1)
                dve.wait_ge(summed, i + 1)
                nc.vector.reciprocal(mx[:, :, :], mx[:, :, :]).then_inc(inverted, 1)
                dve.wait_ge(inverted, i + 1)
                for j in range(4):
                    op = nc.vector.tensor_tensor(ex[:, j, :, :], ex[:, j, :, :], bcast(mx[:, j, :], 2, [NIMG, 6, NIMG]),
                                                 ALU.mult)
                op.then_inc(probs, 1)
                dve.wait_ge(projected, i + 1)
                for m in range(KD):
                    op = nc.vector.scalar_tensor_tensor(
                        out=x2[:, m, ds(i * WT, WT)], in0=PS[0:P, 4, m * WT:(m + 1) * WT], scalar=vec[:, 4, m:m + 1],
                        in1=ident[:, m, ds(i * WT, WT)], op0=ALU.add, op1=ALU.add)
                op.then_inc(x2_ready, 1)
            dve.wait_ge(x2_ready, NW)
            with dve.Fori(0, NL) as i:
                nc.vector.sem_inc(ff.in_ready, 1)
                dve.wait_ge(ff.out_summed, i + NL + 1)
                for m in range(KD):
                    op = nc.vector.scalar_tensor_tensor(
                        out=h4[:, m, ds(i * 8, 8), 0:NIMG],
                        in0=PS[0:P, 4 + m, :].rearrange("p (b t) -> p b t", t=NIMG), scalar=vec[:, 3, m:m + 1],
                        in1=x2[:, m, ds(i * NB, NB)].rearrange("p (b t) -> p b t", t=NIMG), op0=ALU.add, op1=ALU.add)
                op.then_inc(h_ready, 1)
                dve.wait_ge(h_ready, i + 1)


def mamba(nc, dr, PS, C, h):
    L, DI, DS, DC, DR = 4, 384, 16, 4, 12
    CT = DI // 128
    QW = 4 * T
    NQ = N // QW
    HW = QW // 2
    SP2 = DS // 2
    UW = 2 * QW
    RESTART = 1e20
    with ExitStack() as ctx:
        s = Scope(nc, ctx, "ssm")
        res = s.sb("res", [P, KD, N])
        winx = s.sb("winx", [P, KD, DI])
        winz = s.sb("winz", [P, KD, DI])
        nvec = s.sb("nvec", [P, 2, KD])
        fvec = s.sb("fvec", [P, 2, KD])
        cvec = s.sb("cvec", [128, CT, DC + 3])
        a_log = s.sb("a_log", [128, CT, DS])
        amat = s.sb("amat", [128, CT, DS])
        wbc = s.sb("wbc", [128, CT, P])
        wdt = s.sb("wdt", [128, CT, DR])
        wdt2 = s.sb("wdt2", [DR, DI])
        wout = s.sb("wout", [128, CT, D])
        sel = s.sb("sel", [P, 2 * DS * 128], BF16)
        hn = s.sb("hn", [P, KD, QW])
        xs = s.sb("xs", [128, CT, QW])
        sz = s.sb("sz", [128, CT, QW])
        dt = s.sb("dt", [128, CT, QW])
        sp = s.sb("sp", [128, CT, QW])
        us = s.sb("us", [128, CT, QW])
        low = s.sb("low", [DR, QW])
        bcf = s.sb("bcf", [P, QW])
        bcr = s.sb("bcr", [P, QW])
        mid = s.sb("mid", [P, QW], BF16)
        bcp = s.sb("bcp", [P, QW], BF16)
        bb = s.sb("bb", [128, DS, QW])
        cb = s.sb("cb", [128, DS, QW])
        da = s.sb("da", [128, 2, UW])
        hs = s.sb("hs", [128, 2, UW])
        hc = s.sb("hc", [128, 2, UW])
        flat = PS[:, :, :].rearrange("p a b -> p (a b)")
        u_ps = flat[:, 0:QW]
        dbx = [flat[:, QW + n * UW:QW + (n + 1) * UW] for n in range(2)]
        assert QW + 2 * UW <= 6 * 512
        ln = Norm(s, "ln", 2, HW, PS[0:P, 0:2, 0:HW], PS[0:P, 2:4, 0:HW], C.ones, C.eps5,
                  xc=us[0:P, 0:KD, :], sq=sp[0:P, 0:KD, :])
        loaded, wloaded, layer_done, gained, xin_summed, tap, conv_done, z_summed, sz_ready, xs_ready, low_summed, \
            low_ready, dt_summed, dt_pre, dt_abs, dt_exp, dt_log, dt_ready, split1, split2, split3, bcp_ready, \
            b_summed, c_summed, b_ready, c_ready, a_exp, a_ready, us_ready, restart, u_ready, \
            da_ready, dbx_ready, scanned, weighted, reduced, y_taken, gated, out_summed, res_ready, h_ready = s.sems(
                "loaded", "wloaded", "layer_done", "gained", "xin_summed", "tap", "conv_done", "z_summed", "sz_ready",
                "xs_ready", "low_summed", "low_ready", "dt_summed", "dt_pre", "dt_abs", "dt_exp", "dt_log", "dt_ready",
                "split1", "split2", "split3", "bcp_ready", "b_summed", "c_summed", "b_ready", "c_ready", "a_exp",
                "a_ready", "us_ready", "restart", "u_ready", "da_ready", "dbx_ready", "scanned", "weighted", "reduced",
                "y_taken", "gated", "out_summed", "res_ready", "h_ready")
        entered = s.sems("pe_loop_entered", "dve_loop_entered", "pool_loop_entered")
        wloads = [(winx[:, :, :], "ssm_winx"), (winz[:, :, :], "ssm_winz"), (nvec[:, :, :], "ssm_nvec"),
                  (cvec[:, :, :], "ssm_cvec"), (a_log[:, :, :], "ssm_alog"), (wbc[:, :, :], "ssm_wbc"),
                  (wdt[:, :, :], "ssm_wdt"), (wdt2[:, :], "ssm_wdt2"), (wout[:, :, :], "ssm_wout")]
        NWL = 16 * len(wloads)
        two = lambda ap: ap.rearrange("p (q t) -> p q t", t=HW)
        block = ctx.enter_context(nc.Block())

        @block.sync
        def _(sync):
            sync.dma_start(sel[:, :], dr["ssm_sel"]).then_inc(loaded, 16)
            sync.dma_start(fvec[:, :, :], dr["ssm_fvec"]).then_inc(loaded, 16)
            with sync.Fori(0, L) as l:
                sync.wait_ge(layer_done, l + 1)
                for dst, name in wloads:
                    src = dr[name][ds(l, 1)]
                    src = src.rearrange("a p b -> (a p) b") if len(src.shape) == 3 else \
                        src.rearrange("a p b c -> (a p) b c")
                    sync.dma_start(dst, src).then_inc(wloaded, 16)
            sync.wait_ge(wloaded, NWL * L)
            sync.wait_ge(loaded, 32)

        @block.tensor
        def _(pe):
            with pe.Fori(0, NQ) as q:
                ln.pe(nc, pe, q + 1, lambda k, at, w: h[:, k, ds(q * QW + at, w)])
            pe.wait_ge(loaded, 32)
            with pe.Fori(0, L) as l:
                pe.wait_ge(wloaded, l * NWL + NWL)
                nc.tensor.sem_inc(entered[0], 1)
                with pe.Fori(0, NQ) as q:
                    v = l * NQ + q
                    ln.pe(nc, pe, v + (NQ + 1), lambda k, at, w: res[:, k, ds(q * QW + at, w)])
                    pe.wait_ge(gained, v + 1)
                    for c in range(CT):
                        for b in range(2):
                            for k in range(KD):
                                mm = nc.tensor.matmul(PS[:, 2 * c + b, 0:HW], winx[:, k, c * 128:(c + 1) * 128],
                                                      hn[:, k, b * HW:(b + 1) * HW], start=k == 0, stop=k == KD - 1)
                    mm.then_inc(xin_summed, 1)
                    for c in range(CT):
                        pe.wait_ge(sz_ready, v * CT + (c + 1))
                        for b in range(2):
                            for k in range(KD):
                                mm = nc.tensor.matmul(PS[:, 6 + b, 0:HW], winz[:, k, c * 128:(c + 1) * 128],
                                                      hn[:, k, b * HW:(b + 1) * HW], start=k == 0, stop=k == KD - 1)
                        mm.then_inc(z_summed, 1)
                    pe.wait_ge(xs_ready, v + 1)
                    pe.wait_ge(sz_ready, v * CT + (CT + 1))
                    for b in range(2):
                        for c in range(CT):
                            nc.tensor.matmul(PS[0:P, 6 + b, 0:HW], wbc[:, c, :], xs[:, c, b * HW:(b + 1) * HW],
                                             start=c == 0, stop=c == CT - 1)
                    for b in range(2):
                        for c in range(CT):
                            mm = nc.tensor.matmul(PS[0:DR, b, 0:HW], wdt[:, c, :], xs[:, c, b * HW:(b + 1) * HW],
                                                  start=c == 0, stop=c == CT - 1)
                    mm.then_inc(low_summed, 1)
                    pe.wait_ge(low_ready, v + 1)
                    for c in range(CT):
                        for b in range(2):
                            mm = nc.tensor.matmul(PS[:, 2 + 2 * c + b, 0:HW], wdt2[:, c * 128:(c + 1) * 128],
                                                  low[:, b * HW:(b + 1) * HW], start=True, stop=True)
                    mm.then_inc(dt_summed, 1)
                    pe.wait_ge(dt_pre, v + 1)
                    pe.wait_ge(bcp_ready, v + 1)
                    nc.tensor.sem_inc(entered[0], 1)

                    def spread(x, n, e, col, taken, summed):
                        pe.wait_ge(taken, v * DS + (n + 1))
                        for b in range(2):
                            mm = nc.tensor.matmul(PS[:, 4 * x + 2 * e + b, 0:HW], sel[:, col],
                                                  bcp[:, b * HW:(b + 1) * HW], start=True, stop=True)
                        mm.then_inc(summed, 1)

                    with pe.Fori(0, DS // 4) as j:
                        for e in range(2):
                            spread(1, j * 2 + e, e, ds(j * 256 + (DS + e) * 128, 128), c_ready, c_summed)
                    nc.tensor.sem_inc(entered[0], 1)
                    with pe.Fori(0, DS // 4) as j:
                        for e in range(2):
                            spread(0, j * 2 + e, e, ds(j * 256 + e * 128, 128), b_ready, b_summed)
                            spread(1, j * 2 + (DS // 2 + e), e, ds(j * 256 + (DS + DS // 2 + e) * 128, 128), c_ready,
                                   c_summed)
                    nc.tensor.sem_inc(entered[0], 1)
                    with pe.Fori(0, DS // 4) as j:
                        for e in range(2):
                            spread(0, j * 2 + (DS // 2 + e), e, ds(j * 256 + (DS // 2 + e) * 128, 128), b_ready, b_summed)
                    with pe.Fori(0, CT) as c:
                        pe.wait_ge(y_taken, v * CT + c + 1)
                        for n in range(SP2):
                            pe.wait_ge(weighted, v * CT * SP2 + c * SP2 + (n + 3))
                            for e in range(2):
                                for b in range(2):
                                    at = e * QW + b * HW
                                    mm = nc.tensor.matmul(PS[:, 6 + b, 0:HW], C.ident[:, :], hc[:, n % 2, at:at + HW],
                                                          start=n == 0 and e == 0, stop=n == SP2 - 1 and e == 1)
                            mm.then_inc(reduced, 1)
                    pe.wait_ge(gated, v + 1)
                    for m in range(KD):
                        for b in range(2):
                            for c in range(CT):
                                mm = nc.tensor.matmul(PS[0:P, 2 * m + b, 0:HW], wout[:, c, m * P:(m + 1) * P],
                                                      xs[:, c, b * HW:(b + 1) * HW], start=c == 0, stop=c == CT - 1)
                    mm.then_inc(out_summed, 1)
            with pe.Fori(0, NQ) as q:
                ln.pe(nc, pe, q + (NQ + L * NQ + 1), lambda k, at, w: res[:, k, ds(q * QW + at, w)])

        @block.scalar
        def _(act):
            with act.Fori(0, NQ) as q:
                ln.act(nc, act, q + 1)
            with act.Fori(0, L) as l:
                act.wait_ge(wloaded, l * NWL + NWL)
                with act.Fori(0, NQ) as q:
                    v = l * NQ + q
                    ln.act(nc, act, v + (NQ + 1))
                    nc.scalar.activation(amat[:, :, :], a_log[:, :, :], ACT.Exp).then_inc(a_exp, 1)
                    for c in range(CT):
                        act.wait_ge(z_summed, v * CT + (c + 1))
                        nc.scalar.activation(two(sz[:, c, :]), PS[:, 6:8, 0:HW], ACT.Silu).then_inc(sz_ready, 1)
                    act.wait_ge(conv_done, v + 1)
                    nc.scalar.activation(xs[:, :, :], xs[:, :, :], ACT.Silu).then_inc(xs_ready, 1)
                    act.wait_ge(low_summed, v + 1)
                    nc.scalar.activation(two(bcf[:, :]), PS[0:P, 6:8, 0:HW], ACT.Copy)
                    nc.scalar.activation(two(low[:, :]), PS[0:DR, 0:2, 0:HW], ACT.Copy).then_inc(low_ready, 1)
                    act.wait_ge(dt_summed, v + 1)
                    for c in range(CT):
                        op = nc.scalar.activation(two(dt[:, c, :]), PS[:, 2 + 2 * c:4 + 2 * c, 0:HW], ACT.Identity,
                                                  bias=cvec[:, c, DC + 1:DC + 2])
                    op.then_inc(dt_pre, 1)
                    act.wait_ge(dt_pre, v + 1)
                    nc.scalar.activation(sp[:, :, :], dt[:, :, :], ACT.Abs).then_inc(dt_abs, 1)
                    act.wait_ge(dt_abs, v + 1)
                    nc.scalar.activation(sp[:, :, :], sp[:, :, :], ACT.Exp, scale=-1.0).then_inc(dt_exp, 1)
                    act.wait_ge(dt_exp, v + 1)
                    nc.scalar.activation(sp[:, :, :], sp[:, :, :], ACT.Ln, bias=1.0).then_inc(dt_log, 1)
                    with act.Fori(0, DS // 2) as j:
                        for e in range(2):
                            n = v * DS + j * 2 + e
                            act.wait_ge(b_summed, n + 1)
                            nc.scalar.activation(two(bb[:, ds(j * 2 + e, 1), :].rearrange("p a t -> p (a t)")),
                                                 PS[:, 2 * e:2 * e + 2, 0:HW], ACT.Copy).then_inc(b_ready, 1)
                    act.wait_ge(restart, v + 1)
                    act.wait_ge(a_ready, v + 1)
                    with act.Fori(0, CT) as c:
                        for n in range(SP2):
                            act.wait_ge(scanned, v * CT * SP2 + c * SP2 + (n + 1))
                            for e in range(2):
                                op = nc.scalar.activation(
                                    da[:, n % 2, e * QW:(e + 1) * QW],
                                    dt[:, ds(c, 1), :].rearrange("p a t -> p (a t)"), ACT.Exp,
                                    scale=amat[:, ds(c, 1), 2 * n + e:2 * n + e + 1].rearrange("p a t -> p (a t)"))
                            op.then_inc(da_ready, 1)
            with act.Fori(0, NQ) as q:
                ln.act(nc, act, q + (NQ + L * NQ + 1))

        @block.gpsimd
        def _(pool):
            pool.sem_inc(weighted, 2)
            with pool.Fori(0, L * NQ) as v:
                pool.wait_ge(c_ready, v * DS + (DS + 2))
                nc.gpsimd.sem_inc(entered[2], 1)
                with pool.Fori(0, CT) as c:
                    for n in range(SP2):
                        u = v * CT * SP2 + c * SP2 + n
                        pool.wait_ge(scanned, u + 3)
                        pool.wait_ge(reduced, u + 1)
                        nc.gpsimd.tensor_tensor(hc[:, n % 2, :], hs[:, n % 2, :],
                                                cb[:, 2 * n:2 * n + 2, :].rearrange("p a t -> p (a t)"),
                                                ALU.mult).then_inc(weighted, 1)

        @block.vector
        def _(dve):
            nc.vector.sem_inc(layer_done, 1)
            nc.vector.sem_inc(scanned, 2)
            nc.vector.sem_inc(reduced, 2)
            nc.vector.sem_inc(b_ready, 2)
            nc.vector.sem_inc(c_ready, 2)
            nc.vector.sem_inc(y_taken, 1)
            nc.vector.sem_inc(sz_ready, 1)
            with dve.Fori(0, NQ) as q:
                nc.vector.sem_inc(ln.x_ready, 1)
                ln.dve(nc, dve, q + 1, h[:, :, ds(q * QW, QW)], res[:, :, ds(q * QW, QW)])
                dve.wait_ge(ln.normed, q + 1)
            with dve.Fori(0, L) as l:
                dve.wait_ge(wloaded, l * NWL + NWL)
                nc.vector.sem_inc(entered[1], 1)
                with dve.Fori(0, NQ) as q:
                    v = l * NQ + q
                    nc.vector.sem_inc(ln.x_ready, 1)
                    ln.dve(nc, dve, v + (NQ + 1), res[:, :, ds(q * QW, QW)], hn[:, :, :])
                    dve.wait_ge(ln.normed, v + (NQ + 1))
                    for m in range(KD):
                        op = nc.vector.tensor_scalar(hn[:, m, :], hn[:, m, :], nvec[:, 0, m:m + 1],
                                                     nvec[:, 1, m:m + 1], ALU.mult, ALU.add)
                    op.then_inc(gained, 1)
                    dve.wait_ge(a_exp, v + 1)
                    nc.vector.tensor_scalar(amat[:, :, :], amat[:, :, :], -1.0, -2e-18, ALU.mult, ALU.min)\
                        .then_inc(a_ready, 1)
                    dve.wait_ge(xin_summed, v + 1)
                    for back in range(DC):
                        if back:
                            dve.wait_ge(tap, v * (DC - 1) + back)
                        for c in range(CT):
                            for b in range(2):
                                src = PS[:, 2 * c + b, 0:HW].rearrange("p (b t) -> p b t", t=T)
                                dst = xs[:, c, b * HW:(b + 1) * HW].rearrange("p (b t) -> p b t", t=T)
                                w = cvec[:, c, DC - 1 - back:DC - back]
                                if back == 0:
                                    op = nc.vector.tensor_scalar(dst, src, w, cvec[:, c, DC:DC + 1],
                                                                 ALU.mult, ALU.add)
                                else:
                                    op = nc.vector.scalar_tensor_tensor(
                                        out=dst[:, :, back:T], in0=src[:, :, 0:T - back], scalar=w,
                                        in1=dst[:, :, back:T], op0=ALU.mult, op1=ALU.add)
                        op.then_inc(tap if back < DC - 1 else conv_done, 1)
                    dve.wait_ge(low_ready, v + 1)
                    nc.vector.tensor_copy(bcp[:, :], bcf[:, :]).then_inc(split1, 1)
                    dve.wait_ge(split1, v + 1)
                    nc.vector.tensor_tensor(bcr[:, :], bcf[:, :], bcp[:, :], ALU.subtract).then_inc(split2, 1)
                    dve.wait_ge(split2, v + 1)
                    nc.vector.tensor_copy(mid[:, :], bcr[:, :]).then_inc(split3, 1)
                    dve.wait_ge(split3, v + 1)
                    nc.vector.tensor_copy(bcp[32:64, :], mid[32:64, :])
                    nc.vector.tensor_tensor(bcp[64:96, :], bcr[64:96, :], mid[64:96, :], ALU.subtract)\
                        .then_inc(bcp_ready, 1)
                    nc.vector.sem_inc(entered[1], 1)
                    with dve.Fori(0, DS // 2) as j:
                        for e in range(2):
                            n = v * DS + j * 2 + e
                            dve.wait_ge(c_summed, n + 1)
                            nc.vector.tensor_copy(two(cb[:, ds(j * 2 + e, 1), :].rearrange("p a t -> p (a t)")),
                                                  PS[:, 4 + 2 * e:6 + 2 * e, 0:HW]).then_inc(c_ready, 1)
                    dve.wait_ge(dt_log, v + 1)
                    nc.vector.scalar_tensor_tensor(
                        out=dt[:, :, :].rearrange("p c t -> p (c t)"), in0=dt[:, :, :].rearrange("p c t -> p (c t)"),
                        scalar=0.0, in1=sp[:, :, :].rearrange("p c t -> p (c t)"), op0=ALU.max, op1=ALU.add)\
                        .then_inc(dt_ready, 1)
                    dve.wait_ge(dt_ready, v + 1)
                    nc.vector.tensor_tensor(us[:, :, :], dt[:, :, :], xs[:, :, :], ALU.mult).then_inc(us_ready, 1)
                    dve.wait_ge(us_ready, v + 1)
                    nc.vector.memset(dt[:, :, :].rearrange("p c (b t) -> p (c b) t", t=T)[:, :, 0:1], RESTART)\
                        .then_inc(restart, 1)
                    dve.wait_ge(b_ready, v * DS + (DS + 2))
                    dve.wait_ge(us_ready, v + 1)
                    nc.vector.sem_inc(entered[1], 1)
                    def finish(c):
                        dve.wait_ge(reduced, (v * CT + c) * SP2 + (SP2 + 2))
                        nc.vector.scalar_tensor_tensor(
                            out=two(xs[:, c, :]), in0=two(xs[:, c, :]), scalar=cvec[:, c, DC + 2:DC + 3],
                            in1=PS[:, 6:8, 0:HW], op0=ALU.mult, op1=ALU.add).then_inc(y_taken, 1)

                    for c in range(CT):
                        vc = v * CT + c
                        u0 = vc * SP2
                        if c:
                            dve.wait_ge(dbx_ready, u0)
                        nc.vector.tensor_copy(u_ps, us[:, c, :]).then_inc(u_ready, 1)
                        dve.wait_ge(u_ready, vc + 1)

                        def inject(n):
                            dve.wait_ge(scanned, u0 + (n + 1))
                            nc.vector.tensor_tensor(dbx[n % 2].rearrange("p (a t) -> p a t", t=QW),
                                                    bcast(u_ps, 1, [128, 2, QW]), bb[:, 2 * n:2 * n + 2, :],
                                                    ALU.mult).then_inc(dbx_ready, 1)

                        inject(0)
                        for n in range(SP2):
                            if n + 1 < SP2:
                                inject(n + 1)
                            dve.wait_ge(da_ready, u0 + (n + 1))
                            dve.wait_ge(dbx_ready, u0 + (n + 1))
                            dve.wait_ge(weighted, u0 + (n + 1))
                            nc.vector.tensor_tensor_scan(out=hs[:, n % 2, :], data0=da[:, n % 2, :], data1=dbx[n % 2],
                                                         initial=0.0, op0=ALU.mult, op1=ALU.add).then_inc(scanned, 1)
                            if c and n == 1:
                                finish(c - 1)
                    finish(CT - 1)
                    dve.wait_ge(y_taken, v * CT + (CT + 1))
                    nc.vector.tensor_tensor(xs[:, :, :], xs[:, :, :], sz[:, :, :], ALU.mult).then_inc(gated, 1)
                    dve.wait_ge(out_summed, v + 1)
                    nc.vector.tensor_tensor(
                        ln.split(res[:, :, ds(q * QW, QW)]), ln.split(res[:, :, ds(q * QW, QW)]),
                        PS[0:P, 0:4, 0:HW].rearrange("p (k b) t -> p k b t", b=2), ALU.add).then_inc(res_ready, 1)
                    dve.wait_ge(res_ready, v + 1)
                nc.vector.sem_inc(layer_done, 1)
            dve.wait_ge(loaded, 32)
            with dve.Fori(0, NQ) as q:
                v = q + (NQ + L * NQ + 1)
                nc.vector.sem_inc(ln.x_ready, 1)
                ln.dve(nc, dve, v, res[:, :, ds(q * QW, QW)], hn[:, :, :])
                dve.wait_ge(ln.normed, v)
                for m in range(KD):
                    op = nc.vector.tensor_scalar(hn[:, m, :], hn[:, m, :], fvec[:, 0, m:m + 1], fvec[:, 1, m:m + 1],
                                                 ALU.mult, ALU.add)
                op.then_inc(gained, 1)
                dve.wait_ge(gained, q + (L * NQ + 1))
                nc.vector.tensor_tensor(h[:, :, ds(q * QW, QW)], h[:, :, ds(q * QW, QW)], hn[:, :, :], ALU.add)\
                    .then_inc(h_ready, 1)
                dve.wait_ge(h_ready, q + 1)


def experts(nc, dr, PS, C, h):
    E, EH = 8, 192
    G = E + 1
    TW = 94
    NT = N // TW
    SC = FF // 128
    NU = E * KD + SC
    with ExitStack() as ctx:
        s = Scope(nc, ctx, "moe")
        x = s.sb("x", [P, KD, N])
        xb = s.sb("xb", [P, KD, PAIR])
        wr = s.sb("wr", [P, KD, G])
        wg = s.sb("wg", [P, KD, E * EH])
        wu = s.sb("wu", [P, KD, E * EH])
        wd = s.sb("wd", [P, E * KD, D])
        wsg = s.sb("wsg", [P, KD, FF])
        wsu = s.sb("wsu", [P, KD, FF])
        wsd = s.sb("wsd", [128, SC, D])
        sgb = s.sb("sgb", [TW, 1])
        rank = s.sb("rank", [TW, E])
        pick = s.sb("pick", [G, G * 128])
        lg = s.sb("lg", [TW, NT, G])
        pr = s.sb("pr", [TW, NT, E])
        pr2 = s.sb("pr2", [TW, NT, E])
        c1 = s.sb("c1", [TW, NT, E])
        c2 = s.sb("c2", [TW, NT, E])
        m1 = s.sb("m1", [TW, NT])
        m2 = s.sb("m2", [TW, NT])
        mm_ = s.sb("mm_", [TW, NT])
        al = s.sb("al", [TW, NT])
        gates = s.sb("gates", [TW, NT, G])
        gT = s.sb("gT", [G, N])
        sg = s.sb("sg", [128, 2, PAIR])
        gu = s.sb("gu", [128, 2, PAIR])
        hid = s.sb("hid", [128, 2, PAIR])
        ln = Norm(s, "ln", 1, PAIR, PS[0:P, 0:1, 0:PAIR], PS[0:P, 1:2, 0:PAIR], C.ones, C.eps5)
        small, loaded, routed, logits, kept, shifted, exped, step, al_in, al_exp, gates_ready, turned, gT_ready, \
            gb_ready, gu_summed, silu_ready, gu_ready, hid_ready, down_done, out_summed, h_ready = s.sems(
                "small", "loaded", "routed", "logits", "kept", "shifted", "exped", "step", "al_in", "al_exp",
                "gates_ready", "turned", "gT_ready", "gb_ready", "gu_summed", "silu_ready", "gu_ready", "hid_ready",
                "down_done", "out_summed", "h_ready")
        gate_asked = s.sem("gate_asked")
        smalls = [(wr[:, :, :], "moe_wr"), (rank[:, :], "moe_rank"), (pick[:, :], "moe_pick")]
        bigs = [(wg[:, :, :], "moe_wg"), (wu[:, :, :], "moe_wu"), (wd[:, :, :], "moe_wd"), (wsg[:, :, :], "moe_wsg"),
                (wsu[:, :, :], "moe_wsu"), (wsd[:, :, :], "moe_wsd")]
        NS, NBIG = 16 * (len(smalls) + 1), 16 * len(bigs)
        gcols = [slice(t % 5 * TW, (t % 5 + 1) * TW) for t in range(NT)]
        block = ctx.enter_context(nc.Block())

        @block.sync
        def _(sp):
            sp.dma_start(sgb[:, :], dr["moe_sgb"].partition_broadcast(TW)).then_inc(small, 16)
            for dst, name in smalls:
                sp.dma_start(dst, dr[name]).then_inc(small, 16)
            for dst, name in bigs:
                sp.dma_start(dst, dr[name]).then_inc(loaded, 16)
            sp.wait_ge(loaded, NBIG)

        @block.tensor
        def _(pe):
            pe.wait_ge(small, NS)
            with pe.Fori(0, NPAIR) as i:
                ln.pe(nc, pe, i + 1, lambda k, at, w: h[:, k, ds(i * PAIR + at, w)])
                pe.wait_ge(ln.normed, i + 1)
                for t in range(3):
                    for k in range(KD):
                        mm = nc.tensor.matmul(PS[0:TW, 4, t * G:(t + 1) * G], xb[:, k, t * TW:(t + 1) * TW],
                                              wr[:, k, :], start=k == 0, stop=k == KD - 1)
                mm.then_inc(routed, 1)
            pe.wait_ge(gates_ready, 1)
            for t in range(NT):
                mm = nc.tensor.transpose(PS[0:G, t // 5, gcols[t]], gates[:, t, :], C.ident[0:TW, 0:TW])
            mm.then_inc(turned, 1)
            pe.wait_ge(gT_ready, 1)
            pe.wait_ge(loaded, NBIG)
            pe.wait_ge(kept, NPAIR + 1)
            with pe.Fori(0, NPAIR) as i:
                cols = ds(i * PAIR, PAIR)

                def down(u):
                    if u == 0:
                        pe.wait_ge(h_ready, i + 1)
                    pe.wait_ge(hid_ready, i * NU + (u + 2))
                    for m in range(KD):
                        if u < E * KD:
                            w, hd = wd[:, u, m * P:(m + 1) * P], hid[0:P, u % 2, :]
                        else:
                            w, hd = wsd[:, u - E * KD, m * P:(m + 1) * P], hid[:, u % 2, :]
                        mm = nc.tensor.matmul(PS[0:P, 6 + m, 0:PAIR], w, hd, start=u == 0, stop=u == NU - 1)
                    mm.then_inc(down_done, 1)
                    return mm

                for u in range(NU):
                    g = min(u // KD, E)
                    if u == g * KD:
                        pe.wait_ge(hid_ready, i * NU + (max(0, 2 * g - 2) + 1))
                        nc.tensor.sem_inc(gate_asked, 1)
                        nc.tensor.matmul(PS[:, 4 + g % 2, 0:PAIR], pick[:, g * 128:(g + 1) * 128], gT[:, cols],
                                         start=True, stop=True).then_inc(gb_ready, 1)
                    pe.wait_ge(gu_ready, i * NU + (u + 1))
                    for b, w in enumerate((wg, wu) if u < E * KD else (wsg, wsu)):
                        M = P if u < E * KD else 128
                        at = u * P if u < E * KD else (u - E * KD) * 128
                        for k in range(KD):
                            mm = nc.tensor.matmul(PS[0:M, u % 2 * 2 + b, 0:PAIR], w[:, k, at:at + M], x[:, k, cols],
                                                  start=k == 0, stop=k == KD - 1)
                    mm.then_inc(gu_summed, 1)
                    if u >= 2:
                        down(u - 2)
                down(NU - 2)
                down(NU - 1)

        @block.scalar
        def _(act):
            with act.Fori(0, NPAIR) as i:
                ln.act(nc, act, i + 1)
                act.wait_ge(routed, i + 1)
                nc.scalar.activation(lg[:, ds(i * 3, 3), :], PS[0:TW, 4, 0:3 * G].rearrange("p (t g) -> p t g", g=G),
                                     ACT.Copy).then_inc(logits, 1)
            act.wait_ge(shifted, 1)
            nc.scalar.activation(pr[:, :, :], pr[:, :, :], ACT.Exp).then_inc(exped, 1)
            act.wait_ge(al_in, 1)
            nc.scalar.activation(al[:, :], al[:, :], ACT.Exp, scale=-1.0).then_inc(al_exp, 1)
            act.wait_ge(turned, 1)
            full = NT // 5
            nc.scalar.activation(gT[:, 0:full * 5 * TW].rearrange("p (a t) -> p a t", a=full),
                                 PS[0:G, 0:full, 0:5 * TW], ACT.Copy)
            nc.scalar.activation(gT[:, full * 5 * TW:N], PS[0:G, full, 0:(NT - full * 5) * TW], ACT.Copy)\
                .then_inc(gT_ready, 1)
            with act.Fori(0, NPAIR) as i:
                for u in range(NU):
                    M = P if u < E * KD else 128
                    act.wait_ge(gu_summed, i * NU + (u + 1))
                    act.wait_ge(gu_ready, i * NU + (u + 1))
                    nc.scalar.activation(sg[0:M, u % 2, :], PS[0:M, u % 2 * 2, 0:PAIR], ACT.Silu)\
                        .then_inc(silu_ready, 1)

        @block.gpsimd
        def _(pool):
            with pool.Fori(0, NPAIR) as i:
                pool.wait_ge(ln.normed, i + 1)
                nc.gpsimd.tensor_copy(x[:, :, ds(i * PAIR, PAIR)], xb[:, :, :]).then_inc(kept, 1)

        @block.vector
        def _(dve):
            nc.vector.sem_inc(gu_ready, 2)
            nc.vector.sem_inc(hid_ready, 1)
            nc.vector.sem_inc(down_done, 2)
            nc.vector.sem_inc(h_ready, 1)
            nc.vector.sem_inc(kept, 1)
            with dve.Fori(0, NPAIR) as i:
                nc.vector.sem_inc(ln.x_ready, 1)
                dve.wait_ge(kept, i + 1)
                ln.dve(nc, dve, i + 1, h[:, :, ds(i * PAIR, PAIR)], xb[:, :, :])
            dve.wait_ge(small, NS)
            dve.wait_ge(logits, NPAIR)
            steps = [0]

            def link(op):
                steps[0] += 1
                op.then_inc(step, 1)
                dve.wait_ge(step, steps[0])

            V = nc.vector
            sh = [TW, NT, E]
            rk = bcast(rank[:, :], 1, sh)
            link(V.reduce_max(m1[:, :], lg[:, :, 0:E], AX.X))
            V.tensor_tensor(pr[:, :, :], lg[:, :, 0:E], bcast(m1[:, :], 2, sh), ALU.subtract).then_inc(shifted, 1)
            V.tensor_scalar(al[:, :], lg[:, :, E], sgb[:, 0:1], None, ALU.add).then_inc(al_in, 1)
            dve.wait_ge(exped, 1)
            link(V.reduce_sum(m1[:, :], pr[:, :, :], AX.X))
            link(V.reciprocal(m1[:, :], m1[:, :]))
            link(V.tensor_tensor(pr[:, :, :], pr[:, :, :], bcast(m1[:, :], 2, sh), ALU.mult))
            link(V.reduce_max(m1[:, :], pr[:, :, :], AX.X))
            link(V.tensor_tensor(c1[:, :, :], pr[:, :, :], bcast(m1[:, :], 2, sh), ALU.is_equal))
            link(V.tensor_tensor(c1[:, :, :], c1[:, :, :], rk, ALU.mult))
            link(V.reduce_max(mm_[:, :], c1[:, :, :], AX.X))
            link(V.tensor_tensor(c1[:, :, :], c1[:, :, :], bcast(mm_[:, :], 2, sh), ALU.is_equal))
            link(V.scalar_tensor_tensor(out=pr2[:, :, :], in0=c1[:, :, :], scalar=-2.0, in1=pr[:, :, :],
                                        op0=ALU.mult, op1=ALU.add))
            link(V.reduce_max(m2[:, :], pr2[:, :, :], AX.X))
            link(V.tensor_tensor(c2[:, :, :], pr2[:, :, :], bcast(m2[:, :], 2, sh), ALU.is_equal))
            link(V.tensor_tensor(c2[:, :, :], c2[:, :, :], rk, ALU.mult))
            link(V.reduce_max(mm_[:, :], c2[:, :, :], AX.X))
            link(V.tensor_tensor(c2[:, :, :], c2[:, :, :], bcast(mm_[:, :], 2, sh), ALU.is_equal))
            link(V.tensor_tensor(mm_[:, :], m1[:, :], m2[:, :], ALU.add))
            link(V.reciprocal(mm_[:, :], mm_[:, :]))
            dve.wait_ge(al_exp, 1)
            link(V.tensor_scalar(al[:, :], al[:, :], 1.0, None, ALU.add))
            link(V.reciprocal(gates[:, :, E], al[:, :]))
            link(V.tensor_scalar(al[:, :], gates[:, :, E], -1.0, 1.0, ALU.mult, ALU.add))
            link(V.tensor_tensor(m1[:, :], m1[:, :], mm_[:, :], ALU.mult))
            link(V.tensor_tensor(m2[:, :], m2[:, :], mm_[:, :], ALU.mult))
            link(V.tensor_tensor(c1[:, :, :], c1[:, :, :], bcast(m1[:, :], 2, sh), ALU.mult))
            link(V.tensor_tensor(c2[:, :, :], c2[:, :, :], bcast(m2[:, :], 2, sh), ALU.mult))
            link(V.tensor_tensor(c1[:, :, :], c1[:, :, :], c2[:, :, :], ALU.add))
            V.tensor_tensor(gates[:, :, 0:E], c1[:, :, :], bcast(al[:, :], 2, sh), ALU.mult).then_inc(gates_ready, 1)
            with dve.Fori(0, NPAIR) as i:
                for u in range(NU):
                    M = P if u < E * KD else 128
                    g = min(u // KD, E)
                    U = i * NU + u
                    dve.wait_ge(silu_ready, U + 1)
                    V.tensor_tensor(gu[0:M, u % 2, :], sg[0:M, u % 2, :], PS[0:M, u % 2 * 2 + 1, 0:PAIR], ALU.mult)\
                        .then_inc(gu_ready, 1)
                    dve.wait_ge(gu_ready, U + 3)
                    dve.wait_ge(gb_ready, i * G + (g + 1))
                    dve.wait_ge(down_done, U + 1)
                    V.tensor_tensor(hid[0:M, u % 2, :], gu[0:M, u % 2, :], PS[0:M, 4 + g % 2, 0:PAIR], ALU.mult)\
                        .then_inc(hid_ready, 1)
                dve.wait_ge(down_done, i * NU + (NU + 2))
                V.tensor_tensor(h[:, :, ds(i * PAIR, PAIR)], h[:, :, ds(i * PAIR, PAIR)], PS[0:P, 6:8, 0:PAIR],
                                ALU.add).then_inc(h_ready, 1)
            dve.wait_ge(h_ready, NPAIR + 1)


def attention(nc, dr, PS, C, h):
    TT = 71
    PT = 2 * TT
    STEP = 0.5 * DH ** -0.5
    TILT = STEP * DH ** -0.5
    EG = 8
    SH = 2 * NH
    with ExitStack() as ctx:
        s = Scope(nc, ctx, "att")
        wqk = s.sb("wqk", [P, KD, 2, QC * 128])
        wk = s.sb("wk", [P, KD, D])
        wv = s.sb("wv", [P, KD, QC * 128])
        wo = s.sb("wo", [128, QC, D])
        bo = s.sb("bo", [P, KD])
        mean_sel = s.sb("mean_sel", [128, 2, HP])
        xn = s.sb("xn", [P, KD, B, PT])
        cur = s.sb("cur", [P, KD, PT])
        qk = s.sb("qk", [128, 2, QC, PT])
        qs = s.sb("qs", [128, 4, QC, PT])
        keys = s.sb("keys", [TT, 2, D])
        tilt = s.sb("tilt", [128, 2, NH, 2, DH])
        spread_sel = s.sb("spread_sel", [2 * DH, 4, 128])
        v = s.sb("v", [128, 2, QC * 128])
        wvt = s.sb("wvt", [128, 2, 2, 2, DH, DH])
        ex = s.sb("ex", [TT, 3, 2, PT])
        mx = s.sb("mx", [TT, 3, 2])
        eT = s.sb("eT", [128, 3, 2, PT])
        inv = s.sb("inv", [2 * DH, 2, T])
        rb = s.sb("rb", [128, 2, 2, T])
        rat = s.sb("rat", [128, 2, 2, T])
        dif = s.sb("dif", [128, 2, T])
        absd = s.sb("absd", [128, 2, T])
        acc = s.sb("acc", [128, NH, 2])
        oT = s.sb("oT", [128, QC, PT])
        ln = Norm(s, "ln", 1, PAIR, PS[0:P, 2:3, 0:PAIR], PS[0:P, 3:4, 0:PAIR], C.ones, C.eps5)
        nb = s.sb("nb", [P, KD, PAIR])
        loaded, padded, qk_summed, qk_ready, kv_summed, keys_ready, tilt_ready, v_ready, scored, maxed, shifted, exped, e_ready, \
            turned, eT_ready, wvt_ready, weights_summed, sums_ready, inverted, spread, rb_ready, ratio, differed, \
            acc_ready, w_summed, qs_ready, rowinv, mixed, oT_ready, projected, h_ready = s.sems(
                "loaded", "padded", "qk_summed", "qk_ready", "kv_summed", "keys_ready", "tilt_ready", "v_ready", "scored", "maxed",
                "shifted", "exped", "e_ready", "turned", "eT_ready", "wvt_ready", "weights_summed", "sums_ready",
                "inverted", "spread", "rb_ready", "ratio", "differed", "acc_ready", "w_summed", "qs_ready", "rowinv", "mixed", "oT_ready",
                "projected", "h_ready")
        xn_ready, cur_ready, cur_used, entered = s.sems("xn_ready", "cur_ready", "cur_used", "entered")
        loads = [(wqk[:, :, :, :], "att_wqk"), (wk[:, :, :], "att_wk"), (wv[:, :, :], "att_wv"), (wo[:, :, :], "att_wo"),
                 (bo[:, :], "att_bo"), (mean_sel[:, :, :], "att_sel"), (spread_sel[:, :, :], "att_spread")]
        NLD, PADS = 16 * len(loads), 7
        acc_j = acc[:, :, :].rearrange("p (c j) g -> p j c g", j=4)
        block = ctx.enter_context(nc.Block())

        @block.sync
        def _(sp):
            for dst, name in loads:
                sp.dma_start(dst, dr[name]).then_inc(loaded, 16)
            sp.wait_ge(loaded, NLD)

        @block.tensor
        def _(pe):
            pe.wait_ge(loaded, NLD)
            pe.wait_ge(padded, PADS)
            with pe.Fori(0, NPAIR) as i:
                ln.pe(nc, pe, i + 1, lambda k, at, w: h[:, k, ds(i * PAIR + at, w)])
            pe.wait_ge(xn_ready, NPAIR + 1)
            nc.tensor.sem_inc(entered, 1)
            with pe.Fori(0, B) as i:
                pe.wait_ge(h_ready, i + 1)
                pe.wait_ge(cur_ready, i + 1)
                nc.tensor.sem_inc(entered, 1)
                for a in range(2):
                    for c in range(QC):
                        for k in range(KD):
                            mm = nc.tensor.matmul(PS[:, a, c * PT:(c + 1) * PT], wqk[:, k, a, c * 128:(c + 1) * 128],
                                                  cur[:, k, :], start=k == 0, stop=k == KD - 1)
                mm.then_inc(qk_summed, 1)
                for bank, w, n in ((4, wk, D), (6, wv, QC * 128)):
                    for t in range(2):
                        for k in range(KD):
                            mm = nc.tensor.matmul(PS[0:TT, bank + t, 0:n], cur[:, k, t * TT:(t + 1) * TT], w[:, k, :],
                                                  start=k == 0, stop=k == KD - 1)
                mm.then_inc(kv_summed, 1)
                nc.tensor.sem_inc(cur_used, 1)
                pe.wait_ge(qk_ready, i + 1)

                def score(p, n):
                    H = i * SH + (p * NH + n)
                    c, r = n // 4, slice(HP * (n % 4), HP * (n % 4 + 1))
                    pe.wait_ge(shifted, H + 1)
                    for t in range(2):
                        q = qk[r, 0, c, t * TT:(t + 1) * TT] if p == 0 else qs[:, n % 4, c, t * TT:(t + 1) * TT]
                        k = qk[r, 1, c, 0:T] if p == 0 else qk[:, 1, c, 0:T]
                        mm = nc.tensor.matmul(PS[0:TT, n % 2, t * PT:t * PT + T], q, k, start=True, stop=True)
                    mm.then_inc(scored, 1)

                def turn(p, n):
                    H = i * SH + (p * NH + n)
                    pe.wait_ge(e_ready, H + 1)
                    pe.wait_ge(eT_ready, H + 1)
                    if p == 0 and n >= 2:
                        pe.wait_ge(inverted, i * NH + (n - 1))
                    for t in range(2):
                        for kt in range(2):
                            at = kt * PT + t * TT
                            mm = nc.tensor.transpose(PS[0:TT, 2 + n % 2, at:at + TT],
                                                     ex[:, n % 3, t, kt * TT:(kt + 1) * TT], C.ident[0:TT, 0:TT])
                    mm.then_inc(turned, 1)

                def spread_of(m):
                    pe.wait_ge(inverted, i * NH + (m + 1))
                    if m == 0:
                        pe.wait_ge(v_ready, i + 1)
                    for g in range(2):
                        pe.wait_ge(rb_ready, (i * NH + m) * 2 + (g + 1))
                        for sign in range(2):
                            mm = nc.tensor.matmul(PS[:, 6 + g, sign * PT:sign * PT + T],
                                                  spread_sel[:, 2 * g + sign, :], inv[:, m % 2, :],
                                                  start=True, stop=True)
                        mm.then_inc(spread, 1)

                def weights_of(m):
                    pe.wait_ge(eT_ready, i * SH + (m + 3))
                    pe.wait_ge(tilt_ready, i + 1)
                    for kt in range(2):
                        mm = nc.tensor.matmul(PS[0:2 * DH, 2 + m % 2, 2 * PT:2 * PT + T],
                                              tilt[:, kt, m, :, :].rearrange("p s e -> p (s e)"),
                                              eT[:, m % 3, kt, 0:T], start=kt == 0, stop=kt == 1)
                    mm.then_inc(weights_summed, 1)

                def values_of(m):
                    pe.wait_ge(wvt_ready, i * NH + (m + 1))
                    for g in range(2):
                        pe.wait_ge(ratio, (i * NH + m) * 2 + (g + 1))
                        for sign in range(2):
                            for kt in range(2):
                                mm = nc.tensor.matmul(
                                    PS[:, 4 + g, sign * PT:sign * PT + T],
                                    wvt[:, m % 2, kt, sign, g * EG:(g + 1) * EG, :].rearrange("p e d -> p (e d)"),
                                    eT[:, m % 3, kt, 0:T], start=kt == 0, stop=kt == 1)
                        mm.then_inc(sums_ready, 1)

                for n in range(NH + 3):
                    if n < NH:
                        score(0, n)
                    if 1 <= n <= NH:
                        turn(0, n - 1)
                    if n >= 3:
                        spread_of(n - 3)
                    if 2 <= n <= NH + 1:
                        weights_of(n - 2)
                    if n >= 3:
                        values_of(n - 3)
                pe.wait_ge(acc_ready, (i + 1) * 2 * NH)
                for j in range(4):
                    for g in range(2):
                        mm = nc.tensor.matmul(PS[HP * j:HP * (j + 1), 4, 0:QC], mean_sel[:, g, :], acc_j[:, j, :, g],
                                              start=g == 0, stop=g == 1)
                mm.then_inc(w_summed, 1)
                pe.wait_ge(qs_ready, i + 1)
                for n in range(NH + 3):
                    if n < NH:
                        score(1, n)
                    if 2 <= n <= NH + 1:
                        turn(1, n - 2)
                    if n >= 3:
                        m = n - 3
                        pe.wait_ge(eT_ready, i * SH + (NH + m + 3))
                        for kt in range(2):
                            mm = nc.tensor.matmul(PS[HP * (m % 4):HP * (m % 4 + 1), 5, m // 4 * PT:(m // 4 + 1) * PT],
                                                  v[:, kt, m * HP:(m + 1) * HP], eT[:, m % 3, kt, :],
                                                  start=kt == 0, stop=kt == 1)
                        mm.then_inc(mixed, 1)
                pe.wait_ge(oT_ready, i + 1)
                for m in range(KD):
                    for c in range(QC):
                        mm = nc.tensor.matmul(PS[0:P, 6, m * PT:m * PT + T], wo[:, c, m * P:(m + 1) * P],
                                              oT[:, c, 0:T], start=c == 0, stop=c == QC - 1)
                mm.then_inc(projected, 1)

        @block.scalar
        def _(act):
            with act.Fori(0, NPAIR) as i:
                ln.act(nc, act, i + 1)
            with act.Fori(0, B) as i:
                act.wait_ge(qk_summed, i + 1)
                nc.scalar.activation(qk[:, :, :, :].rearrange("p a c t -> p a (c t)"), PS[:, 0:2, 0:QC * PT], ACT.Copy)\
                    .then_inc(qk_ready, 1)
                act.wait_ge(kv_summed, i + 1)
                nc.scalar.activation(keys[:, :, :], PS[0:TT, 4:6, 0:D], ACT.Copy).then_inc(keys_ready, 1)
                act.wait_ge(keys_ready, i + 1)

                for sign in range(2):
                    op = nc.scalar.activation(tilt[0:TT, :, :, sign, :],
                                              keys[:, :, :].rearrange("p a (n e) -> p a n e", e=DH), ACT.Exp,
                                              scale=TILT * (1 - 2 * sign))
                op.then_inc(tilt_ready, 1)

                def exp_of(p, n):
                    H = i * SH + (p * NH + n)
                    act.wait_ge(shifted, H + 3)
                    if p == 0:
                        nc.scalar.activation(ex[:, n % 3, :, 0:T], ex[:, n % 3, :, 0:T], ACT.Exp, scale=DH ** -0.5)\
                            .then_inc(e_ready, 1)
                    else:
                        for t in range(2):
                            op = nc.scalar.activation(ex[:, n % 3, t, 0:T], ex[:, n % 3, t, 0:T], ACT.Exp,
                                                      scale=DH ** -0.5, accum_out=mx[:, n % 3, t:t + 1])
                        op.then_inc(exped, 1)

                def keep_turned(p, n):
                    H = i * SH + (p * NH + n)
                    act.wait_ge(turned, H + 1)
                    if p == 0:
                        act.wait_ge(sums_ready, (i * NH + n) * 2 + 2)
                    elif n < 3:
                        act.wait_ge(sums_ready, (i + 1) * 2 * NH + 6)
                    else:
                        act.wait_ge(mixed, i * NH + (n - 2))
                    nc.scalar.activation(eT[0:TT, n % 3, :, :].rearrange("p a t -> p (a t)"),
                                         PS[0:TT, 2 + n % 2, 0:2 * PT], ACT.Copy).then_inc(eT_ready, 1)

                for n in range(NH + 4):
                    if 1 <= n <= NH:
                        keep_turned(0, n - 1)
                    if 3 <= n <= NH + 2:
                        for g in range(2):
                            M = (i * NH + (n - 3)) * 2 + g
                            act.wait_ge(spread, M + 1)
                            act.wait_ge(ratio, M + 1)
                            nc.scalar.activation(rb[:, g, :, :], PS[:, 6 + g, 0:2 * PT].rearrange(
                                "p (a t) -> p a t", t=PT)[:, :, 0:T], ACT.Copy).then_inc(rb_ready, 1)
                    if n < NH:
                        exp_of(0, n)
                    if n >= 4:
                        m = n - 4
                        for g in range(2):
                            act.wait_ge(differed, (i * NH + m) * 2 + (g + 1))
                            nc.scalar.activation(absd[:, g, :], dif[:, g, :], ACT.Abs, accum_out=acc[:, m, g:g + 1])\
                                .then_inc(acc_ready, 1)
                for n in range(NH + 2):
                    if n < NH:
                        exp_of(1, n)
                    if n >= 2:
                        keep_turned(1, n - 2)
                act.wait_ge(mixed, (i + 1) * NH)
                nc.scalar.activation(oT[:, :, :].rearrange("p c t -> p (c t)"), PS[:, 5, 0:QC * PT], ACT.Copy)\
                    .then_inc(oT_ready, 1)

        @block.gpsimd
        def _(pool):
            pool.memset(xn[:, :, :, T:PT], 0.0).then_inc(padded, 1)
            pool.memset(ex[:, :, :, T:PT], 0.0).then_inc(padded, 1)
            pool.memset(tilt[:, :, :, :, :], 0.0).then_inc(padded, 1)
            pool.memset(wvt[:, :, :, :, :, :], 0.0).then_inc(padded, 1)
            pool.memset(v[:, :, :], 0.0).then_inc(padded, 1)
            pool.memset(qs[:, :, :, :], 0.0).then_inc(padded, 1)
            pool.memset(eT[:, :, :, :], 0.0).then_inc(padded, 1)
            pool.wait_ge(padded, PADS)
            pool.sem_inc(xn_ready, 1)
            with pool.Fori(0, NPAIR) as i:
                pool.wait_ge(ln.normed, i + 1)
                pool.tensor_copy(xn[:, :, ds(i * 2, 2), 0:T], nb[:, :, :].rearrange("p k (a t) -> p k a t", t=T))\
                    .then_inc(xn_ready, 1)
            with pool.Fori(0, B) as i:
                pool.wait_ge(cur_used, i + 1)
                pool.tensor_copy(cur[:, :, :], xn[:, :, ds(i, 1), :].rearrange("p k a t -> p k (a t)")).then_inc(cur_ready, 1)
                pool.wait_ge(v_ready, i + 1)
                pool.wait_ge(tilt_ready, i + 1)
                for n in range(NH):
                    pool.wait_ge(sums_ready, (i * NH + n) * 2 + 4)
                    for kt in range(2):
                        op = nc.gpsimd.tensor_tensor(
                            wvt[0:TT, n % 2, kt, :, :, :].rearrange("p s e d -> p (s e) d"),
                            bcast(tilt[0:TT, kt, n, :, :].rearrange("p s e -> p (s e)"), 2, [TT, 2 * DH, DH]),
                            bcast(v[0:TT, kt, n * HP:n * HP + DH], 1, [TT, 2 * DH, DH]), ALU.mult)
                    op.then_inc(wvt_ready, 1)

        @block.vector
        def _(dve):
            V = nc.vector
            V.sem_inc(shifted, 2)
            V.sem_inc(eT_ready, 2)
            V.sem_inc(ratio, 2)
            V.sem_inc(rb_ready, 2)
            V.sem_inc(sums_ready, 6)
            V.sem_inc(h_ready, 1)
            V.sem_inc(cur_used, 1)
            with dve.Fori(0, NPAIR) as i:
                V.sem_inc(ln.x_ready, 1)
                dve.wait_ge(xn_ready, i + 1)
                ln.dve(nc, dve, i + 1, h[:, :, ds(i * PAIR, PAIR)], nb[:, :, :])
                dve.wait_ge(ln.normed, i + 1)
            with dve.Fori(0, B) as i:
                dve.wait_ge(kv_summed, i + 1)
                V.tensor_copy(v[0:TT, :, :], PS[0:TT, 6:8, 0:QC * 128]).then_inc(v_ready, 1)

                def shift(p, n):
                    H = i * SH + (p * NH + n)
                    dve.wait_ge(scored, H + 1)
                    sc = PS[0:TT, n % 2, 0:2 * PT].rearrange("p (a t) -> p a t", t=PT)[:, :, 0:T]
                    V.reduce_max(mx[:, n % 3, :], sc, AX.X).then_inc(maxed, 1)
                    dve.wait_ge(maxed, H + 1)
                    if p == 1 or n >= 3:
                        dve.wait_ge(turned, H - 2)
                    V.tensor_tensor(ex[:, n % 3, :, 0:T], sc, bcast(mx[:, n % 3, :], 2, [TT, 2, T]), ALU.subtract)\
                        .then_inc(shifted, 1)

                for n in range(NH + 3):
                    if n < NH:
                        shift(0, n)
                    if 2 <= n <= NH + 1:
                        m = n - 2
                        dve.wait_ge(weights_summed, i * NH + (m + 1))
                        V.reciprocal(inv[:, m % 2, :], PS[0:2 * DH, 2 + m % 2, 2 * PT:2 * PT + T]).then_inc(inverted, 1)
                    if n >= 3:
                        m = n - 3
                        M = (i * NH + m) * 2
                        for g in range(2):
                            dve.wait_ge(sums_ready, M + (g + 7))
                            dve.wait_ge(rb_ready, M + (g + 3))
                            if m >= 1:
                                dve.wait_ge(differed, M + (g - 1))
                            V.tensor_tensor(rat[:, g, :, :], rb[:, g, :, :], PS[:, 4 + g, 0:2 * PT].rearrange(
                                "p (a t) -> p a t", t=PT)[:, :, 0:T], ALU.mult).then_inc(ratio, 1)
                        for g in range(2):
                            dve.wait_ge(ratio, M + (g + 3))
                            if m >= 1:
                                dve.wait_ge(acc_ready, M + (g - 1))
                            V.tensor_tensor(dif[:, g, :], rat[:, g, 0, :], rat[:, g, 1, :], ALU.subtract)\
                                .then_inc(differed, 1)
                dve.wait_ge(w_summed, i + 1)
                for j in range(4):
                    r = slice(HP * j, HP * (j + 1))
                    op = V.tensor_tensor(qs[r, j, :, :], qk[r, 0, :, :], bcast(PS[r, 4, 0:QC], 2, [HP, QC, PT]),
                                         ALU.mult)
                op.then_inc(qs_ready, 1)
                for n in range(NH + 1):
                    if n < NH:
                        shift(1, n)
                    if n >= 1:
                        m = n - 1
                        dve.wait_ge(exped, i * NH + (m + 1))
                        V.reciprocal(mx[:, m % 3, :], mx[:, m % 3, :]).then_inc(rowinv, 1)
                        dve.wait_ge(rowinv, i * NH + (m + 1))
                        V.tensor_tensor(ex[:, m % 3, :, 0:T], ex[:, m % 3, :, 0:T],
                                        bcast(mx[:, m % 3, :], 2, [TT, 2, T]), ALU.mult).then_inc(e_ready, 1)
                dve.wait_ge(projected, i + 1)
                for m in range(KD):
                    op = V.scalar_tensor_tensor(out=h[:, m, ds(i * T, T)], in0=PS[0:P, 6, m * PT:m * PT + T],
                                                scalar=bo[:, m:m + 1], in1=h[:, m, ds(i * T, T)],
                                                op0=ALU.add, op1=ALU.add)
                op.then_inc(h_ready, 1)
                dve.wait_ge(h_ready, i + 2)


def switch(nc, dr, PS, C, h):
    E, CAP = 16, 64
    TW = 94
    NT = N // TW
    BLOCKS = [(0, 0), (0, 1), (1, 1), (1, 2), (2, 2)]
    TR = 128
    ET = B * CAP // TR
    U = 4
    TILES = -(-(N // TR + E) // U) * U
    BEHIND = (TILES + 1) * TR
    with ExitStack() as ctx:
        s = Scope(nc, ctx, "sw")
        slots = nc.dram_tensor("sw_slots", (BEHIND + N, D), F32, kind="Internal").ap()
        xb = s.sb("xb", [P, KD, PAIR])
        nb = s.sb("nb", [P, KD, PAIR])
        lnw = s.sb("lnw", [P, KD])
        wr = s.sb("wr", [P, KD, E])
        wi = s.sb("wi", [P, U, KD, FF])
        wo = s.sb("wo", [128, U, FC, D])
        zero = s.sb("zero", [TR, D])
        token = s.sb("token", [TW, NT])
        carry = s.sb("carry", [TW, E, NT])
        every = s.sb("every", [TW, TW])
        filled = s.sb("filled", [TW, ET])
        tile_no = s.sb("tile_no", [1, TILES])
        normed = s.sb("normed", [TW, NT, D])
        oh = s.sb("oh", [TW, NT, E])
        kept = s.sb("kept", [TW, NT, E])
        totals = s.sb("totals", [TW, E, NT])
        sofar = s.sb("sofar", [TW, E, NT])
        full = s.sb("full", [TW, E, ET])
        ntiles = s.sb("ntiles", [TW, E])
        tiles_to = s.sb("tiles_to", [TW, E])
        base = s.sb("base", [TW, E])
        row = s.sb("row", [TW, NT, E])
        dest = s.sb("dest", [TW, NT])
        dest_i = s.sb("dest_i", [TW, NT], I32)
        passed = s.sb("passed", [1, TILES, E])
        whose = s.sb("whose", [1, TILES])
        whose_i = s.sb("whose_i", [1, TILES], I32)
        xt = s.sb("xt", [TR, 2, D])
        xT = s.sb("xT", [P, 2, KD, TR])
        hid = s.sb("hid", [128, 2, FC, TR])
        yt = s.sb("yt", [TR, 2, D])
        back = s.sb("back", [TW, 4, D])
        rank = s.sb("rank", [TW, E])
        upto = s.sb("upto", [TW, len(BLOCKS), TW])
        lg = s.sb("lg", [TW, NT, E])
        m1 = s.sb("m1", [TW, NT])
        m2 = s.sb("m2", [TW, NT])
        eps6 = s.sb("eps6", [P, 1])
        ln = Norm(s, "ln", 1, PAIR, PS[0:P, 0:1, 0:PAIR], PS[0:P, 1:2, 0:PAIR], C.ones, C.eps5)
        rms = Norm(s, "rms", 1, PAIR, None, PS[0:P, 2:3, 0:PAIR], C.ones, eps6, center=False)
        small, eps_ready, summed, weighted, routed, logits, turned, normed_ready, shifted, exped, step, oh_ready, \
            counted, kept_ready, ranked, sorted_, zeroed, scattered, xt_turned, xT_ready, up_summed, hid_ready, \
            down_summed, y_ready, y_free, scaled, back_turned, h_ready, entered, fetched = s.sems(
                "small", "eps_ready", "summed", "weighted", "routed", "logits", "turned", "normed_ready", "shifted",
                "exped", "step", "oh_ready", "counted", "kept_ready", "ranked", "sorted", "zeroed", "scattered",
                "xt_turned", "xT_ready", "up_summed", "hid_ready", "down_summed", "y_ready", "y_free", "scaled",
                "back_turned", "h_ready", "entered", "fetched")
        wloaded = s.sems(*(f"wloaded{b}" for b in range(U)))
        xloaded = s.sems("xloaded0", "xloaded1")
        ystored = s.sems("ystored0", "ystored1")
        gathered = s.sems(*(f"gathered{b}" for b in range(4)))
        smalls = [(lnw[:, :], "sw_lnw"), (wr[:, :, :], "sw_wr"), (rank[:, :], "sw_rank"), (upto[:, :, :], "sw_upto"),
                  (token[:, :], "sw_token"), (carry[:, :, :], "sw_carry"), (every[:, :], "sw_every"),
                  (filled[:, :], "sw_filled"), (tile_no[:, :], "sw_tile_no")]
        NS = 16 * len(smalls)
        block = ctx.enter_context(nc.Block())

        @block.sync
        def _(sp):
            for dst, name in smalls:
                sp.dma_start(dst, dr[name]).then_inc(small, 16)
            sp.wait_ge(zeroed, 1)
            for r0 in range(0, BEHIND + N, TR):
                rows = min(TR, BEHIND + N - r0)
                sp.dma_start(slots[r0:r0 + rows], zero[0:rows, :]).then_inc(zeroed, 16)
            sp.wait_ge(sorted_, 1)
            sp.wait_ge(scattered, 16 * NT)
            sp.dma_start(xt[:, 0, :], slots[0:TR]).then_inc(xloaded[0], 16)
            with sp.Fori(0, TILES // U) as mm:
                for b in range(U):
                    m = mm * U + b
                    sp.wait_ge(down_summed, m + 1)
                    e = sp.value_load(whose_i[0:1, ds(m, 1)], min_val=0, max_val=E - 1)
                    sp.dma_start(wi[:, b, :, :], dr["sw_wi"][ds(e, 1)].rearrange("a p k f -> (a p) k f"))\
                        .then_inc(wloaded[b], 16)
                    sp.dma_start(wo[:, b, :, :], dr["sw_wo"][ds(e, 1)].rearrange("a p k f -> (a p) k f"))\
                        .then_inc(wloaded[b], 16)
                    sp.wait_ge(xt_turned, m + 2)
                    x = (b + 1) % 2
                    sp.dma_start(xt[:, x, :], slots[ds((m + 1) * TR, TR)]).then_inc(xloaded[x], 16)
            for b in range(U):
                sp.wait_ge(wloaded[b], TILES // U * 32)
            sp.wait_ge(xloaded[0], (TILES // 2 + 1) * 16)
            sp.wait_ge(xloaded[1], TILES // 2 * 16)

        @block.tensor
        def _(pe):
            pe.wait_ge(small, NS)
            with pe.Fori(0, NPAIR) as i:
                ln.pe(nc, pe, i + 1, lambda k, at, w: h[:, k, ds(i * PAIR + at, w)])
                rms.pe(nc, pe, i + 1)
                pe.wait_ge(weighted, i + 1)
                for t in range(3):
                    for k in range(KD):
                        mm = nc.tensor.matmul(PS[0:TW, 4, t * E:(t + 1) * E], nb[:, k, t * TW:(t + 1) * TW],
                                              wr[:, k, :], start=k == 0, stop=k == KD - 1)
                mm.then_inc(routed, 1)
                pe.wait_ge(normed_ready, i + 1)
                nc.tensor.sem_inc(entered, 1)
                for t in range(3):
                    for k in range(KD):
                        mm = nc.tensor.transpose(PS[0:TW, 5 + t, k * P:(k + 1) * P], nb[:, k, t * TW:(t + 1) * TW],
                                                 C.ident[0:P, 0:P])
                mm.then_inc(turned, 1)
            pe.wait_ge(oh_ready, 1)
            pe.wait_ge(normed_ready, NPAIR + 1)
            ohp = oh[:, :, :].rearrange("p (i t) e -> p t i e", t=3)
            for t in range(3):
                srcs = [(n, a) for n, (a, b) in enumerate(BLOCKS) if b == t]
                for n, a in srcs:
                    mm = nc.tensor.matmul(PS[0:TW, 5 + t, 0:NPAIR * E], upto[:, n, :], ohp[:, a, :, :],
                                          start=n == srcs[0][0], stop=n == srcs[-1][0])
            mm.then_inc(counted, 1)
            pe.wait_ge(kept_ready, 1)
            nc.tensor.matmul(PS[0:TW, 0, 0:NT * E], upto[:, 0, :], kept[:, :, :], start=True, stop=True)
            nc.tensor.matmul(PS[0:TW, 1, 0:NT * E], every[:, :], kept[:, :, :], start=True, stop=True)\
                .then_inc(ranked, 1)
            pe.wait_ge(sorted_, 1)

            def turn(m, x):
                pe.wait_ge(xT_ready, m + 1)
                nc.tensor.sem_inc(entered, 1)
                for k in range(KD):
                    op = nc.tensor.transpose(PS[0:P, 4 * x, k * TR:(k + 1) * TR], xt[:, x, k * P:(k + 1) * P],
                                             C.ident[:, :])
                op.then_inc(xt_turned, 1)

            pe.wait_ge(xloaded[0], 16)
            turn(0, 0)
            with pe.Fori(0, TILES // U) as mm:
                for b in range(U):
                    m, a = mm * U + b, b % 2
                    pe.wait_ge(xT_ready, m + 3)
                    pe.wait_ge(wloaded[b], mm * 32 + 32)
                    nc.tensor.sem_inc(entered, 1)
                    for j in range(FC):
                        if j % 4 == 0:
                            pe.wait_ge(hid_ready, m * 2 + (j // 4 + 1))
                        for k in range(KD):
                            op = nc.tensor.matmul(PS[:, 4 * a + 1 + j // 4, j % 4 * TR:(j % 4 + 1) * TR],
                                                  wi[:, b, k, j * 128:(j + 1) * 128], xT[:, a, k, :],
                                                  start=k == 0, stop=k == KD - 1)
                        if j in (3, FC - 1):
                            op.then_inc(up_summed, 1)
                    pe.wait_ge(xloaded[1 - a], (mm * 2 + (b + 1) // 2) * 16 + 16 * a if a else mm * 32 + (b // 2) * 16 + 16)
                    turn(m + 1, 1 - a)
                    pe.wait_ge(y_ready, m + 1)
                    for j in range(FC):
                        if j % 4 == 0:
                            pe.wait_ge(hid_ready, m * 2 + (j // 4 + 5))
                            nc.tensor.sem_inc(entered, 1)
                        op = nc.tensor.matmul(PS[:, 4 * a + 3, 0:D], hid[:, a, j, :], wo[:, b, j, :],
                                              start=j == 0, stop=j == FC - 1)
                    op.then_inc(down_summed, 1)
            pe.wait_ge(y_ready, TILES + 2)
            pe.wait_ge(xT_ready, TILES + 3)
            with pe.Fori(0, NT // 4) as tt:
                for o in range(4):
                    pe.wait_ge(scaled, tt * 4 + (o + 1))
                    pe.wait_ge(h_ready, tt * 4 + (o + 1))
                    nc.tensor.sem_inc(entered, 1)
                    for k in range(KD):
                        op = nc.tensor.transpose(PS[0:P, o % 2, k * TW:(k + 1) * TW],
                                                 back[:, o, k * P:(k + 1) * P],
                                                 C.ident[0:TW, 0:TW])
                    op.then_inc(back_turned, 1)

        @block.scalar
        def _(act):
            act.wait_ge(eps_ready, 1)
            with act.Fori(0, NPAIR) as i:
                ln.act(nc, act, i + 1)
                rms.act(nc, act, i + 1, xb[:, :, :])
                act.wait_ge(routed, i + 1)
                nc.scalar.activation(lg[:, ds(i * 3, 3), :], PS[0:TW, 4, 0:3 * E].rearrange("p (t g) -> p t g", g=E),
                                     ACT.Copy).then_inc(logits, 1)
                act.wait_ge(turned, i + 2)
                nc.scalar.activation(normed[:, ds(i * 3, 3), :], PS[0:TW, 5:8, 0:D], ACT.Copy).then_inc(normed_ready, 1)
            act.wait_ge(shifted, 1)
            nc.scalar.activation(lg[:, :, :], lg[:, :, :], ACT.Exp).then_inc(exped, 1)
            act.wait_ge(xt_turned, 3)
            nc.scalar.activation(xT[:, 0, :, :].rearrange("p k t -> p (k t)"), PS[0:P, 0, 0:KD * TR], ACT.Copy)\
                .then_inc(xT_ready, 1)
            with act.Fori(0, TILES // U) as mm:
                for b in range(U):
                    m, a = mm * U + b, b % 2
                    act.wait_ge(down_summed, m + 3)
                    act.wait_ge(up_summed, m * 2 + 1)
                    nc.scalar.activation(hid[:, a, 0:4, :].rearrange("p j t -> p (j t)"), PS[:, 4 * a + 1, :],
                                         ACT.Relu).then_inc(hid_ready, 1)
                    act.wait_ge(up_summed, m * 2 + 2)
                    nc.scalar.activation(hid[:, a, 4:FC, :].rearrange("p j t -> p (j t)"),
                                         PS[:, 4 * a + 2, 0:(FC - 4) * TR], ACT.Relu).then_inc(hid_ready, 1)
                    act.wait_ge(xt_turned, m + 4)
                    nc.scalar.activation(xT[:, 1 - a, :, :].rearrange("p k t -> p (k t)"),
                                         PS[0:P, 4 * (1 - a), 0:KD * TR], ACT.Copy).then_inc(xT_ready, 1)

        @block.gpsimd
        def _(pool):
            pool.memset(zero[:, :], 0.0).then_inc(zeroed, 1)
            pool.wait_ge(zeroed, 1 + 16 * -(-(BEHIND + N) // TR))
            pool.wait_ge(sorted_, 1)
            pool.wait_ge(normed_ready, NPAIR + 1)
            for t in range(NT):
                pool.indirect_dma_start(slots[:, :], bass.IndirectOffsetOnAxis(ap=dest_i[:, t:t + 1], axis=0),
                                        normed[:, t, :], None).then_inc(scattered, 16)
            with pool.Fori(0, TILES // U) as mm:
                for b in range(U):
                    pool.wait_ge(y_ready, mm * U + (b + 3))
                    pool.dma_start(slots[ds((mm * U + b) * TR, TR)], yt[:, b % 2, :]).then_inc(ystored[b % 2], 16)
                    pool.wait_ge(ystored[b % 2], mm * 32 + (b // 2 + 1) * 16)
                    nc.gpsimd.sem_inc(y_free, 1)
            for b in range(2):
                pool.wait_ge(ystored[b], TILES // 2 * 16)
            pool.wait_ge(scattered, 16 * NT)
            for t in range(NT):
                if t >= 4:
                    pool.wait_ge(back_turned, t - 3)
                pool.indirect_dma_start(back[:, t % 4, :], None, slots[:, :],
                                        bass.IndirectOffsetOnAxis(ap=dest_i[:, t:t + 1], axis=0))\
                    .then_inc(gathered[t % 4], 16)
            for b in range(4):
                pool.wait_ge(gathered[b], NT // 4 * 16)

        @block.vector
        def _(dve):
            V = nc.vector
            V.memset(eps6[:, :], 1e-6).then_inc(eps_ready, 1)
            V.sem_inc(normed_ready, 1)
            V.sem_inc(turned, 1)
            V.sem_inc(xt_turned, 2)
            V.sem_inc(xT_ready, 2)
            V.sem_inc(hid_ready, 4)
            V.sem_inc(down_summed, U)
            V.sem_inc(y_ready, 2)
            V.sem_inc(y_free, 2)
            V.sem_inc(h_ready, 2)
            dve.wait_ge(small, NS)
            with dve.Fori(0, NPAIR) as i:
                V.sem_inc(ln.x_ready, 1)
                cols = ds(i * PAIR, PAIR)
                ln.dve(nc, dve, i + 1, h[:, :, cols], xb[:, :, :])
                dve.wait_ge(ln.normed, i + 1)
                V.sem_inc(rms.x_ready, 1)
                V.tensor_tensor(h[:, :, cols], h[:, :, cols], xb[:, :, :], ALU.add).then_inc(summed, 1)
                dve.wait_ge(turned, i + 1)
                rms.dve(nc, dve, i + 1, xb[:, :, :], nb[:, :, :])
                dve.wait_ge(rms.normed, i + 1)
                for m in range(KD):
                    op = V.tensor_scalar(nb[:, m, :], nb[:, m, :], lnw[:, m:m + 1], None, ALU.mult)
                op.then_inc(weighted, 1)
            dve.wait_ge(logits, NPAIR)
            dve.wait_ge(summed, NPAIR)
            steps = [0]

            def link(op):
                steps[0] += 1
                op.then_inc(step, 1)
                dve.wait_ge(step, steps[0])

            sh = [TW, NT, E]
            link(V.reduce_max(m1[:, :], lg[:, :, :], AX.X))
            V.tensor_tensor(lg[:, :, :], lg[:, :, :], bcast(m1[:, :], 2, sh), ALU.subtract).then_inc(shifted, 1)
            dve.wait_ge(exped, 1)
            link(V.reduce_sum(m1[:, :], lg[:, :, :], AX.X))
            link(V.reciprocal(m1[:, :], m1[:, :]))
            link(V.tensor_tensor(lg[:, :, :], lg[:, :, :], bcast(m1[:, :], 2, sh), ALU.mult))
            link(V.reduce_max(m1[:, :], lg[:, :, :], AX.X))
            link(V.tensor_tensor(oh[:, :, :], lg[:, :, :], bcast(m1[:, :], 2, sh), ALU.is_equal))
            link(V.tensor_tensor(oh[:, :, :], oh[:, :, :], bcast(rank[:, :], 1, sh), ALU.mult))
            link(V.reduce_max(m2[:, :], oh[:, :, :], AX.X))
            V.tensor_tensor(oh[:, :, :], oh[:, :, :], bcast(m2[:, :], 2, sh), ALU.is_equal).then_inc(oh_ready, 1)
            dve.wait_ge(counted, 1)
            ohp = oh[:, :, :].rearrange("p (i t) e -> p t i e", t=3)
            kp = kept[:, :, :].rearrange("p (i t) e -> p t i e", t=3)
            for t in range(3):
                op = V.scalar_tensor_tensor(out=kp[:, t, :, :],
                                            in0=PS[0:TW, 5 + t, 0:NPAIR * E].rearrange("p (i e) -> p i e", e=E),
                                            scalar=float(CAP), in1=ohp[:, t, :, :], op0=ALU.is_le, op1=ALU.mult)
            op.then_inc(kept_ready, 1)
            dve.wait_ge(ranked, 1)
            fl = lambda ap: ap.rearrange("p e t -> p (e t)")
            link(V.tensor_copy(totals[:, :, :], PS[0:TW, 1, 0:NT * E].rearrange("p (t e) -> p e t", e=E)))
            link(V.tensor_tensor_scan(out=fl(sofar[:, :, :]), data0=fl(carry[:, :, :]), data1=fl(totals[:, :, :]),
                                      initial=0.0, op0=ALU.mult, op1=ALU.add))
            link(V.tensor_tensor(full[:, :, :], bcast(sofar[:, :, NT - 1], 2, [TW, E, ET]),
                                 bcast(filled[:, :], 1, [TW, E, ET]), ALU.is_gt))
            link(V.reduce_sum(ntiles[:, :], full[:, :, :], AX.X))
            link(V.tensor_tensor_scan(out=tiles_to[:, :], data0=carry[:, 0, 1:1 + E], data1=ntiles[:, :],
                                      initial=0.0, op0=ALU.mult, op1=ALU.add))
            link(V.tensor_tensor(base[:, :], tiles_to[:, :], ntiles[:, :], ALU.subtract))
            link(V.tensor_scalar(base[:, :], base[:, :], float(TR), -1.0, ALU.mult, ALU.add))
            link(V.tensor_tensor(sofar[:, :, :], sofar[:, :, :], totals[:, :, :], ALU.subtract))
            link(V.tensor_tensor(sofar[:, :, :], sofar[:, :, :], bcast(base[:, :], 2, [TW, E, NT]), ALU.add))
            link(V.tensor_tensor(row[:, :, :], sofar[:, :, :].rearrange("p e t -> p t e"),
                                 PS[0:TW, 0, 0:NT * E].rearrange("p (t e) -> p t e", e=E), ALU.add))
            link(V.tensor_tensor(row[:, :, :], row[:, :, :], kept[:, :, :], ALU.mult))
            link(V.reduce_sum(dest[:, :], row[:, :, :], AX.X))
            link(V.reduce_sum(m2[:, :], kept[:, :, :], AX.X))
            link(V.tensor_scalar(m2[:, :], m2[:, :], -1.0, 1.0, ALU.mult, ALU.add))
            link(V.tensor_tensor(m2[:, :], m2[:, :], token[:, :], ALU.mult))
            link(V.tensor_tensor(dest[:, :], dest[:, :], m2[:, :], ALU.add))
            link(V.tensor_copy(dest_i[:, :], dest[:, :]))
            link(V.tensor_tensor(passed[:, :, :], bcast(tiles_to[0:1, :], 1, [1, TILES, E]),
                                 bcast(tile_no[:, :], 2, [1, TILES, E]), ALU.is_le))
            link(V.reduce_sum(whose[:, :], passed[:, :, :], AX.X))
            link(V.tensor_scalar(whose[:, :], whose[:, :], float(E - 1), None, ALU.min))
            V.tensor_copy(whose_i[:, :], whose[:, :]).then_inc(sorted_, 1)
            with dve.Fori(0, TILES // U) as mm:
                for b in range(U):
                    m, a = mm * U + b, b % 2
                    dve.wait_ge(down_summed, m + (U + 1))
                    dve.wait_ge(y_free, m + 1)
                    V.tensor_copy(yt[:, a, :], PS[:, 4 * a + 3, 0:D]).then_inc(y_ready, 1)
            with dve.Fori(0, NT // 4) as tt:
                for o in range(4):
                    dve.wait_ge(gathered[o], tt * 16 + 16)
                    V.tensor_scalar(back[:, o, :], back[:, o, :], m1[:, ds(tt * 4 + o, 1)], None, ALU.mult)\
                        .then_inc(scaled, 1)
                    dve.wait_ge(back_turned, tt * 4 + (o + 1))
                    cols = ds(tt * 4 * TW + o * TW, TW)
                    V.tensor_tensor(h[:, :, cols], h[:, :, cols],
                                    PS[0:P, o % 2, 0:KD * TW].rearrange("p (k t) -> p k t", t=TW), ALU.add)\
                        .then_inc(h_ready, 1)
            dve.wait_ge(h_ready, NT + 2)


class Consts:
    pass


def store(nc, h, out):
    with nc.semaphore("out_stored") as stored, nc.Block() as block:

        @block.sync
        def _(sp):
            for k in range(KD):
                sp.dma_start(out[:, k, :], h[:, k, :]).then_inc(stored, 16)
            sp.wait_ge(stored, 16 * KD)


STAGES = 5


def build(nc, dr, out):
    with ExitStack() as ctx:
        s = Scope(nc, ctx, "all")
        h = s.sb("h", [P, KD, N])
        PS = ctx.enter_context(nc.psum_tensor("PS", [128, 8, 512], F32))
        C = Consts()
        C.ones = s.sb("ones", [P, P])
        C.ident = s.sb("identity", [128, 128])
        C.eps5 = s.sb("eps5", [P, 1])
        with nc.Block() as block:

            @block.vector
            def _(dve):
                nc.vector.memset(C.eps5[:, :], 1e-5)

        tokenizer(nc, dr, PS, C, h)
        if STAGES >= 2:
            mamba(nc, dr, PS, C, h)
        if STAGES >= 3:
            experts(nc, dr, PS, C, h)
        if STAGES >= 4:
            attention(nc, dr, PS, C, h)
        if STAGES >= 5:
            switch(nc, dr, PS, C, h)
        store(nc, h, out)



def layouts(i):
    a = {k: np.asarray(v) for k, v in i.items()}

    def rows(w, p):
        return w.reshape(w.shape[0] // p, p, *w.shape[1:]).transpose(1, 0, *range(2, w.ndim + 1))

    def headpad(w):
        z = np.zeros((*w.shape[:-1], NH, HP), w.dtype)
        z[..., :DH] = w.reshape(*w.shape[:-1], NH, DH)
        return z.reshape(*w.shape[:-1], NH * HP)

    o = {}
    o["pix"] = rows(a["x"].reshape(B, 3, 8, 16, 8, 16).transpose(1, 3, 5, 0, 2, 4).reshape(768, B * NIMG), 128)
    o["txt"] = rows(a["txt"].transpose(2, 0, 1), P)
    o["wp"] = rows(a["L0_tok_patch_w"].reshape(D, 768).T, 128)
    o["tok_vec"] = np.stack([rows(a["L0_tok_" + n], P) for n in ("patch_b", "ln_g", "ln_b", "ff2_b", "proj_b")], 1)
    o["ff1"] = rows(a["L0_tok_ff1_w"], P)
    o["ff1_b"] = rows(a["L0_tok_ff1_b"], 128)
    o["ff2"] = rows(a["L0_tok_ff2_w"], 128)
    qkv, qkvb = a["L0_tok_qkv_w"].reshape(D, 3, D), a["L0_tok_qkv_b"].reshape(3, D)
    o["tok_wqk"] = rows(headpad(qkv[:, 0:2]), P)
    o["tok_bqk"] = headpad(qkvb[0:2]).reshape(2, QC, 128).transpose(2, 0, 1)
    o["tok_wv"] = rows(headpad(qkv[:, 2]), P)
    o["tok_bv"] = headpad(qkvb[2])
    o["tok_wo"] = rows(headpad(a["L0_tok_proj_w"].T).T, 128)
    inw = a["L0_attn_in_proj_w"].transpose(0, 2, 1)
    lrows = lambda w, p: np.stack([rows(x, p) for x in w])
    o["ssm_winx"], o["ssm_winz"] = lrows(inw[:, :, :384], P), lrows(inw[:, :, 384:], P)
    o["ssm_nvec"] = np.stack([lrows(a["L0_attn_norm_w"], P), lrows(a["L0_attn_norm_b"], P)], 2)
    o["ssm_fvec"] = np.stack([rows(a["L0_attn_norm_f_w"], P), rows(a["L0_attn_norm_f_b"], P)], 1)
    o["ssm_cvec"] = lrows(np.concatenate([a["L0_attn_conv_w"], *(a["L0_attn_" + n][..., None] for n in
                                                                 ("conv_b", "dt_proj_b", "D_skip"))], -1), 128)
    o["ssm_alog"] = lrows(a["L0_attn_A_log"], 128)
    xw = a["L0_attn_x_proj_w"].transpose(0, 2, 1)
    o["ssm_wbc"] = lrows(np.concatenate([xw[:, :, 12:]] * 3, -1), 128)
    o["ssm_wdt"] = lrows(xw[:, :, :12], 128)
    o["ssm_wdt2"] = a["L0_attn_dt_proj_w"].transpose(0, 2, 1)
    o["ssm_wout"] = lrows(a["L0_attn_out_proj_w"].transpose(0, 2, 1), 128)
    pick = np.zeros((3, 32, 32, 128), mybir.dt.np(BF16))
    for n in range(32):
        pick[:, n, n] = 1
    o["ssm_sel"] = pick.reshape(P, 32 * 128)
    m = {k[7:]: v for k, v in a.items() if k.startswith("L0_ffn_")}
    o["moe_wr"] = rows(np.concatenate([m["router_w"], m["sg_w"]], 1), P)
    o["moe_wg"], o["moe_wu"] = (rows(m[k].transpose(1, 0, 2).reshape(D, 8 * 192), P) for k in ("w_gate", "w_up"))
    o["moe_wd"] = rows(m["w_down"].reshape(8 * 192, D), P)
    o["moe_wsg"], o["moe_wsu"], o["moe_wsd"] = rows(m["ws_gate"], P), rows(m["ws_up"], P), rows(m["ws_down"], 128)
    o["moe_sgb"] = m["sg_b"]
    o["moe_rank"] = np.tile(np.arange(8, 0, -1, dtype=np.float32), (94, 1))
    o["moe_pick"] = np.repeat(np.eye(9, dtype=np.float32), 128, 1)
    qkv = a["L1_attn_qkv_w"].T.reshape(D, 3, D)
    o["att_wqk"], o["att_wk"], o["att_wv"] = rows(headpad(qkv[:, 0:2]), P), rows(qkv[:, 1], P), \
        rows(headpad(qkv[:, 2]), P)
    o["att_wo"] = rows(headpad(a["L1_attn_proj_w"]).T, 128)
    o["att_bo"] = rows(a["L1_attn_proj_b"], P)
    pick = np.zeros((8, DH, 2, HP), np.float32)
    for g in range(2):
        for r in range(8):
            pick[r, :, g, g * 8 + r] = 1 / (2 * (0.5 * DH ** -0.5) * T)
    o["att_sel"] = pick.reshape(128, 2, HP)
    pick = np.zeros((2, 2, 8, 2, 2, 8, DH), np.float32)
    for g in range(2):
        for sign in range(2):
            for r in range(8):
                pick[sign, g, r, g, sign, r] = 1
    o["att_spread"] = pick.reshape(2 * DH, 4, 128)
    o["sw_lnw"], o["sw_wr"] = rows(a["L1_ffn_ln_w"], P), rows(a["L1_ffn_w_router"], P)
    o["sw_wi"], o["sw_wo"] = lrows(a["L1_ffn_wi"], P), lrows(a["L1_ffn_wo"], 128)
    o["sw_rank"] = np.tile(np.arange(16, 0, -1, dtype=np.float32), (94, 1))
    o["sw_every"] = np.ones((94, 94), np.float32)
    o["sw_carry"] = np.tile((np.arange(24) > 0).astype(np.float32), (94, 16, 1))
    o["sw_filled"] = np.tile(128 * np.arange(8, dtype=np.float32), (94, 1))
    o["sw_tile_no"] = np.arange(36, dtype=np.float32)[None]
    o["sw_token"] = (37 * 128 + np.arange(N, dtype=np.float32)).reshape(24, 94).T
    at = np.arange(PAIR)
    before = ((at[:, None] <= at[None]) & (at[:, None] // T == at[None] // T)).astype(np.float32)
    o["sw_upto"] = np.stack([before[x * 94:(x + 1) * 94, y * 94:(y + 1) * 94] for x, y in
                             ((0, 0), (0, 1), (1, 1), (1, 2), (2, 2))], 1)
    at, fr = np.arange(NIMG, dtype=np.float32)[:, None], np.arange(D // 2, dtype=np.float32)[None, :]
    ang = at / np.power(np.float32(10000.0), np.float32(2.0) * fr / np.float32(D))
    pe = np.zeros((NIMG, D), np.float32)
    pe[:, 0::2], pe[:, 1::2] = np.sin(ang), np.cos(ang)
    o["pos"] = rows(pe.T, P)
    o["ones"] = np.full((P, P), 1.0 / D, np.float32)
    o["ident"] = np.eye(128, dtype=np.float32)
    return {k: np.ascontiguousarray(v) for k, v in o.items()}


def kernel(**inputs):
    import concourse.bacc as _bacc
    from concourse.bass_utils import run_bass_kernel_spmd as _run

    nc = _bacc.Bacc("TRN2", target_bir_lowering=False, num_devices=1)
    arrays = layouts(inputs)
    dr = {k: nc.dram_tensor("in_" + k, v.shape, mybir.dt.from_np(v.dtype), kind="ExternalInput").ap() for k, v in arrays.items()}
    out = nc.dram_tensor("out", (P, KD, N), F32, kind="ExternalOutput").ap()
    build(nc, dr, out)
    r = _run(nc, [{"in_" + k: v for k, v in arrays.items()}], core_ids=[0]).results[0]["out"]
    return np.ascontiguousarray(r.transpose(1, 0, 2).reshape(D, B, T).transpose(1, 2, 0))
```

```python
from contextlib import ExitStack

import numpy as np

import concourse.bass as bass
from concourse import mybir

F32 = mybir.dt.float32
BF16 = mybir.dt.bfloat16
I32 = mybir.dt.int32
ALU = mybir.AluOpType
ACT = mybir.ActivationFunctionType
AX = mybir.AxisListType

B = 16
NIMG, NTXT = 64, 77
T = NIMG + NTXT
N = B * T
D = 192
P = 96
KD = D // P
NH, DH = 12, 16
HP = 32
QC = NH * HP // 128
FF = 768
FC = FF // 128
PAIR = 2 * T
NPAIR = B // 2
ds = bass.ds


def bcast(ap, axis, shape):
    return ap.unsqueeze(axis).broadcast_to(shape)


class Scope:

    def __init__(self, nc, ctx, tag):
        self.nc, self.ctx, self.tag = nc, ctx, tag
        self.all_sems = []
        ctx.callback(self.clear)

    def clear(self):
        if self.all_sems:
            self.nc.all_engine_barrier()
            self.nc.clear_and_free_semaphores(self.all_sems)
            self.nc.all_engine_barrier()

    def sb(self, name, shape, dt=F32):
        return self.ctx.enter_context(self.nc.sbuf_tensor(f"{self.tag}_{name}", shape, dt))

    def sem(self, name):
        self.all_sems.append(self.nc.alloc_semaphore(f"{self.tag}_{name}"))
        return self.all_sems[-1]

    def sems(self, *names):
        return [self.sem(n) for n in names]


class Norm:

    def __init__(self, s, tag, q, w, mean_ps, var_ps, ones, eps, center=True, xc=None, sq=None):
        self.q, self.w, self.mean_ps, self.var_ps, self.ones, self.eps = q, w, mean_ps, var_ps, ones, eps
        self.center = center
        self.xc = s.sb(f"{tag}_xc", [P, KD, q * w]) if center and xc is None else xc
        self.sq = s.sb(f"{tag}_sq", [P, KD, q * w]) if sq is None else sq
        self.rstd = s.sb(f"{tag}_rstd", [P, q * w])
        self.x_ready, self.mean_ready, self.centered, self.squared, self.var_ready, self.logvar, \
            self.rstd_ready, self.normed = s.sems(*(f"{tag}_{x}" for x in (
                "x_ready", "mean_ready", "centered", "squared", "var_ready", "logvar", "rstd_ready", "normed")))

    def total(self, nc, ps, x):
        for q in range(self.q):
            for k in range(KD):
                mm = nc.tensor.matmul(ps[:, q, :], self.ones[:, :], x[:, k, q * self.w:(q + 1) * self.w],
                                      start=k == 0, stop=k == KD - 1)
        return mm

    def split(self, ap):
        return ap.rearrange("p k (q t) -> p k q t", t=self.w)

    def pe(self, nc, pe, v, cols):
        self.pe_mean(nc, pe, v, cols)
        self.pe_var(nc, pe, v)

    def pe_mean(self, nc, pe, v, cols):
        pe.wait_ge(self.x_ready, v)
        for q in range(self.q):
            for k in range(KD):
                mm = nc.tensor.matmul(self.mean_ps[:, q, :], self.ones[:, :], cols(k, q * self.w, self.w),
                                      start=k == 0, stop=k == KD - 1)
        mm.then_inc(self.mean_ready, 1)

    def pe_var(self, nc, pe, v):
        pe.wait_ge(self.squared, v)
        self.total(nc, self.var_ps, self.sq).then_inc(self.var_ready, 1)

    def act(self, nc, act, v, x=None):
        if self.center:
            act.wait_ge(self.centered, v)
            nc.scalar.activation(self.sq[:, :, :], self.xc[:, :, :], ACT.Square).then_inc(self.squared, 1)
        else:
            act.wait_ge(self.x_ready, v)
            nc.scalar.activation(self.sq[:, :, :], x, ACT.Square).then_inc(self.squared, 1)
        act.wait_ge(self.var_ready, v)
        nc.scalar.activation(self.rstd[:, :].rearrange("p (q t) -> p q t", t=self.w), self.var_ps, ACT.Ln,
                             bias=self.eps[:, 0:1]).then_inc(self.logvar, 1)
        act.wait_ge(self.logvar, v)
        nc.scalar.activation(self.rstd[:, :], self.rstd[:, :], ACT.Exp, scale=-0.5).then_inc(self.rstd_ready, 1)

    def dve(self, nc, dve, v, x, out):
        if self.center:
            dve.wait_ge(self.mean_ready, v)
            nc.vector.tensor_tensor(self.split(self.xc[:, :, :]), self.split(x),
                                    bcast(self.mean_ps, 1, [P, KD, self.q, self.w]),
                                    ALU.subtract).then_inc(self.centered, 1)
        dve.wait_ge(self.rstd_ready, v)
        src = self.xc[:, :, :] if self.center else x
        nc.vector.tensor_tensor(out, src, bcast(self.rstd[:, :], 1, [P, KD, self.q * self.w]), ALU.mult)\
            .then_inc(self.normed, 1)


class NormAll:

    def __init__(self, s, tag, PS, ones, eps, xc, center=True, view=lambda ap: ap,
                 sq=None, rstd=None):
        self.PS, self.ones, self.eps, self.xc, self.center, self.view = PS, ones, eps, xc, center, view
        self.sq = s.sb(f"{tag}_sq", [P, 2, KD, PAIR]) if sq is None else sq
        self.rstd = s.sb(f"{tag}_rstd", [P, N]) if rstd is None else rstd
        self.start, self.mean_ready, self.centered, self.squared, self.var_ready, self.var_kept, self.logvar, \
            self.rstd_ready, self.entered = s.sems(*(f"{tag}_{x}" for x in (
                "start", "mean_ready", "centered", "squared", "var_ready", "var_kept", "logvar", "rstd_ready",
                "entered")))

    def pe(self, nc, pe, cols):
        if self.center:
            with pe.Fori(0, NPAIR // 2) as ii:
                for o in range(2):
                    pe.wait_ge(self.centered, ii * 2 + (o + 1))
                    nc.tensor.sem_inc(self.entered, 1)
                    for k in range(KD):
                        mm = nc.tensor.matmul(self.PS[0:P, o, 0:PAIR], self.ones[:, :], cols(k, ii * 2 + o),
                                              start=k == 0, stop=k == KD - 1)
                    mm.then_inc(self.mean_ready, 1)
        with pe.Fori(0, NPAIR // 2) as ii:
            for o in range(2):
                pe.wait_ge(self.squared, ii * 2 + (o + 1))
                pe.wait_ge(self.var_kept, ii * 2 + (o + 1))
                nc.tensor.sem_inc(self.entered, 1)
                for k in range(KD):
                    mm = nc.tensor.matmul(self.PS[0:P, 2 + o, 0:PAIR], self.ones[:, :], self.sq[:, o, k, :],
                                          start=k == 0, stop=k == KD - 1)
                mm.then_inc(self.var_ready, 1)

    def act(self, nc, act):
        act.wait_ge(self.start, 1)
        with act.Fori(0, NPAIR // 2) as ii:
            for o in range(2):
                if self.center:
                    act.wait_ge(self.centered, ii * 2 + (o + 3))
                act.wait_ge(self.var_ready, ii * 2 + (o + 1))
                nc.scalar.activation(self.view(self.sq[:, o, :, :]), self.xc(ii * 2 + o), ACT.Square)\
                    .then_inc(self.squared, 1)
        act.wait_ge(self.var_kept, NPAIR + 2)
        nc.scalar.activation(self.rstd[:, :], self.rstd[:, :], ACT.Ln, bias=self.eps[:, 0:1]).then_inc(self.logvar, 1)
        act.wait_ge(self.logvar, 1)
        nc.scalar.activation(self.rstd[:, :], self.rstd[:, :], ACT.Exp, scale=-0.5).then_inc(self.rstd_ready, 1)

    def dve(self, nc, dve, x=None):
        nc.vector.sem_inc(self.centered, 2)
        nc.vector.sem_inc(self.var_ready, 2)
        nc.vector.sem_inc(self.var_kept, 2)
        nc.vector.sem_inc(self.start, 1)
        if self.center:
            with dve.Fori(0, NPAIR // 2) as ii:
                for o in range(2):
                    dve.wait_ge(self.mean_ready, ii * 2 + (o + 1))
                    nc.vector.tensor_tensor(self.xc(ii * 2 + o), self.view(x(ii * 2 + o)),
                                            self.view(bcast(self.PS[0:P, o, 0:PAIR], 1, [P, KD, PAIR])),
                                            ALU.subtract).then_inc(self.centered, 1)
        with dve.Fori(0, NPAIR // 2) as ii:
            for o in range(2):
                dve.wait_ge(self.var_ready, ii * 2 + (o + 3))
                nc.vector.tensor_copy(self.rstd[:, ds((ii * 2 + o) * PAIR, PAIR)], self.PS[0:P, 2 + o, 0:PAIR])\
                    .then_inc(self.var_kept, 1)
        dve.wait_ge(self.rstd_ready, 1)
        if self.center:
            dve.wait_ge(self.centered, NPAIR + 2)

    def scale(self, i):
        return self.view(bcast(self.rstd[:, ds(i * PAIR, PAIR)], 1, [P, KD, PAIR]))


class FeedForward:

    def __init__(self, s, n, PS, bank, w1, b1, w2):
        self.n, self.PS, self.bank, self.w1, self.b1, self.w2 = n, PS, bank, w1, b1, w2
        self.hid = s.sb("ff_hid", [128, FC, n])
        self.in_ready, self.hid_summed, self.hid_ready, self.out_summed = s.sems(
            "ff_in_ready", "ff_hid_summed", "ff_hid_ready", "ff_out_summed")

    def pe(self, nc, pe, v, x):
        pe.wait_ge(self.in_ready, v + 1)
        for j in range(FC):
            if j >= 2:
                pe.wait_ge(self.hid_ready, v * FC + (j - 1))
            for k in range(KD):
                mm = nc.tensor.matmul(self.PS[:, self.bank + j % 2, 0:self.n], self.w1[:, k, j * 128:(j + 1) * 128],
                                      x[:, k, :], start=k == 0, stop=k == KD - 1)
            mm.then_inc(self.hid_summed, 1)
        for j in range(FC):
            pe.wait_ge(self.hid_ready, v * FC + (j + 1))
            for m in range(KD):
                mm = nc.tensor.matmul(self.PS[0:P, self.bank + 2 + m, 0:self.n], self.w2[:, j, m * P:(m + 1) * P],
                                      self.hid[:, j, :], start=j == 0, stop=j == FC - 1)
        mm.then_inc(self.out_summed, 1)

    def act(self, nc, act, v):
        for j in range(FC):
            act.wait_ge(self.hid_summed, v * FC + (j + 1))
            nc.scalar.activation(self.hid[:, j, :], self.PS[:, self.bank + j % 2, 0:self.n], ACT.Gelu_apprx_tanh,
                                 bias=self.b1[:, j:j + 1]).then_inc(self.hid_ready, 1)


def tokenizer(nc, dr, PS, C, h):
    NI = B * NIMG
    NB = 512
    NL = NI // NB
    WT = 2 * NIMG
    NW = NI // WT
    KP = 6
    with ExitStack() as ctx:
        s = Scope(nc, ctx, "tok")
        pix = s.sb("pix", [128, KP, NI])
        wp = s.sb("wp", [128, KP, D])
        ff1 = s.sb("ff1", [P, KD, FF])
        ff2 = s.sb("ff2", [128, FC, D])
        wqk = s.sb("wqk", [P, KD, 2, QC * 128])
        wv = s.sb("wv", [P, KD, QC * 128])
        wo = s.sb("wo", [128, QC, D])
        vec = s.sb("vec", [P, 5, KD])
        b1 = s.sb("b1", [128, FC])
        bqk = s.sb("bqk", [128, 2, QC])
        bv = s.sb("bv", [NIMG, QC * 128])
        pos = s.sb("pos", [P, KD, NIMG])
        emb = s.sb("emb", [P, KD, NB])
        xg = s.sb("xg", [P, KD, NB])
        ident = s.sb("ident", [P, KD, NI])
        y1 = s.sb("y1", [P, KD, NI])
        x2 = s.sb("x2", [P, KD, NI])
        yb = s.sb("yb", [P, KD, WT])
        qk = s.sb("qk", [128, 2, QC, WT])
        v = s.sb("v", [NIMG, 2, QC * 128])
        mx = s.sb("mx", [NIMG, 4, 6])
        sx = s.sb("sx", [NIMG, 4, 6, NIMG])
        ex = s.sb("ex", [NIMG, 4, 6, NIMG])
        pT = s.sb("pT", [NIMG, 24, NIMG])
        oT = s.sb("oT", [128, QC, WT])
        ln = Norm(s, "ln", 1, NB, PS[0:P, 6:7, :], PS[0:P, 7:8, :], C.ones, C.eps5)
        ff = FeedForward(s, NB, PS, 2, ff1, b1, ff2)
        loaded, patch_summed, y1_ready, gained = s.sems(
            "loaded", "patch_summed", "y1_ready", "gained")
        yb_ready, qk_summed, qk_ready, v_summed, v_ready, scored, maxed, shifted, exped, summed, inverted, probs, \
            turned, pT_ready, mixed, oT_ready, projected, x2_ready, h_ready = s.sems(
                "yb_ready", "qk_summed", "qk_ready", "v_summed", "v_ready", "scored", "maxed", "shifted", "exped",
                "summed", "inverted", "probs", "turned", "pT_ready", "mixed", "oT_ready", "projected", "x2_ready",
                "h_ready")
        h4 = h[:, :, :].rearrange("p k (b t) -> p k b t", t=T)
        loads = [(pix[:, :, :], dr["pix"]), (wp[:, :, :], dr["wp"]), (vec[:, :, :], dr["tok_vec"]),
                 (pos[:, :, :], dr["pos"]), (ff1[:, :, :], dr["ff1"]), (b1[:, :], dr["ff1_b"]),
                 (ff2[:, :, :], dr["ff2"]), (wqk[:, :, :, :], dr["tok_wqk"]), (bqk[:, :, :], dr["tok_bqk"]),
                 (wv[:, :, :], dr["tok_wv"]), (bv[:, :], dr["tok_bv"].partition_broadcast(NIMG)),
                 (wo[:, :, :], dr["tok_wo"]), (C.ones[:, :], dr["ones"]), (C.ident[:, :], dr["ident"])]
        loads += [(h4[:, k, :, NIMG:T], dr["txt"][:, k, :, :]) for k in range(KD)]
        ALL = 16 * len(loads)
        block = ctx.enter_context(nc.Block())

        @block.sync
        def _(sp):
            for dst, src in loads:
                sp.dma_start(dst, src).then_inc(loaded, 16)
            sp.wait_ge(loaded, ALL)

        @block.tensor
        def _(pe):
            pe.wait_ge(loaded, ALL)
            with pe.Fori(0, NL) as i:
                for m in range(KD):
                    for k in range(KP):
                        mm = nc.tensor.matmul(PS[0:P, m, :], wp[:, k, m * P:(m + 1) * P], pix[:, k, ds(i * NB, NB)],
                                              start=k == 0, stop=k == KP - 1)
                mm.then_inc(patch_summed, 1)
                ln.pe(nc, pe, i + 1, lambda k, at, w: emb[:, k, at:at + w])
                ff.pe(nc, pe, i, ident[:, :, ds(i * NB, NB)])
            with pe.Fori(0, NW) as i:
                pe.wait_ge(yb_ready, i + 1)
                for a in range(2):
                    for c in range(QC):
                        for k in range(KD):
                            mm = nc.tensor.matmul(PS[:, a, c * WT:(c + 1) * WT], wqk[:, k, a, c * 128:(c + 1) * 128],
                                                  yb[:, k, :], start=k == 0, stop=k == KD - 1)
                    mm.then_inc(qk_summed, 1)
                for w in range(2):
                    for k in range(KD):
                        mm = nc.tensor.matmul(PS[0:NIMG, 2 + w, 0:QC * 128], yb[:, k, w * NIMG:(w + 1) * NIMG],
                                              wv[:, k, :], start=k == 0, stop=k == KD - 1)
                mm.then_inc(v_summed, 1)
                pe.wait_ge(qk_ready, 2 * i + 2)
                for j in range(4):
                    for w in range(2):
                        for c in range(QC):
                            rows, cols, slot = slice(HP * j, HP * j + DH), slice(w * NIMG, (w + 1) * NIMG), w * QC + c
                            mm = nc.tensor.matmul(PS[0:NIMG, 4 + j, slot * NIMG:(slot + 1) * NIMG],
                                                  qk[rows, 0, c, cols], qk[rows, 1, c, cols], start=True, stop=True)
                mm.then_inc(scored, 1)
                pe.wait_ge(loaded, ALL)
                pe.wait_ge(probs, i + 1)
                pe.wait_ge(v_ready, i + 1)
                for n in range(24):
                    mm = nc.tensor.transpose(PS[0:NIMG, n // 8, (n % 8) * NIMG:(n % 8 + 1) * NIMG],
                                             ex[:, n // 6, n % 6, :], C.ident[0:NIMG, 0:NIMG])
                mm.then_inc(turned, 1)
                pe.wait_ge(loaded, ALL)
                pe.wait_ge(pT_ready, i + 1)
                for j in range(4):
                    for w in range(2):
                        for c in range(QC):
                            mm = nc.tensor.matmul(PS[HP * j:HP * (j + 1), 3, c * WT + w * NIMG:c * WT + (w + 1) * NIMG],
                                                  v[:, w, (4 * c + j) * HP:(4 * c + j + 1) * HP],
                                                  pT[:, j * 6 + w * QC + c, :], start=True, stop=True)
                mm.then_inc(mixed, 1)
                pe.wait_ge(oT_ready, i + 1)
                for m in range(KD):
                    for c in range(QC):
                        mm = nc.tensor.matmul(PS[0:P, 4, m * WT:(m + 1) * WT], wo[:, c, m * P:(m + 1) * P],
                                              oT[:, c, :], start=c == 0, stop=c == QC - 1)
                mm.then_inc(projected, 1)
            with pe.Fori(0, NL) as i:
                ff.pe(nc, pe, i + NL, x2[:, :, ds(i * NB, NB)])

        @block.scalar
        def _(act):
            act.wait_ge(loaded, ALL)
            with act.Fori(0, NL) as i:
                act.wait_ge(patch_summed, i + 1)
                for m in range(KD):
                    op = nc.scalar.activation(emb[:, m, :], PS[0:P, m, :], ACT.Identity, bias=vec[:, 0, m:m + 1])
                op.then_inc(ln.x_ready, 1)
                ln.act(nc, act, i + 1)
                ff.act(nc, act, i)
                act.wait_ge(ff.out_summed, i + 1)
                for m in range(KD):
                    op = nc.scalar.activation(y1[:, m, ds(i * NB, NB)], PS[0:P, 4 + m, :], ACT.Identity,
                                              bias=vec[:, 3, m:m + 1])
                op.then_inc(y1_ready, 1)
            with act.Fori(0, NW) as i:
                act.wait_ge(shifted, i + 1)
                nc.scalar.activation(ex[:, :, :, :], sx[:, :, :, :], ACT.Exp, scale=DH ** -0.5).then_inc(exped, 1)
                act.wait_ge(turned, i + 1)
                nc.scalar.activation(pT[:, :, :], PS[0:NIMG, 0:3, :].rearrange("p a (b t) -> p (a b) t", t=NIMG),
                                     ACT.Copy).then_inc(pT_ready, 1)
                act.wait_ge(mixed, i + 1)
                nc.scalar.activation(oT[:, :, :], PS[:, 3, 0:QC * WT].rearrange("p (c t) -> p c t", t=WT),
                                     ACT.Copy).then_inc(oT_ready, 1)
            with act.Fori(0, NL) as i:
                ff.act(nc, act, i + NL)

        @block.vector
        def _(dve):
            dve.wait_ge(loaded, ALL)
            with dve.Fori(0, NL) as i:
                ln.dve(nc, dve, i + 1, emb[:, :, :], emb[:, :, :])
                dve.wait_ge(ln.normed, i + 1)
                for m in range(KD):
                    op = nc.vector.tensor_scalar(xg[:, m, :], emb[:, m, :], vec[:, 1, m:m + 1], vec[:, 2, m:m + 1],
                                                 ALU.mult, ALU.add)
                op.then_inc(gained, 1)
                dve.wait_ge(gained, i + 1)
                for m in range(KD):
                    op = nc.vector.tensor_tensor(
                        ident[:, m, ds(i * NB, NB)].rearrange("p (b t) -> p b t", t=NIMG),
                        xg[:, m, :].rearrange("p (b t) -> p b t", t=NIMG),
                        bcast(pos[:, m, :], 1, [P, NB // NIMG, NIMG]), ALU.add)
                op.then_inc(ff.in_ready, 1)
            with dve.Fori(0, NW) as i:
                dve.wait_ge(y1_ready, NL)
                nc.vector.tensor_copy(yb[:, :, :], y1[:, :, ds(i * WT, WT)]).then_inc(yb_ready, 1)
                for a in range(2):
                    dve.wait_ge(qk_summed, 2 * i + (a + 1))
                    nc.vector.tensor_tensor(qk[:, a, :, :], PS[:, a, 0:QC * WT].rearrange("p (c t) -> p c t", t=WT),
                                            bcast(bqk[:, a, :], 2, [128, QC, WT]), ALU.add).then_inc(qk_ready, 1)
                dve.wait_ge(v_summed, i + 1)
                nc.vector.tensor_tensor(v[:, :, :], PS[0:NIMG, 2:4, 0:QC * 128],
                                        bcast(bv[:, :], 1, [NIMG, 2, QC * 128]), ALU.add).then_inc(v_ready, 1)
                sc = PS[0:NIMG, 4:8, 0:6 * NIMG].rearrange("p j (n t) -> p j n t", t=NIMG)
                dve.wait_ge(scored, i + 1)
                nc.vector.reduce_max(mx[:, :, :], sc, AX.X).then_inc(maxed, 1)
                dve.wait_ge(maxed, i + 1)
                for j in range(4):
                    op = nc.vector.tensor_tensor(sx[:, j, :, :], sc[:, j, :, :], bcast(mx[:, j, :], 2, [NIMG, 6, NIMG]),
                                                 ALU.subtract)
                op.then_inc(shifted, 1)
                dve.wait_ge(exped, i + 1)
                nc.vector.reduce_sum(mx[:, :, :], ex[:, :, :, :], AX.X).then_inc(summed, 1)
                dve.wait_ge(summed, i + 1)
                nc.vector.reciprocal(mx[:, :, :], mx[:, :, :]).then_inc(inverted, 1)
                dve.wait_ge(inverted, i + 1)
                for j in range(4):
                    op = nc.vector.tensor_tensor(ex[:, j, :, :], ex[:, j, :, :], bcast(mx[:, j, :], 2, [NIMG, 6, NIMG]),
                                                 ALU.mult)
                op.then_inc(probs, 1)
                dve.wait_ge(projected, i + 1)
                for m in range(KD):
                    op = nc.vector.scalar_tensor_tensor(
                        out=x2[:, m, ds(i * WT, WT)], in0=PS[0:P, 4, m * WT:(m + 1) * WT], scalar=vec[:, 4, m:m + 1],
                        in1=ident[:, m, ds(i * WT, WT)], op0=ALU.add, op1=ALU.add)
                op.then_inc(x2_ready, 1)
            dve.wait_ge(x2_ready, NW)
            with dve.Fori(0, NL) as i:
                nc.vector.sem_inc(ff.in_ready, 1)
                dve.wait_ge(ff.out_summed, i + NL + 1)
                for m in range(KD):
                    op = nc.vector.scalar_tensor_tensor(
                        out=h4[:, m, ds(i * 8, 8), 0:NIMG],
                        in0=PS[0:P, 4 + m, :].rearrange("p (b t) -> p b t", t=NIMG), scalar=vec[:, 3, m:m + 1],
                        in1=x2[:, m, ds(i * NB, NB)].rearrange("p (b t) -> p b t", t=NIMG), op0=ALU.add, op1=ALU.add)
                op.then_inc(h_ready, 1)
                dve.wait_ge(h_ready, i + 1)


def mamba(nc, dr, PS, C, h):
    L, DI, DS, DC, DR = 4, 384, 16, 4, 12
    CT = DI // 128
    QW = 4 * T
    NQ = N // QW
    HW = QW // 2
    SP2 = DS // 2
    UW = 2 * QW
    RESTART = 1e20
    with ExitStack() as ctx:
        s = Scope(nc, ctx, "ssm")
        res = s.sb("res", [P, KD, N])
        winx = s.sb("winx", [P, KD, DI])
        winz = s.sb("winz", [P, KD, DI])
        nvec = s.sb("nvec", [P, 2, KD])
        fvec = s.sb("fvec", [P, 2, KD])
        cvec = s.sb("cvec", [128, CT, DC + 3])
        a_log = s.sb("a_log", [128, CT, DS])
        amat = s.sb("amat", [128, CT, DS])
        R = P + DR
        wx = s.sb("wx", [128, CT, R])
        wdt2 = s.sb("wdt2", [R, DI])
        wout = s.sb("wout", [128, CT, D])
        sel = s.sb("sel", [P, 2 * DS * 128], BF16)
        hn = s.sb("hn", [P, KD, QW])
        xs = s.sb("xs", [128, CT, QW])
        sz = s.sb("sz", [128, CT, QW])
        dt = s.sb("dt", [128, CT, QW])
        sp = s.sb("sp", [128, CT, QW])
        us = s.sb("us", [128, CT, QW])
        bcf = s.sb("bcf", [R, QW])
        bcr = s.sb("bcr", [P, QW])
        mid = s.sb("mid", [P, QW], BF16)
        bcp = s.sb("bcp", [P, QW], BF16)
        bb = s.sb("bb", [128, DS, QW])
        cb = s.sb("cb", [128, DS, QW])
        da = s.sb("da", [128, 2, UW])
        hs = s.sb("hs", [128, 2, UW])
        hc = s.sb("hc", [128, 2, UW])
        flat = PS[:, :, :].rearrange("p a b -> p (a b)")
        u_ps = flat[:, 0:QW]
        dbx = [flat[:, QW + n * UW:QW + (n + 1) * UW] for n in range(2)]
        assert QW + 2 * UW <= 6 * 512
        ln = Norm(s, "ln", 2, HW, PS[0:P, 0:2, 0:HW], PS[0:P, 2:4, 0:HW], C.ones, C.eps5,
                  xc=us[0:P, 0:KD, :], sq=sp[0:P, 0:KD, :])
        loaded, wloaded, layer_done, gained, xin_summed, tap, conv_done, z_summed, sz_ready, xs_ready, low_summed, \
            low_ready, dt_summed, dt_pre, dt_abs, dt_exp, dt_log, dt_ready, split1, split2, split3, bcp_ready, \
            b_summed, c_summed, b_ready, c_ready, a_exp, a_ready, us_ready, restart, u_ready, \
            da_ready, dbx_ready, scanned, weighted, reduced, y_taken, gated, out_summed, res_ready, h_ready = s.sems(
                "loaded", "wloaded", "layer_done", "gained", "xin_summed", "tap", "conv_done", "z_summed", "sz_ready",
                "xs_ready", "low_summed", "low_ready", "dt_summed", "dt_pre", "dt_abs", "dt_exp", "dt_log", "dt_ready",
                "split1", "split2", "split3", "bcp_ready", "b_summed", "c_summed", "b_ready", "c_ready", "a_exp",
                "a_ready", "us_ready", "restart", "u_ready", "da_ready", "dbx_ready", "scanned", "weighted", "reduced",
                "y_taken", "gated", "out_summed", "res_ready", "h_ready")
        pairs = lambda ap: lambda i: ap[:, :, ds(i * PAIR, PAIR)]
        first, last = (NormAll(s, tag, PS, C.ones, C.eps5, pairs(res),
                               sq=cb[0:P, 0:2, :].rearrange("p o (k t) -> p o k t", t=PAIR),
                               rstd=bb[0:P, 0:N // QW, :].rearrange("p a t -> p (a t)")) for tag in ("first", "last"))
        first_ready, last_scaled = s.sems("first_ready", "last_scaled")
        hc_filled = s.sem("hc_filled")
        entered = s.sems("pe_loop_entered", "dve_loop_entered", "pool_loop_entered")
        wloads = [(winx[:, :, :], "ssm_winx"), (winz[:, :, :], "ssm_winz"), (nvec[:, :, :], "ssm_nvec"),
                  (cvec[:, :, :], "ssm_cvec"), (a_log[:, :, :], "ssm_alog"), (wx[:, :, :], "ssm_wx"),
                  (wdt2[P:R, :], "ssm_wdt2"), (wout[:, :, :], "ssm_wout")]
        NWL = 16 * len(wloads)
        two = lambda ap: ap.rearrange("p (q t) -> p q t", t=HW)
        block = ctx.enter_context(nc.Block())

        @block.sync
        def _(sync):
            sync.dma_start(sel[:, :], dr["ssm_sel"]).then_inc(loaded, 16)
            sync.dma_start(fvec[:, :, :], dr["ssm_fvec"]).then_inc(loaded, 16)
            with sync.Fori(0, L) as l:
                sync.wait_ge(layer_done, l + 1)
                for dst, name in wloads:
                    src = dr[name][ds(l, 1)]
                    src = src.rearrange("a p b -> (a p) b") if len(src.shape) == 3 else \
                        src.rearrange("a p b c -> (a p) b c")
                    sync.dma_start(dst, src).then_inc(wloaded, 16)
            sync.wait_ge(wloaded, NWL * L)
            sync.wait_ge(loaded, 32)

        @block.tensor
        def _(pe):
            def keep_clock(n, bank=7):
                for _ in range(n):
                    nc.tensor.matmul(PS[:, bank, 0:HW], C.ident[:, :], hc[:, 0, 0:HW], start=True, stop=True)

            first.pe(nc, pe, lambda k, i: h[:, k, ds(i * PAIR, PAIR)])
            pe.wait_ge(loaded, 32)
            with pe.Fori(0, L) as l:
                pe.wait_ge(wloaded, l * NWL + NWL)
                pe.wait_ge(hc_filled, 1)
                nc.tensor.sem_inc(entered[0], 1)
                with pe.Fori(0, NQ) as q:
                    v = l * NQ + q
                    keep_clock(3)
                    ln.pe_mean(nc, pe, v + 1, lambda k, at, w: res[:, k, ds(q * QW + at, w)])
                    keep_clock(4)
                    ln.pe_var(nc, pe, v + 1)
                    keep_clock(9)
                    pe.wait_ge(gained, v + 1)
                    for c in range(CT):
                        for b in range(2):
                            for k in range(KD):
                                mm = nc.tensor.matmul(PS[:, 2 * c + b, 0:HW], winx[:, k, c * 128:(c + 1) * 128],
                                                      hn[:, k, b * HW:(b + 1) * HW], start=k == 0, stop=k == KD - 1)
                    mm.then_inc(xin_summed, 1)
                    for c in range(CT):
                        pe.wait_ge(sz_ready, v * CT + (c + 1))
                        for b in range(2):
                            for k in range(KD):
                                mm = nc.tensor.matmul(PS[:, 6 + b, 0:HW], winz[:, k, c * 128:(c + 1) * 128],
                                                      hn[:, k, b * HW:(b + 1) * HW], start=k == 0, stop=k == KD - 1)
                        mm.then_inc(z_summed, 1)
                    pe.wait_ge(sz_ready, v * CT + (CT + 1))
                    for c in range(CT):
                        if c == CT - 1:
                            keep_clock(3, 0)
                        pe.wait_ge(xs_ready, v * CT + (c + 1))
                        for b in range(2):
                            mm = nc.tensor.matmul(PS[0:R, 6 + b, 0:HW], wx[:, c, :], xs[:, c, b * HW:(b + 1) * HW],
                                                  start=c == 0, stop=c == CT - 1)
                    mm.then_inc(low_summed, 1)
                    keep_clock(2, 3)
                    pe.wait_ge(low_ready, v + 1)
                    for c in range(CT):
                        for b in range(2):
                            mm = nc.tensor.matmul(PS[:, 2 + 2 * c + b, 0:HW], wdt2[P:R, c * 128:(c + 1) * 128],
                                                  bcf[P:R, b * HW:(b + 1) * HW], start=True, stop=True)
                    mm.then_inc(dt_summed, 1)
                    pe.wait_ge(dt_pre, v + 1)
                    pe.wait_ge(bcp_ready, v + 1)
                    nc.tensor.sem_inc(entered[0], 1)

                    def spread(x, n, e, col, taken, summed):
                        pe.wait_ge(taken, v * DS + (n + 1))
                        for b in range(2):
                            mm = nc.tensor.matmul(PS[:, 4 * x + 2 * e + b, 0:HW], sel[:, col],
                                                  bcp[:, b * HW:(b + 1) * HW], start=True, stop=True)
                        mm.then_inc(summed, 1)

                    with pe.Fori(0, DS // 4) as j:
                        for e in range(2):
                            spread(1, j * 2 + e, e, ds(j * 256 + (DS + e) * 128, 128), c_ready, c_summed)
                    nc.tensor.sem_inc(entered[0], 1)
                    with pe.Fori(0, DS // 4) as j:
                        for e in range(2):
                            spread(0, j * 2 + e, e, ds(j * 256 + e * 128, 128), b_ready, b_summed)
                            spread(1, j * 2 + (DS // 2 + e), e, ds(j * 256 + (DS + DS // 2 + e) * 128, 128), c_ready,
                                   c_summed)
                    nc.tensor.sem_inc(entered[0], 1)
                    with pe.Fori(0, DS // 4) as j:
                        for e in range(2):
                            spread(0, j * 2 + (DS // 2 + e), e, ds(j * 256 + (DS // 2 + e) * 128, 128), b_ready, b_summed)
                    with pe.Fori(0, CT) as c:
                        pe.wait_ge(y_taken, v * CT + c + 1)
                        for n in range(SP2):
                            pe.wait_ge(weighted, v * CT * SP2 + c * SP2 + (n + 3))
                            for e in range(2):
                                for b in range(2):
                                    at = e * QW + b * HW
                                    mm = nc.tensor.matmul(PS[:, 6 + b, 0:HW], C.ident[:, :], hc[:, n % 2, at:at + HW],
                                                          start=n == 0 and e == 0, stop=n == SP2 - 1 and e == 1)
                            mm.then_inc(reduced, 1)
                    keep_clock(5, 3)
                    pe.wait_ge(gated, v + 1)
                    for m in range(KD):
                        for b in range(2):
                            for c in range(CT):
                                mm = nc.tensor.matmul(PS[0:P, 2 * m + b, 0:HW], wout[:, c, m * P:(m + 1) * P],
                                                      xs[:, c, b * HW:(b + 1) * HW], start=c == 0, stop=c == CT - 1)
                    mm.then_inc(out_summed, 1)
            pe.wait_ge(res_ready, L * NQ)
            last.pe(nc, pe, lambda k, i: res[:, k, ds(i * PAIR, PAIR)])

        @block.scalar
        def _(act):
            first.act(nc, act)
            with act.Fori(0, L) as l:
                act.wait_ge(wloaded, l * NWL + NWL)
                with act.Fori(0, NQ) as q:
                    v = l * NQ + q
                    ln.act(nc, act, v + 1)
                    nc.scalar.activation(amat[:, :, :], a_log[:, :, :], ACT.Exp).then_inc(a_exp, 1)
                    for c in range(CT):
                        act.wait_ge(z_summed, v * CT + (c + 1))
                        nc.scalar.activation(two(sz[:, c, :]), PS[:, 6:8, 0:HW], ACT.Silu).then_inc(sz_ready, 1)
                        act.wait_ge(conv_done, v * CT + (c + 1))
                        nc.scalar.activation(xs[:, c, :], xs[:, c, :], ACT.Silu).then_inc(xs_ready, 1)
                    act.wait_ge(low_summed, v + 1)
                    nc.scalar.activation(two(bcf[:, :]), PS[0:R, 6:8, 0:HW], ACT.Copy).then_inc(low_ready, 1)
                    act.wait_ge(dt_summed, v + 1)
                    for c in range(CT):
                        op = nc.scalar.activation(two(dt[:, c, :]), PS[:, 2 + 2 * c:4 + 2 * c, 0:HW], ACT.Identity,
                                                  bias=cvec[:, c, DC + 1:DC + 2])
                    op.then_inc(dt_pre, 1)
                    act.wait_ge(dt_pre, v + 1)
                    nc.scalar.activation(sp[:, :, :], dt[:, :, :], ACT.Abs).then_inc(dt_abs, 1)
                    act.wait_ge(dt_abs, v + 1)
                    nc.scalar.activation(sp[:, :, :], sp[:, :, :], ACT.Exp, scale=-1.0).then_inc(dt_exp, 1)
                    act.wait_ge(dt_exp, v + 1)
                    nc.scalar.activation(sp[:, :, :], sp[:, :, :], ACT.Ln, bias=1.0).then_inc(dt_log, 1)
                    with act.Fori(0, DS // 2) as j:
                        for e in range(2):
                            n = v * DS + j * 2 + e
                            act.wait_ge(b_summed, n + 1)
                            nc.scalar.activation(two(bb[:, ds(j * 2 + e, 1), :].rearrange("p a t -> p (a t)")),
                                                 PS[:, 2 * e:2 * e + 2, 0:HW], ACT.Copy).then_inc(b_ready, 1)
                    act.wait_ge(restart, v + 1)
                    act.wait_ge(a_ready, v + 1)
                    with act.Fori(0, CT) as c:
                        for n in range(SP2):
                            act.wait_ge(scanned, v * CT * SP2 + c * SP2 + (n + 1))
                            for e in range(2):
                                op = nc.scalar.activation(
                                    da[:, n % 2, e * QW:(e + 1) * QW],
                                    dt[:, ds(c, 1), :].rearrange("p a t -> p (a t)"), ACT.Exp,
                                    scale=amat[:, ds(c, 1), 2 * n + e:2 * n + e + 1].rearrange("p a t -> p (a t)"))
                            op.then_inc(da_ready, 1)
            last.act(nc, act)

        @block.gpsimd
        def _(pool):
            pool.memset(hc[:, 0, 0:HW], 0.0).then_inc(hc_filled, 1)
            pool.sem_inc(weighted, 2)
            with pool.Fori(0, L * NQ) as v:
                pool.wait_ge(c_ready, v * DS + (DS + 2))
                nc.gpsimd.sem_inc(entered[2], 1)
                with pool.Fori(0, CT) as c:
                    for n in range(SP2):
                        u = v * CT * SP2 + c * SP2 + n
                        pool.wait_ge(scanned, u + 3)
                        pool.wait_ge(reduced, u + 1)
                        nc.gpsimd.tensor_tensor(hc[:, n % 2, :], hs[:, n % 2, :],
                                                cb[:, 2 * n:2 * n + 2, :].rearrange("p a t -> p (a t)"),
                                                ALU.mult).then_inc(weighted, 1)

        @block.vector
        def _(dve):
            nc.vector.sem_inc(layer_done, 1)
            nc.vector.sem_inc(scanned, 2)
            nc.vector.sem_inc(reduced, 2)
            nc.vector.sem_inc(b_ready, 2)
            nc.vector.sem_inc(c_ready, 2)
            nc.vector.sem_inc(y_taken, 1)
            nc.vector.sem_inc(sz_ready, 1)
            first.dve(nc, dve, pairs(h))
            with dve.Fori(0, NPAIR) as i:
                nc.vector.tensor_tensor(first.xc(i), first.xc(i), first.scale(i), ALU.mult).then_inc(first_ready, 1)
            dve.wait_ge(first_ready, NPAIR)
            with dve.Fori(0, L) as l:
                dve.wait_ge(wloaded, l * NWL + NWL)
                nc.vector.sem_inc(entered[1], 1)
                with dve.Fori(0, NQ) as q:
                    v = l * NQ + q
                    nc.vector.sem_inc(ln.x_ready, 1)
                    ln.dve(nc, dve, v + 1, res[:, :, ds(q * QW, QW)], hn[:, :, :])
                    dve.wait_ge(ln.normed, v + 1)
                    for m in range(KD):
                        op = nc.vector.tensor_scalar(hn[:, m, :], hn[:, m, :], nvec[:, 0, m:m + 1],
                                                     nvec[:, 1, m:m + 1], ALU.mult, ALU.add)
                    op.then_inc(gained, 1)
                    dve.wait_ge(a_exp, v + 1)
                    nc.vector.tensor_scalar(amat[:, :, :], amat[:, :, :], -1.0, -2e-18, ALU.mult, ALU.min)\
                        .then_inc(a_ready, 1)
                    dve.wait_ge(xin_summed, v + 1)
                    for c in range(CT):
                        for back in range(DC):
                            if back:
                                dve.wait_ge(tap, (v * CT + c) * (DC - 1) + back)
                            for b in range(2):
                                src = PS[:, 2 * c + b, 0:HW].rearrange("p (b t) -> p b t", t=T)
                                dst = xs[:, c, b * HW:(b + 1) * HW].rearrange("p (b t) -> p b t", t=T)
                                w = cvec[:, c, DC - 1 - back:DC - back]
                                if back == 0:
                                    op = nc.vector.tensor_scalar(dst, src, w, cvec[:, c, DC:DC + 1],
                                                                 ALU.mult, ALU.add)
                                else:
                                    op = nc.vector.scalar_tensor_tensor(
                                        out=dst[:, :, back:T], in0=src[:, :, 0:T - back], scalar=w,
                                        in1=dst[:, :, back:T], op0=ALU.mult, op1=ALU.add)
                            op.then_inc(tap if back < DC - 1 else conv_done, 1)
                    dve.wait_ge(low_ready, v + 1)
                    nc.vector.tensor_copy(bcp[:, :], bcf[0:P, :]).then_inc(split1, 1)
                    dve.wait_ge(split1, v + 1)
                    nc.vector.tensor_tensor(bcr[:, :], bcf[0:P, :], bcp[:, :], ALU.subtract).then_inc(split2, 1)
                    dve.wait_ge(split2, v + 1)
                    nc.vector.tensor_copy(mid[:, :], bcr[:, :]).then_inc(split3, 1)
                    dve.wait_ge(split3, v + 1)
                    nc.vector.tensor_copy(bcp[32:64, :], mid[32:64, :])
                    nc.vector.tensor_tensor(bcp[64:96, :], bcr[64:96, :], mid[64:96, :], ALU.subtract)\
                        .then_inc(bcp_ready, 1)
                    nc.vector.sem_inc(entered[1], 1)
                    with dve.Fori(0, DS // 2) as j:
                        for e in range(2):
                            n = v * DS + j * 2 + e
                            dve.wait_ge(c_summed, n + 1)
                            nc.vector.tensor_copy(two(cb[:, ds(j * 2 + e, 1), :].rearrange("p a t -> p (a t)")),
                                                  PS[:, 4 + 2 * e:6 + 2 * e, 0:HW]).then_inc(c_ready, 1)
                    dve.wait_ge(dt_log, v + 1)
                    nc.vector.scalar_tensor_tensor(
                        out=dt[:, :, :].rearrange("p c t -> p (c t)"), in0=dt[:, :, :].rearrange("p c t -> p (c t)"),
                        scalar=0.0, in1=sp[:, :, :].rearrange("p c t -> p (c t)"), op0=ALU.max, op1=ALU.add)\
                        .then_inc(dt_ready, 1)
                    dve.wait_ge(dt_ready, v + 1)
                    nc.vector.tensor_tensor(us[:, :, :], dt[:, :, :], xs[:, :, :], ALU.mult).then_inc(us_ready, 1)
                    dve.wait_ge(us_ready, v + 1)
                    nc.vector.memset(dt[:, :, :].rearrange("p c (b t) -> p (c b) t", t=T)[:, :, 0:1], RESTART)\
                        .then_inc(restart, 1)
                    dve.wait_ge(b_ready, v * DS + (DS + 2))
                    dve.wait_ge(us_ready, v + 1)
                    nc.vector.sem_inc(entered[1], 1)
                    def finish(c):
                        dve.wait_ge(reduced, (v * CT + c) * SP2 + (SP2 + 2))
                        nc.vector.scalar_tensor_tensor(
                            out=two(xs[:, c, :]), in0=two(xs[:, c, :]), scalar=cvec[:, c, DC + 2:DC + 3],
                            in1=PS[:, 6:8, 0:HW], op0=ALU.mult, op1=ALU.add).then_inc(y_taken, 1)

                    for c in range(CT):
                        vc = v * CT + c
                        u0 = vc * SP2
                        if c:
                            dve.wait_ge(dbx_ready, u0)
                        nc.vector.tensor_copy(u_ps, us[:, c, :]).then_inc(u_ready, 1)
                        dve.wait_ge(u_ready, vc + 1)

                        def inject(n):
                            dve.wait_ge(scanned, u0 + (n + 1))
                            nc.vector.tensor_tensor(dbx[n % 2].rearrange("p (a t) -> p a t", t=QW),
                                                    bcast(u_ps, 1, [128, 2, QW]), bb[:, 2 * n:2 * n + 2, :],
                                                    ALU.mult).then_inc(dbx_ready, 1)

                        inject(0)
                        for n in range(SP2):
                            if n + 1 < SP2:
                                inject(n + 1)
                            dve.wait_ge(da_ready, u0 + (n + 1))
                            dve.wait_ge(dbx_ready, u0 + (n + 1))
                            dve.wait_ge(weighted, u0 + (n + 1))
                            nc.vector.tensor_tensor_scan(out=hs[:, n % 2, :], data0=da[:, n % 2, :], data1=dbx[n % 2],
                                                         initial=0.0, op0=ALU.mult, op1=ALU.add).then_inc(scanned, 1)
                            if c and n == 1:
                                finish(c - 1)
                    finish(CT - 1)
                    dve.wait_ge(y_taken, v * CT + (CT + 1))
                    nc.vector.tensor_tensor(xs[:, :, :], xs[:, :, :], sz[:, :, :], ALU.mult).then_inc(gated, 1)
                    dve.wait_ge(out_summed, v + 1)
                    nc.vector.tensor_tensor(
                        ln.split(res[:, :, ds(q * QW, QW)]), ln.split(res[:, :, ds(q * QW, QW)]),
                        PS[0:P, 0:4, 0:HW].rearrange("p (k b) t -> p k b t", b=2), ALU.add).then_inc(res_ready, 1)
                    dve.wait_ge(res_ready, v + 1)
                nc.vector.sem_inc(layer_done, 1)
            dve.wait_ge(loaded, 32)
            last.dve(nc, dve, pairs(res))
            with dve.Fori(0, NPAIR) as i:
                nc.vector.tensor_tensor(last.xc(i), last.xc(i), last.scale(i), ALU.mult).then_inc(last_scaled, 1)
                dve.wait_ge(last_scaled, i + 1)
                for m in range(KD):
                    op = nc.vector.tensor_scalar(res[:, m, ds(i * PAIR, PAIR)], res[:, m, ds(i * PAIR, PAIR)],
                                                 fvec[:, 0, m:m + 1], fvec[:, 1, m:m + 1], ALU.mult, ALU.add)
                op.then_inc(gained, 1)
                dve.wait_ge(gained, i + (L * NQ + 1))
                nc.vector.tensor_tensor(pairs(h)(i), pairs(h)(i), last.xc(i), ALU.add).then_inc(h_ready, 1)
            dve.wait_ge(h_ready, NPAIR)


def experts(nc, dr, PS, C, h):
    E, EH = 8, 192
    G = E + 1
    TW = 94
    NT = N // TW
    SC = FF // 128
    NU = E * KD + SC
    with ExitStack() as ctx:
        s = Scope(nc, ctx, "moe")
        x = s.sb("x", [P, KD, N])
        xb = s.sb("xb", [P, KD, PAIR])
        wr = s.sb("wr", [P, KD, G])
        wg = s.sb("wg", [P, KD, E * EH])
        wu = s.sb("wu", [P, KD, E * EH])
        wd = s.sb("wd", [P, E * KD, D])
        wsg = s.sb("wsg", [P, KD, FF])
        wsu = s.sb("wsu", [P, KD, FF])
        wsd = s.sb("wsd", [128, SC, D])
        sgb = s.sb("sgb", [TW, 1])
        rank = s.sb("rank", [TW, E])
        pick = s.sb("pick", [G, G * 128])
        lg = s.sb("lg", [TW, NT, G])
        pr = s.sb("pr", [TW, NT, E])
        pr2 = s.sb("pr2", [TW, NT, E])
        c1 = s.sb("c1", [TW, NT, E])
        c2 = s.sb("c2", [TW, NT, E])
        m1 = s.sb("m1", [TW, NT])
        m2 = s.sb("m2", [TW, NT])
        mm_ = s.sb("mm_", [TW, NT])
        al = s.sb("al", [TW, NT])
        gates = s.sb("gates", [TW, NT, G])
        gT = s.sb("gT", [G, N])
        sg = s.sb("sg", [128, 2, PAIR])
        gu = s.sb("gu", [128, 2, PAIR])
        hid = s.sb("hid", [128, 2, PAIR])
        ln = NormAll(s, "ln", PS, C.ones, C.eps5, lambda i: x[:, :, ds(i * PAIR, PAIR)])
        xb_ready = s.sem("xb_ready")
        small, loaded, routed, logits, kept, shifted, exped, step, al_in, al_exp, gates_ready, turned, gT_ready, \
            gb_ready, gu_summed, silu_ready, gu_ready, hid_ready, down_done, h_ready = s.sems(
                "small", "loaded", "routed", "logits", "kept", "shifted", "exped", "step", "al_in", "al_exp",
                "gates_ready", "turned", "gT_ready", "gb_ready", "gu_summed", "silu_ready", "gu_ready", "hid_ready",
                "down_done", "h_ready")
        gate_asked = s.sem("gate_asked")
        smalls = [(wr[:, :, :], "moe_wr"), (rank[:, :], "moe_rank"), (pick[:, :], "moe_pick")]
        bigs = [(wg[:, :, :], "moe_wg"), (wu[:, :, :], "moe_wu"), (wd[:, :, :], "moe_wd"), (wsg[:, :, :], "moe_wsg"),
                (wsu[:, :, :], "moe_wsu"), (wsd[:, :, :], "moe_wsd")]
        NS, NBIG = 16 * (len(smalls) + 1), 16 * len(bigs)
        gcols = [slice(t % 5 * TW, (t % 5 + 1) * TW) for t in range(NT)]
        block = ctx.enter_context(nc.Block())

        @block.sync
        def _(sp):
            sp.dma_start(sgb[:, :], dr["moe_sgb"].partition_broadcast(TW)).then_inc(small, 16)
            for dst, name in smalls:
                sp.dma_start(dst, dr[name]).then_inc(small, 16)
            for dst, name in bigs:
                sp.dma_start(dst, dr[name]).then_inc(loaded, 16)
            sp.wait_ge(loaded, NBIG)

        @block.tensor
        def _(pe):
            pe.wait_ge(small, NS)
            ln.pe(nc, pe, lambda k, i: h[:, k, ds(i * PAIR, PAIR)])
            with pe.Fori(0, NPAIR) as i:
                pe.wait_ge(logits, i + 1)
                pe.wait_ge(xb_ready, i + 1)
                nc.tensor.sem_inc(gate_asked, 1)
                for t in range(3):
                    for k in range(KD):
                        mm = nc.tensor.matmul(PS[0:TW, 4, t * G:(t + 1) * G], xb[:, k, t * TW:(t + 1) * TW],
                                              wr[:, k, :], start=k == 0, stop=k == KD - 1)
                mm.then_inc(routed, 1)
            pe.wait_ge(gates_ready, 1)
            for t in range(NT):
                mm = nc.tensor.transpose(PS[0:G, t // 5, gcols[t]], gates[:, t, :], C.ident[0:TW, 0:TW])
            mm.then_inc(turned, 1)
            pe.wait_ge(gT_ready, 1)
            pe.wait_ge(loaded, NBIG)
            pe.wait_ge(kept, NPAIR + 1)
            with pe.Fori(0, NPAIR) as i:
                cols = ds(i * PAIR, PAIR)

                def down(u):
                    if u == 0:
                        pe.wait_ge(h_ready, i + 1)
                    pe.wait_ge(hid_ready, i * NU + (u + 2))
                    for m in range(KD):
                        if u < E * KD:
                            w, hd = wd[:, u, m * P:(m + 1) * P], hid[0:P, u % 2, :]
                        else:
                            w, hd = wsd[:, u - E * KD, m * P:(m + 1) * P], hid[:, u % 2, :]
                        mm = nc.tensor.matmul(PS[0:P, 6 + m, 0:PAIR], w, hd, start=u == 0, stop=u == NU - 1)
                    mm.then_inc(down_done, 1)
                    return mm

                for u in range(NU):
                    g = min(u // KD, E)
                    if u == g * KD:
                        pe.wait_ge(hid_ready, i * NU + (max(0, 2 * g - 2) + 1))
                        nc.tensor.sem_inc(gate_asked, 1)
                        nc.tensor.matmul(PS[:, 4 + g % 2, 0:PAIR], pick[:, g * 128:(g + 1) * 128], gT[:, cols],
                                         start=True, stop=True).then_inc(gb_ready, 1)
                    pe.wait_ge(gu_ready, i * NU + (u + 1))
                    for b, w in enumerate((wg, wu) if u < E * KD else (wsg, wsu)):
                        M = P if u < E * KD else 128
                        at = u * P if u < E * KD else (u - E * KD) * 128
                        for k in range(KD):
                            mm = nc.tensor.matmul(PS[0:M, u % 2 * 2 + b, 0:PAIR], w[:, k, at:at + M], x[:, k, cols],
                                                  start=k == 0, stop=k == KD - 1)
                    mm.then_inc(gu_summed, 1)
                    if u >= 2:
                        down(u - 2)
                down(NU - 2)
                down(NU - 1)

        @block.scalar
        def _(act):
            ln.act(nc, act)
            with act.Fori(0, NPAIR) as i:
                act.wait_ge(routed, i + 1)
                nc.scalar.activation(lg[:, ds(i * 3, 3), :], PS[0:TW, 4, 0:3 * G].rearrange("p (t g) -> p t g", g=G),
                                     ACT.Copy).then_inc(logits, 1)
            act.wait_ge(shifted, 1)
            nc.scalar.activation(pr[:, :, :], pr[:, :, :], ACT.Exp).then_inc(exped, 1)
            act.wait_ge(al_in, 1)
            nc.scalar.activation(al[:, :], al[:, :], ACT.Exp, scale=-1.0).then_inc(al_exp, 1)
            act.wait_ge(turned, 1)
            full = NT // 5
            nc.scalar.activation(gT[:, 0:full * 5 * TW].rearrange("p (a t) -> p a t", a=full),
                                 PS[0:G, 0:full, 0:5 * TW], ACT.Copy)
            nc.scalar.activation(gT[:, full * 5 * TW:N], PS[0:G, full, 0:(NT - full * 5) * TW], ACT.Copy)\
                .then_inc(gT_ready, 1)
            with act.Fori(0, NPAIR) as i:
                for u in range(NU):
                    M = P if u < E * KD else 128
                    act.wait_ge(gu_summed, i * NU + (u + 1))
                    act.wait_ge(gu_ready, i * NU + (u + 1))
                    nc.scalar.activation(sg[0:M, u % 2, :], PS[0:M, u % 2 * 2, 0:PAIR], ACT.Silu)\
                        .then_inc(silu_ready, 1)

        @block.gpsimd
        def _(pool):
            with pool.Fori(0, NPAIR) as i:
                pool.wait_ge(xb_ready, i + 1)
                nc.gpsimd.tensor_copy(x[:, :, ds(i * PAIR, PAIR)], xb[:, :, :]).then_inc(kept, 1)

        @block.vector
        def _(dve):
            nc.vector.sem_inc(gu_ready, 2)
            nc.vector.sem_inc(hid_ready, 1)
            nc.vector.sem_inc(down_done, 2)
            nc.vector.sem_inc(h_ready, 1)
            nc.vector.sem_inc(kept, 1)
            nc.vector.sem_inc(logits, 1)
            ln.dve(nc, dve, lambda i: h[:, :, ds(i * PAIR, PAIR)])
            with dve.Fori(0, NPAIR) as i:
                dve.wait_ge(kept, i + 1)
                dve.wait_ge(logits, i + 1)
                nc.vector.tensor_tensor(xb[:, :, :], x[:, :, ds(i * PAIR, PAIR)], ln.scale(i), ALU.mult)\
                    .then_inc(xb_ready, 1)
            dve.wait_ge(small, NS)
            dve.wait_ge(logits, NPAIR + 1)
            steps = [0]

            def link(op):
                steps[0] += 1
                op.then_inc(step, 1)
                dve.wait_ge(step, steps[0])

            V = nc.vector
            sh = [TW, NT, E]
            rk = bcast(rank[:, :], 1, sh)
            link(V.reduce_max(m1[:, :], lg[:, :, 0:E], AX.X))
            V.tensor_tensor(pr[:, :, :], lg[:, :, 0:E], bcast(m1[:, :], 2, sh), ALU.subtract).then_inc(shifted, 1)
            V.tensor_scalar(al[:, :], lg[:, :, E], sgb[:, 0:1], None, ALU.add).then_inc(al_in, 1)
            dve.wait_ge(exped, 1)
            link(V.reduce_sum(m1[:, :], pr[:, :, :], AX.X))
            link(V.reciprocal(m1[:, :], m1[:, :]))
            link(V.tensor_tensor(pr[:, :, :], pr[:, :, :], bcast(m1[:, :], 2, sh), ALU.mult))
            link(V.reduce_max(m1[:, :], pr[:, :, :], AX.X))
            link(V.tensor_tensor(c1[:, :, :], pr[:, :, :], bcast(m1[:, :], 2, sh), ALU.is_equal))
            link(V.tensor_tensor(c1[:, :, :], c1[:, :, :], rk, ALU.mult))
            link(V.reduce_max(mm_[:, :], c1[:, :, :], AX.X))
            link(V.tensor_tensor(c1[:, :, :], c1[:, :, :], bcast(mm_[:, :], 2, sh), ALU.is_equal))
            link(V.scalar_tensor_tensor(out=pr2[:, :, :], in0=c1[:, :, :], scalar=-2.0, in1=pr[:, :, :],
                                        op0=ALU.mult, op1=ALU.add))
            link(V.reduce_max(m2[:, :], pr2[:, :, :], AX.X))
            link(V.tensor_tensor(c2[:, :, :], pr2[:, :, :], bcast(m2[:, :], 2, sh), ALU.is_equal))
            link(V.tensor_tensor(c2[:, :, :], c2[:, :, :], rk, ALU.mult))
            link(V.reduce_max(mm_[:, :], c2[:, :, :], AX.X))
            link(V.tensor_tensor(c2[:, :, :], c2[:, :, :], bcast(mm_[:, :], 2, sh), ALU.is_equal))
            link(V.tensor_tensor(mm_[:, :], m1[:, :], m2[:, :], ALU.add))
            link(V.reciprocal(mm_[:, :], mm_[:, :]))
            dve.wait_ge(al_exp, 1)
            link(V.tensor_scalar(al[:, :], al[:, :], 1.0, None, ALU.add))
            link(V.reciprocal(gates[:, :, E], al[:, :]))
            link(V.tensor_scalar(al[:, :], gates[:, :, E], -1.0, 1.0, ALU.mult, ALU.add))
            link(V.tensor_tensor(m1[:, :], m1[:, :], mm_[:, :], ALU.mult))
            link(V.tensor_tensor(m2[:, :], m2[:, :], mm_[:, :], ALU.mult))
            link(V.tensor_tensor(c1[:, :, :], c1[:, :, :], bcast(m1[:, :], 2, sh), ALU.mult))
            link(V.tensor_tensor(c2[:, :, :], c2[:, :, :], bcast(m2[:, :], 2, sh), ALU.mult))
            link(V.tensor_tensor(c1[:, :, :], c1[:, :, :], c2[:, :, :], ALU.add))
            V.tensor_tensor(gates[:, :, 0:E], c1[:, :, :], bcast(al[:, :], 2, sh), ALU.mult).then_inc(gates_ready, 1)
            with dve.Fori(0, NPAIR) as i:
                for u in range(NU):
                    M = P if u < E * KD else 128
                    g = min(u // KD, E)
                    U = i * NU + u
                    dve.wait_ge(silu_ready, U + 1)
                    V.tensor_tensor(gu[0:M, u % 2, :], sg[0:M, u % 2, :], PS[0:M, u % 2 * 2 + 1, 0:PAIR], ALU.mult)\
                        .then_inc(gu_ready, 1)
                    dve.wait_ge(gu_ready, U + 3)
                    dve.wait_ge(gb_ready, i * G + (g + 1))
                    dve.wait_ge(down_done, U + 1)
                    V.tensor_tensor(hid[0:M, u % 2, :], gu[0:M, u % 2, :], PS[0:M, 4 + g % 2, 0:PAIR], ALU.mult)\
                        .then_inc(hid_ready, 1)
                dve.wait_ge(down_done, i * NU + (NU + 2))
                V.tensor_tensor(h[:, :, ds(i * PAIR, PAIR)], h[:, :, ds(i * PAIR, PAIR)], PS[0:P, 6:8, 0:PAIR],
                                ALU.add).then_inc(h_ready, 1)
            dve.wait_ge(h_ready, NPAIR + 1)


def attention(nc, dr, PS, C, h):
    TT = 71
    PT = 2 * TT
    STEP = 0.5 * DH ** -0.5
    TILT = STEP * DH ** -0.5
    EG = 8
    SH = 2 * NH
    with ExitStack() as ctx:
        s = Scope(nc, ctx, "att")
        wqk = s.sb("wqk", [P, KD, 2, QC * 128])
        wk = s.sb("wk", [P, KD, D])
        wv = s.sb("wv", [P, KD, QC * 128])
        wo = s.sb("wo", [P, KD, D])
        bo = s.sb("bo", [P, KD])
        mean_sel = s.sb("mean_sel", [128, 2, HP])
        xn = s.sb("xn", [P, KD, B + 1, PT])
        cur = s.sb("cur", [P, KD, PT])
        qk = s.sb("qk", [128, 2, QC, PT])
        qn = s.sb("qn", [128, 2, QC, PT])
        qs = s.sb("qs", [128, 4, QC, PT])
        keys = s.sb("keys", [TT, 2, D])
        tilt = s.sb("tilt", [128, 2, NH, 2, DH])
        spread_sel = s.sb("spread_sel", [2 * DH, 4, 128])
        v = s.sb("v", [128, 2, QC * 128])
        wvt = s.sb("wvt", [128, 2, 2, 2, DH, DH])
        ex = s.sb("ex", [TT, 3, 2, PT])
        mx = s.sb("mx", [TT, 3, 2])
        eT = s.sb("eT", [128, 3, 2, PT])
        inv = s.sb("inv", [2 * DH, 2, T])
        rb = s.sb("rb", [128, 2, 2, T])
        rat = s.sb("rat", [128, 2, 2, T])
        dif = s.sb("dif", [128, 2, T])
        absd = s.sb("absd", [128, 2, T])
        acc = s.sb("acc", [128, NH, 2])
        rs = s.sb("rs", [TT, 2, NH])
        rinv = s.sb("rinv", [TT, 2, NH])
        ob = s.sb("ob", [TT, 2, D])
        oT = s.sb("oT", [P, KD, PT])
        ln = NormAll(s, "ln", PS, C.ones, C.eps5, lambda i: xn[:, :, ds(i * 2, 2), 0:T],
                     view=lambda ap: ap.rearrange("p k (a t) -> p k a t", t=T))
        loaded, padded, qk_summed, qk_ready, kv_summed, keys_ready, tilt_ready, v_ready, scored, maxed, shifted, e_ready, \
            turned, eT_ready, wvt_ready, weights_summed, sums_ready, inverted, spread, rb_ready, ratio, differed, \
            acc_ready, w_summed, qs_ready, rowinv, mixed, oT_ready, projected, h_ready = s.sems(
                "loaded", "padded", "qk_summed", "qk_ready", "kv_summed", "keys_ready", "tilt_ready", "v_ready", "scored", "maxed",
                "shifted", "e_ready", "turned", "eT_ready", "wvt_ready", "weights_summed", "sums_ready",
                "inverted", "spread", "rb_ready", "ratio", "differed", "acc_ready", "w_summed", "qs_ready", "rowinv", "mixed", "oT_ready",
                "projected", "h_ready")
        ob_ready, o_turned, qn_ready = s.sems("ob_ready", "o_turned", "qn_ready")
        xn_ready, cur_ready, cur_used, entered = s.sems("xn_ready", "cur_ready", "cur_used", "entered")
        loads = [(wqk[:, :, :, :], "att_wqk"), (wk[:, :, :], "att_wk"), (wv[:, :, :], "att_wv"), (wo[:, :, :], "att_wo"),
                 (bo[:, :], "att_bo"), (mean_sel[:, :, :], "att_sel"), (spread_sel[:, :, :], "att_spread")]
        NLD, PADS = 16 * len(loads), 7
        acc_j = acc[:, :, :].rearrange("p (c j) g -> p j c g", j=4)
        block = ctx.enter_context(nc.Block())

        @block.sync
        def _(sp):
            for dst, name in loads:
                sp.dma_start(dst, dr[name]).then_inc(loaded, 16)
            sp.wait_ge(loaded, NLD)

        @block.tensor
        def _(pe):
            pe.wait_ge(loaded, NLD)
            pe.wait_ge(padded, PADS)
            ln.pe(nc, pe, lambda k, i: h[:, k, ds(i * PAIR, PAIR)])
            pe.wait_ge(xn_ready, NPAIR)
            nc.tensor.sem_inc(entered, 1)

            def queries_keys():
                for a in range(2):
                    for c in range(QC):
                        for k in range(KD):
                            mm = nc.tensor.matmul(PS[:, a, c * PT:(c + 1) * PT], wqk[:, k, a, c * 128:(c + 1) * 128],
                                                  cur[:, k, :], start=k == 0, stop=k == KD - 1)
                mm.then_inc(qk_summed, 1)

            pe.wait_ge(cur_ready, 1)
            queries_keys()
            with pe.Fori(0, B) as i:
                pe.wait_ge(h_ready, i + 1)
                pe.wait_ge(cur_ready, i + 1)
                nc.tensor.sem_inc(entered, 1)
                for bank, w, n in ((4, wk, D), (6, wv, QC * 128)):
                    for t in range(2):
                        for k in range(KD):
                            mm = nc.tensor.matmul(PS[0:TT, bank + t, 0:n], cur[:, k, t * TT:(t + 1) * TT], w[:, k, :],
                                                  start=k == 0, stop=k == KD - 1)
                mm.then_inc(kv_summed, 1)
                nc.tensor.sem_inc(cur_used, 1)
                pe.wait_ge(qk_ready, i + 1)

                def score(p, n):
                    H = i * SH + (p * NH + n)
                    c, r = n // 4, slice(HP * (n % 4), HP * (n % 4 + 1))
                    pe.wait_ge(shifted, H + 1)
                    for t in range(2):
                        q = qk[r, 0, c, t * TT:(t + 1) * TT] if p == 0 else qs[:, n % 4, c, t * TT:(t + 1) * TT]
                        k = qk[r, 1, c, 0:T] if p == 0 else qk[:, 1, c, 0:T]
                        mm = nc.tensor.matmul(PS[0:TT, n % 2, t * PT:t * PT + T], q, k, start=True, stop=True)
                    mm.then_inc(scored, 1)

                def turn(p, n):
                    H = i * SH + (p * NH + n)
                    pe.wait_ge(e_ready, H + 1)
                    pe.wait_ge(eT_ready, H + 1)
                    if p == 0 and n >= 2:
                        pe.wait_ge(inverted, i * NH + (n - 1))
                    for t in range(2):
                        for kt in range(2):
                            at = kt * PT + t * TT
                            mm = nc.tensor.transpose(PS[0:TT, 2 + n % 2, at:at + TT],
                                                     ex[:, n % 3, t, kt * TT:(kt + 1) * TT], C.ident[0:TT, 0:TT])
                    mm.then_inc(turned, 1)

                def spread_of(m):
                    pe.wait_ge(inverted, i * NH + (m + 1))
                    if m == 0:
                        pe.wait_ge(v_ready, i + 1)
                    for g in range(2):
                        pe.wait_ge(rb_ready, (i * NH + m) * 2 + (g + 1))
                        for sign in range(2):
                            mm = nc.tensor.matmul(PS[:, 6 + g, sign * PT:sign * PT + T],
                                                  spread_sel[:, 2 * g + sign, :], inv[:, m % 2, :],
                                                  start=True, stop=True)
                        mm.then_inc(spread, 1)

                def weights_of(m):
                    pe.wait_ge(eT_ready, i * SH + (m + 3))
                    pe.wait_ge(tilt_ready, i + 1)
                    for kt in range(2):
                        mm = nc.tensor.matmul(PS[0:2 * DH, 2 + m % 2, 2 * PT:2 * PT + T],
                                              tilt[:, kt, m, :, :].rearrange("p s e -> p (s e)"),
                                              eT[:, m % 3, kt, 0:T], start=kt == 0, stop=kt == 1)
                    mm.then_inc(weights_summed, 1)

                def values_of(m):
                    pe.wait_ge(wvt_ready, i * NH + (m + 1))
                    for g in range(2):
                        pe.wait_ge(ratio, (i * NH + m) * 2 + (g + 1))
                        for sign in range(2):
                            for kt in range(2):
                                mm = nc.tensor.matmul(
                                    PS[:, 4 + g, sign * PT:sign * PT + T],
                                    wvt[:, m % 2, kt, sign, g * EG:(g + 1) * EG, :].rearrange("p e d -> p (e d)"),
                                    eT[:, m % 3, kt, 0:T], start=kt == 0, stop=kt == 1)
                        mm.then_inc(sums_ready, 1)

                for n in range(NH + 3):
                    if n < NH:
                        score(0, n)
                    if 1 <= n <= NH:
                        turn(0, n - 1)
                    if n >= 3:
                        spread_of(n - 3)
                    if 2 <= n <= NH + 1:
                        weights_of(n - 2)
                    if n >= 3:
                        values_of(n - 3)
                pe.wait_ge(shifted, i * SH + (NH + 2))
                pe.wait_ge(cur_ready, i + 2)
                queries_keys()
                pe.wait_ge(acc_ready, (i + 1) * 2 * NH)
                for j in range(4):
                    for g in range(2):
                        mm = nc.tensor.matmul(PS[HP * j:HP * (j + 1), 4, 0:QC], mean_sel[:, g, :], acc_j[:, j, :, g],
                                              start=g == 0, stop=g == 1)
                mm.then_inc(w_summed, 1)
                pe.wait_ge(rb_ready, (i + 1) * 2 * NH + 2)

                def keep_clock(n):
                    for _ in range(n):
                        nc.tensor.matmul(PS[:, 7, 0:2 * PT], C.ident[:, :],
                                         qk[:, 1, 0:2, :].rearrange("p c t -> p (c t)"), start=True, stop=True)

                keep_clock(3)
                pe.wait_ge(qs_ready, i + 1)
                pe.wait_ge(qn_ready, i + 2)
                for n in range(NH + 3):
                    if n < NH:
                        score(1, n)
                        if n <= 2:
                            keep_clock(1)
                    if 2 <= n <= NH + 1:
                        turn(1, n - 2)
                    if n >= 3:
                        m = n - 3
                        pe.wait_ge(eT_ready, i * SH + (NH + m + 3))
                        for qt in range(2):
                            for kt in range(2):
                                mm = nc.tensor.matmul(PS[0:TT, 5, qt * D + m * DH:qt * D + (m + 1) * DH],
                                                      eT[:, m % 3, kt, qt * TT:(qt + 1) * TT],
                                                      v[:, kt, m * HP:m * HP + DH], start=kt == 0, stop=kt == 1)
                        mm.then_inc(mixed, 1)
                keep_clock(2)
                pe.wait_ge(loaded, NLD)
                pe.wait_ge(ob_ready, i + 1)
                for k in range(KD):
                    for qt in range(2):
                        mm = nc.tensor.transpose(PS[0:P, 6, k * PT + qt * TT:k * PT + (qt + 1) * TT],
                                                 ob[:, qt, k * P:(k + 1) * P], C.ident[0:TT, 0:TT])
                mm.then_inc(o_turned, 1)
                keep_clock(1)
                pe.wait_ge(oT_ready, i + 1)
                for m in range(KD):
                    for k in range(KD):
                        mm = nc.tensor.matmul(PS[0:P, 7, m * PT:m * PT + T], wo[:, k, m * P:(m + 1) * P],
                                              oT[:, k, 0:T], start=k == 0, stop=k == KD - 1)
                mm.then_inc(projected, 1)

        @block.scalar
        def _(act):
            ln.act(nc, act)

            def keep_next(v):
                act.wait_ge(qk_summed, v)
                nc.scalar.activation(qn[:, :, :, :].rearrange("p a c t -> p a (c t)"), PS[:, 0:2, 0:QC * PT], ACT.Copy)\
                    .then_inc(qn_ready, 1)

            keep_next(1)
            with act.Fori(0, B) as i:
                act.wait_ge(h_ready, i + 1)
                act.wait_ge(qn_ready, i + 1)
                nc.scalar.activation(qk[:, :, :, :], qn[:, :, :, :], ACT.Copy).then_inc(qk_ready, 1)
                act.wait_ge(kv_summed, i + 1)
                nc.scalar.activation(keys[:, :, :], PS[0:TT, 4:6, 0:D], ACT.Copy).then_inc(keys_ready, 1)
                act.wait_ge(keys_ready, i + 1)

                for sign in range(2):
                    op = nc.scalar.activation(tilt[0:TT, :, :, sign, :],
                                              keys[:, :, :].rearrange("p a (n e) -> p a n e", e=DH), ACT.Exp,
                                              scale=TILT * (1 - 2 * sign))
                op.then_inc(tilt_ready, 1)

                def exp_of(p, n):
                    H = i * SH + (p * NH + n)
                    act.wait_ge(shifted, H + 3)
                    if p == 0:
                        nc.scalar.activation(ex[:, n % 3, :, 0:T], ex[:, n % 3, :, 0:T], ACT.Exp, scale=DH ** -0.5)\
                            .then_inc(e_ready, 1)
                    else:
                        for t in range(2):
                            op = nc.scalar.activation(ex[:, n % 3, t, 0:T], ex[:, n % 3, t, 0:T], ACT.Exp,
                                                      scale=DH ** -0.5, accum_out=rs[:, t, n:n + 1])
                        op.then_inc(e_ready, 1)

                def keep_turned(p, n):
                    H = i * SH + (p * NH + n)
                    act.wait_ge(turned, H + 1)
                    if p == 0:
                        act.wait_ge(sums_ready, (i * NH + n) * 2 + 2)
                    elif n < 3:
                        act.wait_ge(sums_ready, (i + 1) * 2 * NH + 6)
                    else:
                        act.wait_ge(mixed, i * NH + (n - 2))
                    nc.scalar.activation(eT[0:TT, n % 3, :, :].rearrange("p a t -> p (a t)"),
                                         PS[0:TT, 2 + n % 2, 0:2 * PT], ACT.Copy).then_inc(eT_ready, 1)

                for n in range(NH + 4):
                    if 1 <= n <= NH:
                        keep_turned(0, n - 1)
                    if 3 <= n <= NH + 2:
                        for g in range(2):
                            M = (i * NH + (n - 3)) * 2 + g
                            act.wait_ge(spread, M + 1)
                            act.wait_ge(ratio, M + 1)
                            nc.scalar.activation(rb[:, g, :, :], PS[:, 6 + g, 0:2 * PT].rearrange(
                                "p (a t) -> p a t", t=PT)[:, :, 0:T], ACT.Copy).then_inc(rb_ready, 1)
                    if n < NH:
                        exp_of(0, n)
                    if n >= 4:
                        m = n - 4
                        for g in range(2):
                            act.wait_ge(differed, (i * NH + m) * 2 + (g + 1))
                            nc.scalar.activation(absd[:, g, :], dif[:, g, :], ACT.Abs, accum_out=acc[:, m, g:g + 1])\
                                .then_inc(acc_ready, 1)
                act.wait_ge(qk_ready, i + 1)
                keep_next(i + 2)
                for n in range(NH + 2):
                    if n >= 2:
                        keep_turned(1, n - 2)
                    if n < NH:
                        exp_of(1, n)
                act.wait_ge(o_turned, i + 1)
                nc.scalar.activation(oT[:, :, :].rearrange("p c t -> p (c t)"), PS[0:P, 6, 0:KD * PT], ACT.Copy)\
                    .then_inc(oT_ready, 1)

        @block.gpsimd
        def _(pool):
            pool.memset(xn[:, :, B, :], 0.0)
            pool.memset(xn[:, :, 0:B, T:PT], 0.0).then_inc(padded, 1)
            pool.memset(ex[:, :, :, T:PT], 0.0).then_inc(padded, 1)
            pool.memset(tilt[:, :, :, :, :], 0.0).then_inc(padded, 1)
            pool.memset(wvt[:, :, :, :, :, :], 0.0).then_inc(padded, 1)
            pool.memset(v[:, :, :], 0.0).then_inc(padded, 1)
            pool.memset(qs[:, :, :, :], 0.0).then_inc(padded, 1)
            pool.memset(eT[:, :, :, :], 0.0).then_inc(padded, 1)
            pool.wait_ge(padded, PADS)
            pool.wait_ge(xn_ready, NPAIR)
            pool.sem_inc(padded, 1)
            with pool.Fori(0, B) as i:
                pool.wait_ge(cur_used, i + 1)
                pool.tensor_copy(cur[:, :, :], xn[:, :, ds(i, 1), :].rearrange("p k a t -> p k (a t)")).then_inc(cur_ready, 1)
                pool.wait_ge(v_ready, i + 1)
                pool.wait_ge(tilt_ready, i + 1)
                for n in range(NH):
                    pool.wait_ge(sums_ready, (i * NH + n) * 2 + 4)
                    for kt in range(2):
                        op = nc.gpsimd.tensor_tensor(
                            wvt[0:TT, n % 2, kt, :, :, :].rearrange("p s e d -> p (s e) d"),
                            bcast(tilt[0:TT, kt, n, :, :].rearrange("p s e -> p (s e)"), 2, [TT, 2 * DH, DH]),
                            bcast(v[0:TT, kt, n * HP:n * HP + DH], 1, [TT, 2 * DH, DH]), ALU.mult)
                    op.then_inc(wvt_ready, 1)
            pool.wait_ge(cur_used, B + 1)
            pool.tensor_copy(cur[:, :, :], xn[:, :, B, :]).then_inc(cur_ready, 1)

        @block.vector
        def _(dve):
            V = nc.vector
            V.sem_inc(shifted, 2)
            V.sem_inc(eT_ready, 2)
            V.sem_inc(ratio, 2)
            V.sem_inc(rb_ready, 2)
            V.sem_inc(sums_ready, 6)
            V.sem_inc(h_ready, 1)
            V.sem_inc(cur_used, 1)
            ln.dve(nc, dve, lambda i: h[:, :, ds(i * PAIR, PAIR)])
            with dve.Fori(0, NPAIR) as i:
                V.tensor_tensor(ln.xc(i), ln.xc(i), ln.scale(i), ALU.mult).then_inc(xn_ready, 1)
            with dve.Fori(0, B) as i:
                dve.wait_ge(kv_summed, i + 1)
                V.tensor_copy(v[0:TT, :, :], PS[0:TT, 6:8, 0:QC * 128]).then_inc(v_ready, 1)

                def shift(p, n):
                    H = i * SH + (p * NH + n)
                    dve.wait_ge(scored, H + 1)
                    sc = PS[0:TT, n % 2, 0:2 * PT].rearrange("p (a t) -> p a t", t=PT)[:, :, 0:T]
                    V.reduce_max(mx[:, n % 3, :], sc, AX.X).then_inc(maxed, 1)
                    dve.wait_ge(maxed, H + 1)
                    if p == 1 or n >= 3:
                        dve.wait_ge(turned, H - 2)
                    V.tensor_tensor(ex[:, n % 3, :, 0:T], sc, bcast(mx[:, n % 3, :], 2, [TT, 2, T]), ALU.subtract)\
                        .then_inc(shifted, 1)

                for n in range(NH + 3):
                    if n < NH:
                        shift(0, n)
                    if 2 <= n <= NH + 1:
                        m = n - 2
                        dve.wait_ge(weights_summed, i * NH + (m + 1))
                        V.reciprocal(inv[:, m % 2, :], PS[0:2 * DH, 2 + m % 2, 2 * PT:2 * PT + T]).then_inc(inverted, 1)
                    if n >= 3:
                        m = n - 3
                        M = (i * NH + m) * 2
                        for g in range(2):
                            dve.wait_ge(sums_ready, M + (g + 7))
                            dve.wait_ge(rb_ready, M + (g + 3))
                            if m >= 1:
                                dve.wait_ge(differed, M + (g - 1))
                            V.tensor_tensor(rat[:, g, :, :], rb[:, g, :, :], PS[:, 4 + g, 0:2 * PT].rearrange(
                                "p (a t) -> p a t", t=PT)[:, :, 0:T], ALU.mult).then_inc(ratio, 1)
                        for g in range(2):
                            dve.wait_ge(ratio, M + (g + 3))
                            if m >= 1:
                                dve.wait_ge(acc_ready, M + (g - 1))
                            V.tensor_tensor(dif[:, g, :], rat[:, g, 0, :], rat[:, g, 1, :], ALU.subtract)\
                                .then_inc(differed, 1)
                dve.wait_ge(w_summed, i + 1)
                for j in range(4):
                    r = slice(HP * j, HP * (j + 1))
                    op = V.tensor_tensor(qs[r, j, :, :], qk[r, 0, :, :], bcast(PS[r, 4, 0:QC], 2, [HP, QC, PT]),
                                         ALU.mult)
                op.then_inc(qs_ready, 1)
                for n in range(NH):
                    shift(1, n)
                dve.wait_ge(e_ready, (i + 1) * SH)
                V.reciprocal(rinv[:, :, :], rs[:, :, :]).then_inc(rowinv, 1)
                dve.wait_ge(rowinv, i + 1)
                dve.wait_ge(mixed, (i + 1) * NH)
                V.tensor_tensor(ob[:, :, :].rearrange("p a (n e) -> p (a n) e", e=DH),
                                PS[0:TT, 5, 0:2 * D].rearrange("p (n e) -> p n e", e=DH),
                                bcast(rinv[:, :, :].rearrange("p a n -> p (a n)"), 2, [TT, 2 * NH, DH]),
                                ALU.mult).then_inc(ob_ready, 1)
                dve.wait_ge(projected, i + 1)
                for m in range(KD):
                    op = V.scalar_tensor_tensor(out=h[:, m, ds(i * T, T)], in0=PS[0:P, 7, m * PT:m * PT + T],
                                                scalar=bo[:, m:m + 1], in1=h[:, m, ds(i * T, T)],
                                                op0=ALU.add, op1=ALU.add)
                op.then_inc(h_ready, 1)
                dve.wait_ge(h_ready, i + 2)


def switch(nc, dr, PS, C, h):
    E, CAP = 16, 64
    TW = 94
    NT = N // TW
    BLOCKS = [(0, 0), (0, 1), (1, 1), (1, 2), (2, 2)]
    TR = 128
    ET = B * CAP // TR
    U = 4
    TILES = -(-(N // TR + E) // U) * U
    BEHIND = (TILES + 1) * TR
    with ExitStack() as ctx:
        s = Scope(nc, ctx, "sw")
        slots = nc.dram_tensor("sw_slots", (BEHIND + N, D), F32, kind="Internal").ap()
        nb = s.sb("nb", [P, KD, PAIR])
        lnw = s.sb("lnw", [P, KD])
        wr = s.sb("wr", [P, KD, E])
        wi = s.sb("wi", [P, U, KD, FF])
        wo = s.sb("wo", [128, U, FC, D])
        zero = s.sb("zero", [TR, D])
        token = s.sb("token", [TW, NT])
        carry = s.sb("carry", [TW, E, NT])
        every = s.sb("every", [TW, TW])
        filled = s.sb("filled", [TW, ET])
        tile_no = s.sb("tile_no", [1, TILES])
        normed = s.sb("normed", [TW, NT, D])
        oh = s.sb("oh", [TW, NT, E])
        kept = s.sb("kept", [TW, NT, E])
        totals = s.sb("totals", [TW, E, NT])
        sofar = s.sb("sofar", [TW, E, NT])
        full = s.sb("full", [TW, E, ET])
        ntiles = s.sb("ntiles", [TW, E])
        tiles_to = s.sb("tiles_to", [TW, E])
        base = s.sb("base", [TW, E])
        row = s.sb("row", [TW, NT, E])
        dest = s.sb("dest", [TW, NT])
        dest_i = s.sb("dest_i", [TW, NT], I32)
        passed = s.sb("passed", [1, TILES, E])
        whose = s.sb("whose", [1, TILES])
        whose_i = s.sb("whose_i", [1, TILES], I32)
        xt = s.sb("xt", [TR, 2, D])
        xT = s.sb("xT", [P, 2, KD, TR])
        hid = s.sb("hid", [128, 2, FC, TR])
        yt = s.sb("yt", [TR, 2, D])
        back = s.sb("back", [TW, 4, D])
        rank = s.sb("rank", [TW, E])
        upto = s.sb("upto", [TW, len(BLOCKS), TW])
        lg = s.sb("lg", [TW, NT, E])
        m1 = s.sb("m1", [TW, NT])
        m2 = s.sb("m2", [TW, NT])
        eps6 = s.sb("eps6", [P, 1])
        x = s.sb("x", [P, KD, N])
        pairs = lambda i: x[:, :, ds(i * PAIR, PAIR)]
        ln = NormAll(s, "ln", PS, C.ones, C.eps5, pairs)
        nb_ready, x_ready = s.sems("nb_ready", "x_ready")
        rms = NormAll(s, "rms", PS, C.ones, eps6, pairs, center=False)
        small, eps_ready, summed, weighted, routed, logits, turned, normed_ready, shifted, exped, step, oh_ready, \
            counted, kept_ready, ranked, sorted_, zeroed, scattered, xt_turned, xT_ready, up_summed, hid_ready, \
            down_summed, y_ready, y_free, scaled, back_turned, h_ready, entered = s.sems(
                "small", "eps_ready", "summed", "weighted", "routed", "logits", "turned", "normed_ready", "shifted",
                "exped", "step", "oh_ready", "counted", "kept_ready", "ranked", "sorted", "zeroed", "scattered",
                "xt_turned", "xT_ready", "up_summed", "hid_ready", "down_summed", "y_ready", "y_free", "scaled",
                "back_turned", "h_ready", "entered")
        wloaded = s.sems(*(f"wloaded{b}" for b in range(U)))
        xloaded = s.sems("xloaded0", "xloaded1")
        ystored = s.sems("ystored0", "ystored1")
        gathered = s.sems(*(f"gathered{b}" for b in range(4)))
        smalls = [(lnw[:, :], "sw_lnw"), (wr[:, :, :], "sw_wr"), (rank[:, :], "sw_rank"), (upto[:, :, :], "sw_upto"),
                  (token[:, :], "sw_token"), (carry[:, :, :], "sw_carry"), (every[:, :], "sw_every"),
                  (filled[:, :], "sw_filled"), (tile_no[:, :], "sw_tile_no")]
        NS = 16 * len(smalls)
        block = ctx.enter_context(nc.Block())

        @block.sync
        def _(sp):
            for dst, name in smalls:
                sp.dma_start(dst, dr[name]).then_inc(small, 16)
            sp.wait_ge(zeroed, 1)
            for r0 in range(0, BEHIND + N, TR):
                rows = min(TR, BEHIND + N - r0)
                sp.dma_start(slots[r0:r0 + rows], zero[0:rows, :]).then_inc(zeroed, 16)
            sp.wait_ge(sorted_, 1)
            sp.wait_ge(scattered, 16 * NT)
            sp.dma_start(xt[:, 0, :], slots[0:TR]).then_inc(xloaded[0], 16)
            with sp.Fori(0, TILES // U) as mm:
                for b in range(U):
                    m = mm * U + b
                    sp.wait_ge(down_summed, m + 1)
                    e = sp.value_load(whose_i[0:1, ds(m, 1)], min_val=0, max_val=E - 1)
                    sp.dma_start(wi[:, b, :, :], dr["sw_wi"][ds(e, 1)].rearrange("a p k f -> (a p) k f"))\
                        .then_inc(wloaded[b], 16)
                    sp.dma_start(wo[:, b, :, :], dr["sw_wo"][ds(e, 1)].rearrange("a p k f -> (a p) k f"))\
                        .then_inc(wloaded[b], 16)
                    sp.wait_ge(xt_turned, m + 2)
                    x = (b + 1) % 2
                    sp.dma_start(xt[:, x, :], slots[ds((m + 1) * TR, TR)]).then_inc(xloaded[x], 16)
            for b in range(U):
                sp.wait_ge(wloaded[b], TILES // U * 32)
            sp.wait_ge(xloaded[0], (TILES // 2 + 1) * 16)
            sp.wait_ge(xloaded[1], TILES // 2 * 16)

        @block.tensor
        def _(pe):
            pe.wait_ge(small, NS)
            ln.pe(nc, pe, lambda k, i: h[:, k, ds(i * PAIR, PAIR)])
            rms.pe(nc, pe, None)
            with pe.Fori(0, NPAIR) as i:
                pe.wait_ge(logits, i + 1)
                pe.wait_ge(weighted, i + 1)
                for t in range(3):
                    for k in range(KD):
                        mm = nc.tensor.matmul(PS[0:TW, 4, t * E:(t + 1) * E], nb[:, k, t * TW:(t + 1) * TW],
                                              wr[:, k, :], start=k == 0, stop=k == KD - 1)
                mm.then_inc(routed, 1)
                pe.wait_ge(normed_ready, i + 1)
                nc.tensor.sem_inc(entered, 1)
                for t in range(3):
                    for k in range(KD):
                        mm = nc.tensor.transpose(PS[0:TW, 5 + t, k * P:(k + 1) * P], nb[:, k, t * TW:(t + 1) * TW],
                                                 C.ident[0:P, 0:P])
                mm.then_inc(turned, 1)
            pe.wait_ge(oh_ready, 1)
            pe.wait_ge(normed_ready, NPAIR + 1)
            ohp = oh[:, :, :].rearrange("p (i t) e -> p t i e", t=3)
            for t in range(3):
                srcs = [(n, a) for n, (a, b) in enumerate(BLOCKS) if b == t]
                for n, a in srcs:
                    mm = nc.tensor.matmul(PS[0:TW, 5 + t, 0:NPAIR * E], upto[:, n, :], ohp[:, a, :, :],
                                          start=n == srcs[0][0], stop=n == srcs[-1][0])
            mm.then_inc(counted, 1)
            pe.wait_ge(kept_ready, 1)
            nc.tensor.matmul(PS[0:TW, 0, 0:NT * E], upto[:, 0, :], kept[:, :, :], start=True, stop=True)
            nc.tensor.matmul(PS[0:TW, 1, 0:NT * E], every[:, :], kept[:, :, :], start=True, stop=True)\
                .then_inc(ranked, 1)
            pe.wait_ge(sorted_, 1)

            def turn(m, x):
                pe.wait_ge(xT_ready, m + 1)
                nc.tensor.sem_inc(entered, 1)
                for k in range(KD):
                    op = nc.tensor.transpose(PS[0:P, 4 * x, k * TR:(k + 1) * TR], xt[:, x, k * P:(k + 1) * P],
                                             C.ident[:, :])
                op.then_inc(xt_turned, 1)

            pe.wait_ge(xloaded[0], 16)
            turn(0, 0)
            with pe.Fori(0, TILES // U) as mm:
                for b in range(U):
                    m, a = mm * U + b, b % 2
                    pe.wait_ge(xT_ready, m + 3)
                    pe.wait_ge(wloaded[b], mm * 32 + 32)
                    nc.tensor.sem_inc(entered, 1)
                    for j in range(FC):
                        if j % 4 == 0:
                            pe.wait_ge(hid_ready, m * 2 + (j // 4 + 1))
                        for k in range(KD):
                            op = nc.tensor.matmul(PS[:, 4 * a + 1 + j // 4, j % 4 * TR:(j % 4 + 1) * TR],
                                                  wi[:, b, k, j * 128:(j + 1) * 128], xT[:, a, k, :],
                                                  start=k == 0, stop=k == KD - 1)
                        if j in (3, FC - 1):
                            op.then_inc(up_summed, 1)
                    pe.wait_ge(xloaded[1 - a], (mm * 2 + (b + 1) // 2) * 16 + 16 * a if a else mm * 32 + (b // 2) * 16 + 16)
                    turn(m + 1, 1 - a)
                    pe.wait_ge(y_ready, m + 1)
                    for j in range(FC):
                        if j % 4 == 0:
                            pe.wait_ge(hid_ready, m * 2 + (j // 4 + 5))
                            nc.tensor.sem_inc(entered, 1)
                        op = nc.tensor.matmul(PS[:, 4 * a + 3, 0:D], hid[:, a, j, :], wo[:, b, j, :],
                                              start=j == 0, stop=j == FC - 1)
                    op.then_inc(down_summed, 1)
            pe.wait_ge(y_ready, TILES + 2)
            pe.wait_ge(xT_ready, TILES + 3)
            with pe.Fori(0, NT // 4) as tt:
                for o in range(4):
                    pe.wait_ge(scaled, tt * 4 + (o + 1))
                    pe.wait_ge(h_ready, tt * 4 + (o + 1))
                    nc.tensor.sem_inc(entered, 1)
                    for k in range(KD):
                        op = nc.tensor.transpose(PS[0:P, o % 2, k * TW:(k + 1) * TW],
                                                 back[:, o, k * P:(k + 1) * P],
                                                 C.ident[0:TW, 0:TW])
                    op.then_inc(back_turned, 1)

        @block.scalar
        def _(act):
            act.wait_ge(eps_ready, 1)
            ln.act(nc, act)
            act.wait_ge(x_ready, NPAIR)
            rms.act(nc, act)
            with act.Fori(0, NPAIR) as i:
                act.wait_ge(routed, i + 1)
                nc.scalar.activation(lg[:, ds(i * 3, 3), :], PS[0:TW, 4, 0:3 * E].rearrange("p (t g) -> p t g", g=E),
                                     ACT.Copy).then_inc(logits, 1)
                act.wait_ge(turned, i + 2)
                nc.scalar.activation(normed[:, ds(i * 3, 3), :], PS[0:TW, 5:8, 0:D], ACT.Copy).then_inc(normed_ready, 1)
            act.wait_ge(shifted, 1)
            nc.scalar.activation(lg[:, :, :], lg[:, :, :], ACT.Exp).then_inc(exped, 1)
            act.wait_ge(xt_turned, 3)
            nc.scalar.activation(xT[:, 0, :, :].rearrange("p k t -> p (k t)"), PS[0:P, 0, 0:KD * TR], ACT.Copy)\
                .then_inc(xT_ready, 1)
            with act.Fori(0, TILES // U) as mm:
                for b in range(U):
                    m, a = mm * U + b, b % 2
                    act.wait_ge(down_summed, m + 3)
                    act.wait_ge(up_summed, m * 2 + 1)
                    nc.scalar.activation(hid[:, a, 0:4, :].rearrange("p j t -> p (j t)"), PS[:, 4 * a + 1, :],
                                         ACT.Relu).then_inc(hid_ready, 1)
                    act.wait_ge(up_summed, m * 2 + 2)
                    nc.scalar.activation(hid[:, a, 4:FC, :].rearrange("p j t -> p (j t)"),
                                         PS[:, 4 * a + 2, 0:(FC - 4) * TR], ACT.Relu).then_inc(hid_ready, 1)
                    act.wait_ge(xt_turned, m + 4)
                    nc.scalar.activation(xT[:, 1 - a, :, :].rearrange("p k t -> p (k t)"),
                                         PS[0:P, 4 * (1 - a), 0:KD * TR], ACT.Copy).then_inc(xT_ready, 1)

        @block.gpsimd
        def _(pool):
            pool.memset(zero[:, :], 0.0).then_inc(zeroed, 1)
            pool.wait_ge(zeroed, 1 + 16 * -(-(BEHIND + N) // TR))
            pool.wait_ge(sorted_, 1)
            pool.wait_ge(normed_ready, NPAIR + 1)
            for t in range(NT):
                pool.indirect_dma_start(slots[:, :], bass.IndirectOffsetOnAxis(ap=dest_i[:, t:t + 1], axis=0),
                                        normed[:, t, :], None).then_inc(scattered, 16)
            with pool.Fori(0, TILES // U) as mm:
                for b in range(U):
                    pool.wait_ge(y_ready, mm * U + (b + 3))
                    pool.dma_start(slots[ds((mm * U + b) * TR, TR)], yt[:, b % 2, :]).then_inc(ystored[b % 2], 16)
                    pool.wait_ge(ystored[b % 2], mm * 32 + (b // 2 + 1) * 16)
                    nc.gpsimd.sem_inc(y_free, 1)
            for b in range(2):
                pool.wait_ge(ystored[b], TILES // 2 * 16)
            pool.wait_ge(scattered, 16 * NT)
            for t in range(NT):
                if t >= 4:
                    pool.wait_ge(back_turned, t - 3)
                pool.indirect_dma_start(back[:, t % 4, :], None, slots[:, :],
                                        bass.IndirectOffsetOnAxis(ap=dest_i[:, t:t + 1], axis=0))\
                    .then_inc(gathered[t % 4], 16)
            for b in range(4):
                pool.wait_ge(gathered[b], NT // 4 * 16)

        @block.vector
        def _(dve):
            V = nc.vector
            V.memset(eps6[:, :], 1e-6).then_inc(eps_ready, 1)
            V.sem_inc(normed_ready, 1)
            V.sem_inc(turned, 1)
            V.sem_inc(xt_turned, 2)
            V.sem_inc(xT_ready, 2)
            V.sem_inc(hid_ready, 4)
            V.sem_inc(down_summed, U)
            V.sem_inc(y_ready, 2)
            V.sem_inc(y_free, 2)
            V.sem_inc(h_ready, 2)
            dve.wait_ge(small, NS)
            V.sem_inc(logits, 1)
            ln.dve(nc, dve, lambda i: h[:, :, ds(i * PAIR, PAIR)])
            with dve.Fori(0, NPAIR) as i:
                V.tensor_tensor(pairs(i), pairs(i), ln.scale(i), ALU.mult).then_inc(x_ready, 1)
            dve.wait_ge(x_ready, NPAIR)
            rms.dve(nc, dve)
            with dve.Fori(0, NPAIR) as i:
                cols = ds(i * PAIR, PAIR)
                V.tensor_tensor(h[:, :, cols], h[:, :, cols], pairs(i), ALU.add).then_inc(summed, 1)
                dve.wait_ge(turned, i + 1)
                V.tensor_tensor(nb[:, :, :], pairs(i), rms.scale(i), ALU.mult).then_inc(nb_ready, 1)
                dve.wait_ge(nb_ready, i + 1)
                for m in range(KD):
                    op = V.tensor_scalar(nb[:, m, :], nb[:, m, :], lnw[:, m:m + 1], None, ALU.mult)
                op.then_inc(weighted, 1)
            dve.wait_ge(logits, NPAIR + 1)
            dve.wait_ge(summed, NPAIR)
            steps = [0]

            def link(op):
                steps[0] += 1
                op.then_inc(step, 1)
                dve.wait_ge(step, steps[0])

            sh = [TW, NT, E]
            link(V.reduce_max(m1[:, :], lg[:, :, :], AX.X))
            V.tensor_tensor(lg[:, :, :], lg[:, :, :], bcast(m1[:, :], 2, sh), ALU.subtract).then_inc(shifted, 1)
            dve.wait_ge(exped, 1)
            link(V.reduce_sum(m1[:, :], lg[:, :, :], AX.X))
            link(V.reciprocal(m1[:, :], m1[:, :]))
            link(V.tensor_tensor(lg[:, :, :], lg[:, :, :], bcast(m1[:, :], 2, sh), ALU.mult))
            link(V.reduce_max(m1[:, :], lg[:, :, :], AX.X))
            link(V.tensor_tensor(oh[:, :, :], lg[:, :, :], bcast(m1[:, :], 2, sh), ALU.is_equal))
            link(V.tensor_tensor(oh[:, :, :], oh[:, :, :], bcast(rank[:, :], 1, sh), ALU.mult))
            link(V.reduce_max(m2[:, :], oh[:, :, :], AX.X))
            V.tensor_tensor(oh[:, :, :], oh[:, :, :], bcast(m2[:, :], 2, sh), ALU.is_equal).then_inc(oh_ready, 1)
            dve.wait_ge(counted, 1)
            ohp = oh[:, :, :].rearrange("p (i t) e -> p t i e", t=3)
            kp = kept[:, :, :].rearrange("p (i t) e -> p t i e", t=3)
            for t in range(3):
                op = V.scalar_tensor_tensor(out=kp[:, t, :, :],
                                            in0=PS[0:TW, 5 + t, 0:NPAIR * E].rearrange("p (i e) -> p i e", e=E),
                                            scalar=float(CAP), in1=ohp[:, t, :, :], op0=ALU.is_le, op1=ALU.mult)
            op.then_inc(kept_ready, 1)
            dve.wait_ge(ranked, 1)
            fl = lambda ap: ap.rearrange("p e t -> p (e t)")
            link(V.tensor_copy(totals[:, :, :], PS[0:TW, 1, 0:NT * E].rearrange("p (t e) -> p e t", e=E)))
            link(V.tensor_tensor_scan(out=fl(sofar[:, :, :]), data0=fl(carry[:, :, :]), data1=fl(totals[:, :, :]),
                                      initial=0.0, op0=ALU.mult, op1=ALU.add))
            link(V.tensor_tensor(full[:, :, :], bcast(sofar[:, :, NT - 1], 2, [TW, E, ET]),
                                 bcast(filled[:, :], 1, [TW, E, ET]), ALU.is_gt))
            link(V.reduce_sum(ntiles[:, :], full[:, :, :], AX.X))
            link(V.tensor_tensor_scan(out=tiles_to[:, :], data0=carry[:, 0, 1:1 + E], data1=ntiles[:, :],
                                      initial=0.0, op0=ALU.mult, op1=ALU.add))
            link(V.tensor_tensor(base[:, :], tiles_to[:, :], ntiles[:, :], ALU.subtract))
            link(V.tensor_scalar(base[:, :], base[:, :], float(TR), -1.0, ALU.mult, ALU.add))
            link(V.tensor_tensor(sofar[:, :, :], sofar[:, :, :], totals[:, :, :], ALU.subtract))
            link(V.tensor_tensor(sofar[:, :, :], sofar[:, :, :], bcast(base[:, :], 2, [TW, E, NT]), ALU.add))
            link(V.tensor_tensor(row[:, :, :], sofar[:, :, :].rearrange("p e t -> p t e"),
                                 PS[0:TW, 0, 0:NT * E].rearrange("p (t e) -> p t e", e=E), ALU.add))
            link(V.tensor_tensor(row[:, :, :], row[:, :, :], kept[:, :, :], ALU.mult))
            link(V.reduce_sum(dest[:, :], row[:, :, :], AX.X))
            link(V.reduce_sum(m2[:, :], kept[:, :, :], AX.X))
            link(V.tensor_scalar(m2[:, :], m2[:, :], -1.0, 1.0, ALU.mult, ALU.add))
            link(V.tensor_tensor(m2[:, :], m2[:, :], token[:, :], ALU.mult))
            link(V.tensor_tensor(dest[:, :], dest[:, :], m2[:, :], ALU.add))
            link(V.tensor_copy(dest_i[:, :], dest[:, :]))
            link(V.tensor_tensor(passed[:, :, :], bcast(tiles_to[0:1, :], 1, [1, TILES, E]),
                                 bcast(tile_no[:, :], 2, [1, TILES, E]), ALU.is_le))
            link(V.reduce_sum(whose[:, :], passed[:, :, :], AX.X))
            link(V.tensor_scalar(whose[:, :], whose[:, :], float(E - 1), None, ALU.min))
            V.tensor_copy(whose_i[:, :], whose[:, :]).then_inc(sorted_, 1)
            with dve.Fori(0, TILES // U) as mm:
                for b in range(U):
                    m, a = mm * U + b, b % 2
                    dve.wait_ge(down_summed, m + (U + 1))
                    dve.wait_ge(y_free, m + 1)
                    V.tensor_copy(yt[:, a, :], PS[:, 4 * a + 3, 0:D]).then_inc(y_ready, 1)
            with dve.Fori(0, NT // 4) as tt:
                for o in range(4):
                    dve.wait_ge(gathered[o], tt * 16 + 16)
                    V.tensor_scalar(back[:, o, :], back[:, o, :], m1[:, ds(tt * 4 + o, 1)], None, ALU.mult)\
                        .then_inc(scaled, 1)
                    dve.wait_ge(back_turned, tt * 4 + (o + 1))
                    cols = ds(tt * 4 * TW + o * TW, TW)
                    V.tensor_tensor(h[:, :, cols], h[:, :, cols],
                                    PS[0:P, o % 2, 0:KD * TW].rearrange("p (k t) -> p k t", t=TW), ALU.add)\
                        .then_inc(h_ready, 1)
            dve.wait_ge(h_ready, NT + 2)


class Consts:
    pass


def store(nc, h, out):
    with nc.semaphore("out_stored") as stored, nc.Block() as block:

        @block.sync
        def _(sp):
            for k in range(KD):
                sp.dma_start(out[:, k, :], h[:, k, :]).then_inc(stored, 16)
            sp.wait_ge(stored, 16 * KD)


STAGES = 5


def build(nc, dr, out):
    with ExitStack() as ctx:
        s = Scope(nc, ctx, "all")
        h = s.sb("h", [P, KD, N])
        PS = ctx.enter_context(nc.psum_tensor("PS", [128, 8, 512], F32))
        C = Consts()
        C.ones = s.sb("ones", [P, P])
        C.ident = s.sb("identity", [128, 128])
        C.eps5 = s.sb("eps5", [P, 1])
        with nc.Block() as block:

            @block.vector
            def _(dve):
                nc.vector.memset(C.eps5[:, :], 1e-5)

        tokenizer(nc, dr, PS, C, h)
        if STAGES >= 2:
            mamba(nc, dr, PS, C, h)
        if STAGES >= 3:
            experts(nc, dr, PS, C, h)
        if STAGES >= 4:
            attention(nc, dr, PS, C, h)
        if STAGES >= 5:
            switch(nc, dr, PS, C, h)
        store(nc, h, out)



def layouts(i):
    a = {k: np.asarray(v) for k, v in i.items()}

    def rows(w, p):
        return w.reshape(w.shape[0] // p, p, *w.shape[1:]).transpose(1, 0, *range(2, w.ndim + 1))

    def headpad(w):
        z = np.zeros((*w.shape[:-1], NH, HP), w.dtype)
        z[..., :DH] = w.reshape(*w.shape[:-1], NH, DH)
        return z.reshape(*w.shape[:-1], NH * HP)

    o = {}
    o["pix"] = rows(a["x"].reshape(B, 3, 8, 16, 8, 16).transpose(1, 3, 5, 0, 2, 4).reshape(768, B * NIMG), 128)
    o["txt"] = rows(a["txt"].transpose(2, 0, 1), P)
    o["wp"] = rows(a["L0_tok_patch_w"].reshape(D, 768).T, 128)
    o["tok_vec"] = np.stack([rows(a["L0_tok_" + n], P) for n in ("patch_b", "ln_g", "ln_b", "ff2_b", "proj_b")], 1)
    o["ff1"] = rows(a["L0_tok_ff1_w"], P)
    o["ff1_b"] = rows(a["L0_tok_ff1_b"], 128)
    o["ff2"] = rows(a["L0_tok_ff2_w"], 128)
    qkv, qkvb = a["L0_tok_qkv_w"].reshape(D, 3, D), a["L0_tok_qkv_b"].reshape(3, D)
    o["tok_wqk"] = rows(headpad(qkv[:, 0:2]), P)
    o["tok_bqk"] = headpad(qkvb[0:2]).reshape(2, QC, 128).transpose(2, 0, 1)
    o["tok_wv"] = rows(headpad(qkv[:, 2]), P)
    o["tok_bv"] = headpad(qkvb[2])
    o["tok_wo"] = rows(headpad(a["L0_tok_proj_w"].T).T, 128)
    inw = a["L0_attn_in_proj_w"].transpose(0, 2, 1)
    lrows = lambda w, p: np.stack([rows(x, p) for x in w])
    o["ssm_winx"], o["ssm_winz"] = lrows(inw[:, :, :384], P), lrows(inw[:, :, 384:], P)
    o["ssm_nvec"] = np.stack([lrows(a["L0_attn_norm_w"], P), lrows(a["L0_attn_norm_b"], P)], 2)
    o["ssm_fvec"] = np.stack([rows(a["L0_attn_norm_f_w"], P), rows(a["L0_attn_norm_f_b"], P)], 1)
    o["ssm_cvec"] = lrows(np.concatenate([a["L0_attn_conv_w"], *(a["L0_attn_" + n][..., None] for n in
                                                                 ("conv_b", "dt_proj_b", "D_skip"))], -1), 128)
    o["ssm_alog"] = lrows(a["L0_attn_A_log"], 128)
    xw = a["L0_attn_x_proj_w"].transpose(0, 2, 1)
    o["ssm_wx"] = lrows(np.concatenate([xw[:, :, 12:]] * 3 + [xw[:, :, :12]], -1), 128)
    o["ssm_wdt2"] = a["L0_attn_dt_proj_w"].transpose(0, 2, 1)
    o["ssm_wout"] = lrows(a["L0_attn_out_proj_w"].transpose(0, 2, 1), 128)
    pick = np.zeros((3, 32, 32, 128), mybir.dt.np(BF16))
    for n in range(32):
        pick[:, n, n] = 1
    o["ssm_sel"] = pick.reshape(P, 32 * 128)
    m = {k[7:]: v for k, v in a.items() if k.startswith("L0_ffn_")}
    o["moe_wr"] = rows(np.concatenate([m["router_w"], m["sg_w"]], 1), P)
    o["moe_wg"], o["moe_wu"] = (rows(m[k].transpose(1, 0, 2).reshape(D, 8 * 192), P) for k in ("w_gate", "w_up"))
    o["moe_wd"] = rows(m["w_down"].reshape(8 * 192, D), P)
    o["moe_wsg"], o["moe_wsu"], o["moe_wsd"] = rows(m["ws_gate"], P), rows(m["ws_up"], P), rows(m["ws_down"], 128)
    o["moe_sgb"] = m["sg_b"]
    o["moe_rank"] = np.tile(np.arange(8, 0, -1, dtype=np.float32), (94, 1))
    o["moe_pick"] = np.repeat(np.eye(9, dtype=np.float32), 128, 1)
    qkv = a["L1_attn_qkv_w"].T.reshape(D, 3, D)
    o["att_wqk"], o["att_wk"], o["att_wv"] = rows(headpad(qkv[:, 0:2]), P), rows(qkv[:, 1], P), \
        rows(headpad(qkv[:, 2]), P)
    o["att_wo"] = rows(a["L1_attn_proj_w"].T, P)
    o["att_bo"] = rows(a["L1_attn_proj_b"], P)
    pick = np.zeros((8, DH, 2, HP), np.float32)
    for g in range(2):
        for r in range(8):
            pick[r, :, g, g * 8 + r] = 1 / (2 * (0.5 * DH ** -0.5) * T)
    o["att_sel"] = pick.reshape(128, 2, HP)
    pick = np.zeros((2, 2, 8, 2, 2, 8, DH), np.float32)
    for g in range(2):
        for sign in range(2):
            for r in range(8):
                pick[sign, g, r, g, sign, r] = 1
    o["att_spread"] = pick.reshape(2 * DH, 4, 128)
    o["sw_lnw"], o["sw_wr"] = rows(a["L1_ffn_ln_w"], P), rows(a["L1_ffn_w_router"], P)
    o["sw_wi"], o["sw_wo"] = lrows(a["L1_ffn_wi"], P), lrows(a["L1_ffn_wo"], 128)
    o["sw_rank"] = np.tile(np.arange(16, 0, -1, dtype=np.float32), (94, 1))
    o["sw_every"] = np.ones((94, 94), np.float32)
    o["sw_carry"] = np.tile((np.arange(24) > 0).astype(np.float32), (94, 16, 1))
    o["sw_filled"] = np.tile(128 * np.arange(8, dtype=np.float32), (94, 1))
    o["sw_tile_no"] = np.arange(36, dtype=np.float32)[None]
    o["sw_token"] = (37 * 128 + np.arange(N, dtype=np.float32)).reshape(24, 94).T
    at = np.arange(PAIR)
    before = ((at[:, None] <= at[None]) & (at[:, None] // T == at[None] // T)).astype(np.float32)
    o["sw_upto"] = np.stack([before[x * 94:(x + 1) * 94, y * 94:(y + 1) * 94] for x, y in
                             ((0, 0), (0, 1), (1, 1), (1, 2), (2, 2))], 1)
    at, fr = np.arange(NIMG, dtype=np.float32)[:, None], np.arange(D // 2, dtype=np.float32)[None, :]
    ang = at / np.power(np.float32(10000.0), np.float32(2.0) * fr / np.float32(D))
    pe = np.zeros((NIMG, D), np.float32)
    pe[:, 0::2], pe[:, 1::2] = np.sin(ang), np.cos(ang)
    o["pos"] = rows(pe.T, P)
    o["ones"] = np.full((P, P), 1.0 / D, np.float32)
    o["ident"] = np.eye(128, dtype=np.float32)
    return {k: np.ascontiguousarray(v) for k, v in o.items()}


def kernel(**inputs):
    import concourse.bacc as _bacc
    from concourse.bass_utils import run_bass_kernel_spmd as _run

    nc = _bacc.Bacc("TRN2", target_bir_lowering=False, num_devices=1)
    arrays = layouts(inputs)
    dr = {k: nc.dram_tensor("in_" + k, v.shape, mybir.dt.from_np(v.dtype), kind="ExternalInput").ap() for k, v in arrays.items()}
    out = nc.dram_tensor("out", (P, KD, N), F32, kind="ExternalOutput").ap()
    build(nc, dr, out)
    r = _run(nc, [{"in_" + k: v for k, v in arrays.items()}], core_ids=[0]).results[0]["out"]
    return np.ascontiguousarray(r.transpose(1, 0, 2).reshape(D, B, T).transpose(1, 2, 0))
```
